# Optimizing a Trainium2 kernel written in Bass

```python
import numpy as np
import jax
import jax.numpy as jnp

def _softmax(x, axis=-1):
    return jax.nn.softmax(x, axis=axis)

def _gelu(x):
    return jax.nn.gelu(x, approximate=True)

def _silu(x):
    return jax.nn.silu(x)

def _sigmoid(x):
    return jax.nn.sigmoid(x)

def _layernorm(x, axis=-1, eps=1e-05):
    m = jnp.mean(x, axis=axis, keepdims=True)
    v = jnp.var(x, axis=axis, keepdims=True)
    return (x - m) / jnp.sqrt(v + eps)

def _scatter_add(tgt, idx, src, axis=0):
    return tgt.at[idx].add(src)

def _segment_sum(src, seg, n):
    return jax.ops.segment_sum(src, seg, n)
kernel_name = 'mk_decoder_preln_d1_seqx_r4_a5c9f9'

def setup_inputs(seed: int=0):
    np.random.seed(seed)
    _w = jnp.asarray

    def _rec_inputs():
        import jax
        import jax.numpy as jnp
        _rk = jax.random.key(seed)
        x = 0.0002279 + 0.9999 * jax.random.normal(jax.random.fold_in(_rk, 1), (16, 256, 256), jnp.float32)
        _lenS = 256 - jax.random.randint(jax.random.fold_in(_rk, 7), (16,), 0, max(1, 256 // 4) + 1, jnp.int32)
        _lenS2 = 256 - jax.random.randint(jax.random.fold_in(_rk, 8), (16,), 0, max(1, 256 // 4) + 1, jnp.int32)
        _ctx_1024P = jax.random.normal(jax.random.fold_in(_rk, 11), (16, 16, 256), jnp.float32)
        _ctx_1024c = jax.random.dirichlet(jax.random.fold_in(_rk, 511), 0.3 * jnp.ones((16,), jnp.float32), (16, 256))
        _ctx_1024t = jnp.einsum('bsk,bkd->bsd', _ctx_1024c, _ctx_1024P)
        _ctx_1024t = _ctx_1024t * jax.lax.rsqrt(jnp.mean(jnp.square(_ctx_1024t)) + 1e-12) * 0.953939
        ctx_1024 = -7.10856e-05 + 0.999911 * (_ctx_1024t + 0.3 * jax.random.normal(jax.random.fold_in(_rk, 611), (16, 256, 256), jnp.float32))
        return (x, ctx_1024)
    x, ctx_1024 = _rec_inputs()

    def _L0_attn_setup():
        import jax, jax.numpy as jnp
        import numpy as np
        import math
        B, T, D = (2, 512, 256)
        N_HEADS = 16
        D_HEAD = D // N_HEADS

        def _rope_tables(t, d_head, dtype=jnp.float32):
            theta = 1.0 / 10000.0 ** (jnp.arange(0, d_head, 2, dtype=jnp.float32) / d_head)
            angles = jnp.outer(jnp.arange(t, dtype=jnp.float32), theta)
            angles = jnp.concatenate([angles, angles], axis=-1)
            return (jnp.cos(angles).astype(dtype), jnp.sin(angles).astype(dtype))

        def _rotate_half(x):
            half = x.shape[-1] // 2
            return jnp.concatenate([-x[..., half:], x[..., :half]], axis=-1)

        def _apply_rope(x, cos, sin):
            return x * cos[None, None] + _rotate_half(x) * sin[None, None]
        key = jax.random.key(seed)
        k1, k2, k3, k4 = jax.random.split(key, 4)
        s_in = 1.0 / math.sqrt(D)
        return {'x': jax.random.normal(k1, (B, T, D), dtype=jnp.float32), 'w_qkv': jax.random.normal(k2, (D, 3 * D), dtype=jnp.float32) * s_in, 'w_out': jax.random.normal(k3, (D, D), dtype=jnp.float32) * s_in, 'b_out': jax.random.normal(k4, (D,), dtype=jnp.float32) * 0.01}
    _L0_attn_all = _L0_attn_setup()
    _L0_attn_in = {k: v for k, v in _L0_attn_all.items() if k in ('w_qkv', 'w_out', 'b_out')}
    del _L0_attn_all

    def _L0_xattn_setup():
        import jax, jax.numpy as jnp
        import numpy as np
        EPS = 1e-05

        def layer_norm(x, w, b):
            mu = jnp.mean(x, axis=-1, keepdims=True)
            var = jnp.mean((x - mu) ** 2, axis=-1, keepdims=True)
            return (x - mu) * jax.lax.rsqrt(var + EPS) * w + b
        key = jax.random.key(seed)
        ks = jax.random.split(key, 8)
        b, Nx, Nz, D = (16, 1024, 64, 256)
        H, Dh = (8, 64)
        inner = H * Dh
        s = 1.0 / np.sqrt(D)
        return {'x': jax.random.normal(ks[0], (b, Nx, D), jnp.float32), 'latents': jax.random.normal(ks[1], (b, Nz, D), jnp.float32), 'ln_media_w': jnp.ones((D,), jnp.float32), 'ln_media_b': jnp.zeros((D,), jnp.float32), 'ln_lat_w': jnp.ones((D,), jnp.float32), 'ln_lat_b': jnp.zeros((D,), jnp.float32), 'Wq': jax.random.normal(ks[2], (D, inner), jnp.float32) * s, 'Wk': jax.random.normal(ks[3], (D, inner), jnp.float32) * s, 'Wv': jax.random.normal(ks[4], (D, inner), jnp.float32) * s, 'Wout': jax.random.normal(ks[5], (inner, D), jnp.float32) * (1.0 / np.sqrt(inner))}
    _L0_xattn_all = _L0_xattn_setup()
    _L0_xattn_in = {k: v for k, v in _L0_xattn_all.items() if k in ('ln_media_w', 'ln_media_b', 'ln_lat_w', 'ln_lat_b', 'Wq', 'Wk', 'Wv', 'Wout')}
    del _L0_xattn_all

    def _L0_ffn_setup():
        import jax, jax.numpy as jnp
        import numpy as np
        BS, L, D = (4, 512, 256)
        H, E, K = (8, 16, 2)
        HD = D // H
        I = 1024 // H
        key = jax.random.key(seed)
        ks = jax.random.split(key, 10)
        s = lambda k, shp, fan: jax.random.normal(k, shp, jnp.float32) / np.sqrt(fan)
        return {'x': jax.random.normal(ks[0], (BS, L, D), jnp.float32), 'Wm': s(ks[1], (D, D), D), 'bm': jnp.zeros((D,), jnp.float32), 'expert_emb': jax.random.normal(ks[2], (HD, E), jnp.float32), 'W1': s(ks[3], (E, HD, I), HD), 'b1': jnp.zeros((E, I), jnp.float32), 'W2': s(ks[4], (E, I, HD), I), 'b2': jnp.zeros((E, HD), jnp.float32), 'Wo': s(ks[5], (D, D), D), 'bo': jnp.zeros((D,), jnp.float32)}
    _L0_ffn_all = _L0_ffn_setup()
    _L0_ffn_in = {k: v for k, v in _L0_ffn_all.items() if k in ('Wm', 'bm', 'expert_emb', 'W1', 'b1', 'W2', 'b2', 'Wo', 'bo')}
    del _L0_ffn_all
    return {'x': x, 'ctx_1024': ctx_1024, 'L0_attn_w_qkv': _L0_attn_in['w_qkv'], 'L0_attn_w_out': _L0_attn_in['w_out'], 'L0_attn_b_out': _L0_attn_in['b_out'], 'L0_xattn_ln_media_w': _L0_xattn_in['ln_media_w'], 'L0_xattn_ln_media_b': _L0_xattn_in['ln_media_b'], 'L0_xattn_ln_lat_w': _L0_xattn_in['ln_lat_w'], 'L0_xattn_ln_lat_b': _L0_xattn_in['ln_lat_b'], 'L0_xattn_Wq': _L0_xattn_in['Wq'], 'L0_xattn_Wk': _L0_xattn_in['Wk'], 'L0_xattn_Wv': _L0_xattn_in['Wv'], 'L0_xattn_Wout': _L0_xattn_in['Wout'], 'L0_ffn_Wm': _L0_ffn_in['Wm'], 'L0_ffn_bm': _L0_ffn_in['bm'], 'L0_ffn_expert_emb': _L0_ffn_in['expert_emb'], 'L0_ffn_W1': _L0_ffn_in['W1'], 'L0_ffn_b1': _L0_ffn_in['b1'], 'L0_ffn_W2': _L0_ffn_in['W2'], 'L0_ffn_b2': _L0_ffn_in['b2'], 'L0_ffn_Wo': _L0_ffn_in['Wo'], 'L0_ffn_bo': _L0_ffn_in['bo']}

def reference(x, ctx_1024, L0_attn_w_qkv, L0_attn_w_out, L0_attn_b_out, L0_xattn_ln_media_w, L0_xattn_ln_media_b, L0_xattn_ln_lat_w, L0_xattn_ln_lat_b, L0_xattn_Wq, L0_xattn_Wk, L0_xattn_Wv, L0_xattn_Wout, L0_ffn_Wm, L0_ffn_bm, L0_ffn_expert_emb, L0_ffn_W1, L0_ffn_b1, L0_ffn_W2, L0_ffn_b2, L0_ffn_Wo, L0_ffn_bo):
    import jax
    import jax.numpy as jnp

    def _L0_attn_ref(x, w_qkv, w_out, b_out):
        import jax, jax.numpy as jnp
        import numpy as np
        import math
        B, T, D = (2, 512, 256)
        N_HEADS = 16
        D_HEAD = D // N_HEADS

        def _rope_tables(t, d_head, dtype=jnp.float32):
            theta = 1.0 / 10000.0 ** (jnp.arange(0, d_head, 2, dtype=jnp.float32) / d_head)
            angles = jnp.outer(jnp.arange(t, dtype=jnp.float32), theta)
            angles = jnp.concatenate([angles, angles], axis=-1)
            return (jnp.cos(angles).astype(dtype), jnp.sin(angles).astype(dtype))

        def _rotate_half(x):
            half = x.shape[-1] // 2
            return jnp.concatenate([-x[..., half:], x[..., :half]], axis=-1)

        def _apply_rope(x, cos, sin):
            return x * cos[None, None] + _rotate_half(x) * sin[None, None]
        b, t, d = x.shape
        qkv = x @ w_qkv
        qkv = qkv.reshape(b, t, 3, N_HEADS, D_HEAD)
        q = jnp.transpose(qkv[:, :, 0], (0, 2, 1, 3))
        k = jnp.transpose(qkv[:, :, 1], (0, 2, 1, 3))
        v = jnp.transpose(qkv[:, :, 2], (0, 2, 1, 3))
        cos, sin = _rope_tables(t, D_HEAD, x.dtype)
        q = _apply_rope(q, cos, sin)
        k = _apply_rope(k, cos, sin)
        scores = jnp.einsum('bhqd,bhkd->bhqk', q, k) / math.sqrt(D_HEAD)
        probs = jax.nn.softmax(scores, axis=-1)
        out = jnp.einsum('bhqk,bhkd->bhqd', probs, v)
        out = jnp.transpose(out, (0, 2, 1, 3)).reshape(b, t, d)
        return out @ w_out + b_out

    def _L0_xattn_ref(x, latents, ln_media_w, ln_media_b, ln_lat_w, ln_lat_b, Wq, Wk, Wv, Wout):
        import jax, jax.numpy as jnp
        import numpy as np
        EPS = 1e-05

        def layer_norm(x, w, b):
            mu = jnp.mean(x, axis=-1, keepdims=True)
            var = jnp.mean((x - mu) ** 2, axis=-1, keepdims=True)
            return (x - mu) * jax.lax.rsqrt(var + EPS) * w + b
        H, Dh = (8, 64)
        scale = Dh ** (-0.5)
        b, Nz, D = latents.shape
        xn = layer_norm(x, ln_media_w, ln_media_b)
        zn = layer_norm(latents, ln_lat_w, ln_lat_b)
        q = (zn @ Wq).reshape(b, Nz, H, Dh).transpose(0, 2, 1, 3)
        kv_in = jnp.concatenate([xn, zn], axis=1)
        F = kv_in.shape[1]
        k = (kv_in @ Wk).reshape(b, F, H, Dh).transpose(0, 2, 1, 3)
        v = (kv_in @ Wv).reshape(b, F, H, Dh).transpose(0, 2, 1, 3)
        sim = jnp.einsum('bhqd,bhfd->bhqf', q * scale, k)
        alphas = jax.nn.softmax(sim, axis=-1)
        out = jnp.einsum('bhqf,bhfd->bhqd', alphas, v)
        out = out.transpose(0, 2, 1, 3).reshape(b, Nz, H * Dh)
        return out @ Wout

    def _L0_ffn_ref(x, Wm, bm, expert_emb, W1, b1, W2, b2, Wo, bo):
        import jax, jax.numpy as jnp
        import numpy as np
        BS, L, D = (4, 512, 256)
        H, E, K = (8, 16, 2)
        HD = D // H
        I = 1024 // H
        bs, L_, d = x.shape
        h = x @ Wm + bm
        t = h.reshape(bs * L_ * H, HD)
        logits = t @ expert_emb
        w = jax.nn.softmax(logits, axis=-1)
        topw, topi = jax.lax.top_k(w, K)
        hmid = jax.nn.gelu(jnp.einsum('td,edi->tei', t, W1) + b1, approximate=False)
        eo = jnp.einsum('tei,eio->teo', hmid, W2) + b2
        sel = jnp.take_along_axis(eo, topi[:, :, None], axis=1)
        comb = (sel * topw[:, :, None]).sum(axis=1)
        out = comb.reshape(bs, L_, d)
        return out @ Wo + bo
    x = x + _L0_attn_ref(_layernorm(x, axis=-1), L0_attn_w_qkv, L0_attn_w_out, L0_attn_b_out)
    x = x + _L0_xattn_ref(ctx_1024, _layernorm(x, axis=-1), L0_xattn_ln_media_w, L0_xattn_ln_media_b, L0_xattn_ln_lat_w, L0_xattn_ln_lat_b, L0_xattn_Wq, L0_xattn_Wk, L0_xattn_Wv, L0_xattn_Wout)
    x = x + _L0_ffn_ref(_layernorm(x, axis=-1), L0_ffn_Wm, L0_ffn_bm, L0_ffn_expert_emb, L0_ffn_W1, L0_ffn_b1, L0_ffn_W2, L0_ffn_b2, L0_ffn_Wo, L0_ffn_bo)
    return x

_drawn_inputs = setup_inputs


def setup_inputs(seed=0):
    import zlib

    import numpy as np

    out = dict(_drawn_inputs(seed))
    spreads = {'L0_xattn_ln_media_w': (1.0, 0.2),
     'L0_xattn_ln_media_b': (0.0, 0.1),
     'L0_xattn_ln_lat_w': (1.0, 0.2),
     'L0_xattn_ln_lat_b': (0.0, 0.1),
     'L0_ffn_bm': (0.0, 0.1),
     'L0_ffn_b1': (0.0, 0.1),
     'L0_ffn_b2': (0.0, 0.1),
     'L0_ffn_bo': (0.0, 0.1)}
    factors = {'L0_attn_b_out': 3.251}
    for name, (base, spread) in spreads.items():
        noise = np.random.default_rng([zlib.crc32(name.encode()), seed]).standard_normal(out[name].shape)
        drawn = base * np.exp(spread * noise) if base else spread * noise
        out[name] = jnp.asarray(drawn.astype(out[name].dtype))
    for name, factor in factors.items():
        out[name] = (out[name] * factor).astype(out[name].dtype)
    return out
```

```python
from contextlib import ExitStack

import numpy as np

import concourse.bass as bass
from concourse import mybir

F32 = mybir.dt.float32
F16 = mybir.dt.float16
ALU = mybir.AluOpType
ACT = mybir.ActivationFunctionType
AX = mybir.AxisListType.X

P = 128
B, S, D = 16, 256, 256
TILES = B * S // P
QT = S // P
EPS = 1e-5
H1, DH1 = 16, 16
H2, DH2 = 8, 64
INNER = H2 * DH2
KV = 2 * S
HF, HD, E, I = 8, 32, 16, 128
CH = 512
CHUNKS = B * S // CH
CT_ = CH // P


class Count:

    def __init__(self, sem, credit):
        self.sem, self.credit = sem, credit

    def at(self, n):
        return n + self.credit


class Env:

    def __init__(self, nc, name):
        self.nc, self.name, self.ctx = nc, name, ExitStack()

    def __enter__(self):
        self.ctx.__enter__()
        return self

    def __exit__(self, *a):
        return self.ctx.__exit__(*a)

    def sb(self, name, shape, dt=F32):
        return self.ctx.enter_context(self.nc.sbuf_tensor(f"{self.name}_{name}", shape, dt))

    def psum(self, name, banks=1):
        shape = [P, 512] if banks == 1 else [P, banks, 512]
        return self.ctx.enter_context(self.nc.psum_tensor(f"{self.name}_ps_{name}", shape, F32))

    def sem(self, name, credit=0):
        return Count(self.ctx.enter_context(self.nc.semaphore(f"{self.name}_{name}")), credit)

    def block(self):
        return self.ctx.enter_context(self.nc.Block())


def ln_statistics(nc, dve, env, x, n, mean_var, done, at=0):
    raw = env.sb(f"ln_raw{at}", [P, n, 6])
    for t in range(n):
        nc.vector.bn_stats(raw[:, t, :], x(t)).then_inc(done.sem, 1)
    for t in range(n):
        dve.wait_ge(done.sem, done.at(at + t + 1))
        nc.vector.bn_aggr(mean_var[:, t, :], raw[:, t, :]).then_inc(done.sem, 1)


def refine_rsqrt(nc, dve, rstd, var, tmp, step, at):
    nc.vector.reciprocal(rstd, rstd).then_inc(step.sem, 1)
    dve.wait_ge(step.sem, at + 1)
    nc.vector.tensor_tensor(tmp, rstd, rstd, ALU.mult).then_inc(step.sem, 1)
    dve.wait_ge(step.sem, at + 2)
    nc.vector.tensor_tensor(tmp, tmp, var, ALU.mult).then_inc(step.sem, 1)
    dve.wait_ge(step.sem, at + 3)
    nc.vector.tensor_scalar(tmp, tmp, -0.5, 1.5, ALU.mult, ALU.add).then_inc(step.sem, 1)
    dve.wait_ge(step.sem, at + 4)
    nc.vector.tensor_tensor(rstd, rstd, tmp, ALU.mult).then_inc(step.sem, 1)
    dve.wait_ge(step.sem, at + 5)
    return at + 5


def self_attention(nc, X, C, ident, x_raw, c_raw, x_in, context, ident_in, w_qkv, w_out, b_out, rope, head_mask):
    with Env(nc, "p1") as env:
        wqkv = env.sb("wqkv", [P, 2, 3 * D])
        wrot = env.sb("wrot", [P, 2, 2 * D])
        wout = env.sb("wout", [P, 4, D])
        bout = env.sb("bout", [P, QT, D])
        cs = env.sb("cs", [P, 2, 2 * S])
        mask = env.sb("mask", [P, 8])
        mv = env.sb("mv", [P, TILES, 2])
        var = env.sb("var", [P, TILES])
        rstd = env.sb("rstd", [P, TILES])
        ntmp = env.sb("ntmp", [P, TILES])
        xn = env.sb("xn", [P, QT, D])
        xnT = env.sb("xnT", [P, 2, S])
        rt = env.sb("rt", [P, 2, 2 * S])
        qT = env.sb("qT", [P, 2, S])
        kT = env.sb("kT", [P, S])
        km = env.sb("km", [P, 2, 8, S])
        v = env.sb("v", [P, QT, H1, 32])
        prob = env.sb("prob", [P, 2, QT, 2, S])
        nmax = env.sb("nmax", [P, 2, QT, 2])
        rsum = env.sb("rsum", [P, 2, QT, 2])
        rinv = env.sb("rinv", [P, 2, QT, 2])
        pT = env.sb("pT", [P, 8, 2, S])
        oT = env.sb("oT", [P, 4, S])
        res = env.sb("res", [P, QT, D])

        ps_s = [env.psum(f"s{i}") for i in range(2)]
        ps_t = [env.psum(f"t{i}") for i in range(2)]
        ps_o = env.psum("o")
        ps_p = [env.psum(f"p{i}") for i in range(2)]
        ps_m = env.psum("m")

        x_loaded, w_loaded, zeroed = env.sem("x_loaded"), env.sem("w_loaded"), env.sem("zeroed")
        stats, std_ready, step = env.sem("stats"), env.sem("std_ready"), env.sem("step")
        wrot_ready, c_loaded = env.sem("wrot_ready"), env.sem("c_loaded")
        xn_ready = env.sem("xn_ready")
        xnT_ps = env.sem("xnT_ps")
        xnT_ready = env.sem("xnT_ready")
        qk_ps = env.sem("qk_ps")
        qk_mul = env.sem("qk_mul", 2)
        rope_done = env.sem("rope_done", 2)
        km_ready = env.sem("km_ready")
        v_ps = env.sem("v_ps", 1)
        v_ready = env.sem("v_ready", 1)
        s_ps = env.sem("s_ps", 16)
        nmax_ready = env.sem("nmax_ready")
        exp_done = env.sem("exp_done", 4)
        inv_ready = env.sem("inv_ready")
        prob_ready = env.sem("prob_ready")
        pT_ps = env.sem("pT_ps", 4)
        pT_act = env.sem("pT_act", 1)
        pT_dve = env.sem("pT_dve", 1)
        o_ps = env.sem("o_ps", 2)
        oT_ready = env.sem("oT_ready", 1)
        out_ps = env.sem("out_ps", 1)
        res_ready = env.sem("res_ready")
        x_done = env.sem("x_done", 1)
        block = env.block()
        W_ALL = 16 * (6 + H1)

        @block.sync
        def _(sp):
            xv = x_in.rearrange("b (t p) d -> p (b t) d", p=P)
            for n in range(4):
                sp.dma_start(X[:, 8 * n:8 * n + 8, :], xv[:, 8 * n:8 * n + 8, :]).then_inc(x_loaded.sem, 16)
            sp.dma_start(wqkv[:], w_qkv.rearrange("(k p) n -> p k n", p=P)).then_inc(w_loaded.sem, 16)
            sp.dma_start(cs[:], rope).then_inc(w_loaded.sem, 16)
            sp.dma_start(mask[:], head_mask).then_inc(w_loaded.sem, 16)
            sp.dma_start(ident[:], ident_in).then_inc(w_loaded.sem, 16)
            for t in range(QT):
                sp.dma_start(bout[:, t, :], b_out.rearrange("(a n) -> a n", a=1).broadcast_to([P, D])
                             ).then_inc(w_loaded.sem, 16)
            cv = context.rearrange("b (t p) d -> p (b t) d", p=P)
            for n in range(4):
                sp.dma_start(C[:, 8 * n:8 * n + 8, :], cv[:, 8 * n:8 * n + 8, :]).then_inc(c_loaded.sem, 16)
            sp.wait_ge(zeroed.sem, 1)
            for h in range(H1):
                sp.dma_start(wout[32 * (h % 4):32 * (h % 4) + DH1, h // 4, :],
                             w_out[h * DH1:(h + 1) * DH1, :]).then_inc(w_loaded.sem, 16)

        @block.vector
        def _(dve):
            for c in (qk_mul, pT_dve, x_done):
                dve.sem_inc(c.sem, c.credit)
            nc.vector.memset(wout[:], 0.0).then_inc(zeroed.sem, 1)
            nc.vector.memset(v[:], 0.0).then_inc(zeroed.sem, 1)
            dve.wait_ge(x_loaded.sem, 64)
            ln_statistics(nc, dve, env, lambda t: X[:, t, :], TILES, mv, stats)
            dve.wait_ge(stats.sem, 2 * TILES)
            nc.vector.tensor_scalar(var[:], mv[:, :, 1], EPS, None, ALU.add).then_inc(stats.sem, 1)
            dve.wait_ge(std_ready.sem, 1)
            refine_rsqrt(nc, dve, rstd[:], var[:], ntmp[:], step, 0)
            dve.wait_ge(w_loaded.sem, W_ALL)
            for half in range(2):
                for k in range(2):
                    src = wqkv[:, k, 0:2 * D].rearrange("p (h j) -> p h j", j=DH1)
                    dst = wrot[:, k, :].rearrange("p (h j) -> p h j", j=DH1)
                    nc.vector.tensor_copy(dst[:, :, 8 * half:8 * half + 8],
                                          src[:, :, 8 - 8 * half:16 - 8 * half]).then_inc(wrot_ready.sem, 1)

            def later_stats(b):
                for t in range(QT):
                    nc.vector.bn_stats(x_raw[:, bass.ds(QT * b + t, 1), :].rearrange("p a s -> p (a s)"),
                                       X[:, bass.ds(QT * b + t, 1), :].rearrange("p a d -> p (a d)"))

            def context_stats(b):
                for t in range(QT):
                    nc.vector.bn_stats(c_raw[:, bass.ds(QT * b + t, 1), :].rearrange("p a s -> p (a s)"),
                                       C[:, bass.ds(QT * b + t, 1), :].rearrange("p a d -> p (a d)"))

            def normalise(b):
                for t in range(QT):
                    nc.vector.tensor_scalar(xn[:, t, :], X[:, bass.ds(QT * b + t, 1), :].rearrange("p a d -> p (a d)"),
                                            mv[:, bass.ds(QT * b + t, 1), 0:1].rearrange("p a d -> p (a d)"),
                                            rstd[:, bass.ds(QT * b + t, 1)],
                                            ALU.subtract, ALU.mult).then_inc(xn_ready.sem, 1)

            def rope_mul(b, n):
                dve.wait_ge(qk_ps.sem, qk_ps.at(4 * b + n + 1))
                dve.wait_ge(rope_done.sem, rope_done.at(4 * b + n - 1))
                nc.vector.tensor_tensor(rt[:, n % 2, :], ps_p[n % 2][:], cs[:, n % 2, :], ALU.mult
                                        ).then_inc(qk_mul.sem, 1)

            def maxima(b, u):
                for qt in range(QT):
                    dve.wait_ge(s_ps.sem, s_ps.at(16 * b + 2 * u + qt + 1))
                    nc.vector.tensor_reduce(nmax[:, u % 2, qt, :], ps_s[qt][:].rearrange("p (h k) -> p h k", h=2),
                                            AX, ALU.max, negate=True).then_inc(nmax_ready.sem, 1)

            def divide(b, u):
                for qt in range(QT):
                    dve.wait_ge(exp_done.sem, exp_done.at(32 * b + 4 * u + 2 * qt + 2))
                    nc.vector.reciprocal(rinv[:, u % 2, qt, :], rsum[:, u % 2, qt, :]).then_inc(inv_ready.sem, 1)
                for qt in range(QT):
                    dve.wait_ge(inv_ready.sem, inv_ready.at(16 * b + 2 * u + qt + 1))
                    for hh in range(2):
                        nc.vector.tensor_scalar(prob[:, u % 2, qt, hh, :], prob[:, u % 2, qt, hh, :],
                                                rinv[:, u % 2, qt, hh:hh + 1], None, ALU.mult
                                                ).then_inc(prob_ready.sem, 1)

            def evacuate_pT(b, u):
                h = 2 * u + 1
                dve.wait_ge(pT_ps.sem, pT_ps.at(16 * b + h + 1))
                dve.wait_ge(o_ps.sem, o_ps.at(4 * b + h // 4 - 1))
                nc.vector.tensor_copy(pT[:, h % 8, :, :], ps_t[1][:].rearrange("p (k q) -> p k q", k=2)
                                      ).then_inc(pT_dve.sem, 1)

            def finish(b):
                dve.wait_ge(out_ps.sem, out_ps.at(b + 1))
                nc.vector.tensor_tensor(res[:], ps_m[:].rearrange("p (t d) -> p t d", t=QT), bout[:], ALU.add
                                        ).then_inc(res_ready.sem, 1)
                dve.wait_ge(res_ready.sem, res_ready.at(b + 1))
                nc.vector.tensor_tensor(X[:, bass.ds(QT * b, QT), :], X[:, bass.ds(QT * b, QT), :], res[:],
                                        ALU.add).then_inc(x_done.sem, 1)

            def body(b, before, more):
                for u in range(10):
                    if 1 <= u <= 8:
                        divide(b, u - 1)
                    if u >= 2:
                        evacuate_pT(b, u - 2)
                    if u < 8:
                        maxima(b, u)
                    if before and u == 1:
                        finish(b - 1)
                    if more and u in (5, 6, 8, 9):
                        rope_mul(b + 1, (5, 6, 8, 9).index(u))
                if before:
                    dve.wait_ge(x_done.sem, x_done.at(b))
                    later_stats(b - 1)
                context_stats(b)

            normalise(0)
            for n in range(4):
                rope_mul(0, n)
            dve.wait_ge(c_loaded.sem, 64)
            normalise(1)
            body(0, False, True)
            normalise(2)
            with dve.Fori(1, B - 2) as b:
                body(b, True, True)
                normalise(b + 2)
            body(B - 2, True, True)
            body(B - 1, True, False)
            finish(B - 1)
            dve.wait_ge(x_done.sem, x_done.at(B))
            later_stats(B - 1)

        @block.gpsimd
        def _(pool):
            pool.sem_inc(rope_done.sem, rope_done.credit)

            def rope_add(b, n):
                half = n // 2
                pool.wait_ge(qk_mul.sem, qk_mul.at(4 * b + n + 1))
                pool.wait_ge(s_ps.sem, s_ps.at(16 * (b - 1) + 8 * half + 8))
                if n % 2:
                    pool.wait_ge(km_ready.sem, km_ready.at(2 * b + half))
                nc.gpsimd.tensor_tensor(kT[:] if n % 2 else qT[:, half, :], rt[:, n % 2, 0:S], rt[:, n % 2, S:2 * S],
                                        ALU.add).then_inc(rope_done.sem, 1)
                if n % 2:
                    pool.wait_ge(rope_done.sem, rope_done.at(4 * b + n + 1))
                    nc.gpsimd.tensor_tensor(km[:, half, :, :], kT[:].unsqueeze(1).broadcast_to([P, 8, S]),
                                            mask[:].unsqueeze(2).broadcast_to([P, 8, S]), ALU.mult
                                            ).then_inc(km_ready.sem, 1)

            for n in range(4):
                rope_add(0, n)
            with pool.Fori(1, B) as b:
                for n in range(4):
                    rope_add(b, n)

        @block.scalar
        def _(act):
            for c in (v_ready, exp_done, pT_act, oT_ready):
                act.sem_inc(c.sem, c.credit)
            act.wait_ge(stats.sem, 2 * TILES + 1)
            nc.scalar.activation(rstd[:], var[:], ACT.Sqrt).then_inc(std_ready.sem, 1)
            act.wait_ge(zeroed.sem, 2)

            def evacuate_xnT(b):
                act.wait_ge(xnT_ps.sem, xnT_ps.at(b + 1))
                act.wait_ge(v_ps.sem, v_ps.at(b))
                nc.scalar.activation(xnT[:], ps_m[:].rearrange("p (k s) -> p k s", k=2), ACT.Copy
                                     ).then_inc(xnT_ready.sem, 1)

            def evacuate_v(b):
                act.wait_ge(v_ps.sem, v_ps.at(b + 1))
                act.wait_ge(o_ps.sem, o_ps.at(4 * b))
                for t in range(QT):
                    ins = nc.scalar.activation(v[:, t, :, 0:DH1],
                                               ps_p[0][:, t * D:(t + 1) * D].rearrange("p (h j) -> p h j", h=H1), ACT.Copy)
                ins.then_inc(v_ready.sem, 1)

            def exponentials(b, u):
                for qt in range(QT):
                    act.wait_ge(nmax_ready.sem, nmax_ready.at(16 * b + 2 * u + qt + 1))
                    act.wait_ge(pT_ps.sem, pT_ps.at(16 * b + 2 * u - 2))
                    for hh in range(2):
                        nc.scalar.activation(prob[:, u % 2, qt, hh, :], ps_s[qt][:, hh * S:(hh + 1) * S], ACT.Exp,
                                             bias=nmax[:, u % 2, qt, hh:hh + 1],
                                             accum_out=rsum[:, u % 2, qt, hh:hh + 1]).then_inc(exp_done.sem, 1)

            def evacuate_pT(b, u):
                h = 2 * u
                act.wait_ge(pT_ps.sem, pT_ps.at(16 * b + h + 1))
                act.wait_ge(o_ps.sem, o_ps.at(4 * b + h // 4 - 1))
                nc.scalar.activation(pT[:, h % 8, :, :], ps_t[0][:].rearrange("p (k q) -> p k q", k=2),
                                     ACT.Copy).then_inc(pT_act.sem, 1)

            def evacuate_o(b, g):
                act.wait_ge(o_ps.sem, o_ps.at(4 * b + g + 1))
                act.wait_ge(out_ps.sem, out_ps.at(b))
                nc.scalar.activation(oT[:, g, :], ps_o[:, 0:S], ACT.Copy).then_inc(oT_ready.sem, 1)

            def body(b, more):
                for u in range(10):
                    if u >= 2:
                        evacuate_pT(b, u - 2)
                    if u in (4, 6, 8):
                        evacuate_o(b, u // 2 - 2)
                    if u < 8:
                        exponentials(b, u)
                    if u == 0:
                        evacuate_v(b)
                    if more and u == 2:
                        evacuate_xnT(b + 1)
                evacuate_o(b, 3)

            evacuate_xnT(0)
            with act.Fori(0, B - 1) as b:
                body(b, True)
            body(B - 1, False)

        @block.tensor
        def _(pe):
            for c in (v_ps, s_ps, pT_ps, o_ps, out_ps):
                pe.sem_inc(c.sem, c.credit)
            pe.wait_ge(w_loaded.sem, W_ALL)

            def transpose_xn(b):
                pe.wait_ge(xn_ready.sem, xn_ready.at(2 * b + 2))
                pe.wait_ge(x_done.sem, x_done.at(b - 1))
                for t in range(QT):
                    for k in range(2):
                        ins = pe.transpose(ps_m[:, k * S + t * P:k * S + (t + 1) * P], xn[:, t, k * P:(k + 1) * P],
                                           ident[:])
                ins.then_inc(xnT_ps.sem, 1)

            def project_qk(b, n):
                pe.wait_ge(qk_mul.sem, qk_mul.at(4 * b + n - 1))
                if n == 0:
                    pe.wait_ge(xnT_ready.sem, xnT_ready.at(b + 1))
                    pe.wait_ge(v_ready.sem, v_ready.at(b))
                col = (n % 2) * D + (n // 2) * P
                for j, w in enumerate((wqkv, wrot)):
                    for k in range(2):
                        ins = pe.matmul(ps_p[n % 2][:, j * S:(j + 1) * S], w[:, k, col:col + P], xnT[:, k, :],
                                        start=(k == 0), stop=(k == 1), skip_group_check=True)
                ins.then_inc(qk_ps.sem, 1)

            def project_v(b):
                pe.wait_ge(qk_mul.sem, qk_mul.at(4 * b + 3))
                for t in range(QT):
                    for k in range(2):
                        ins = pe.matmul(ps_p[0][:, t * D:(t + 1) * D], xnT[:, k, t * P:(t + 1) * P],
                                        wqkv[:, k, 2 * D:3 * D], start=(k == 0), stop=(k == 1), skip_group_check=True)
                ins.then_inc(v_ps.sem, 1)

            def scores(b, u):
                half = u // 4
                if u % 4 == 0:
                    pe.wait_ge(rope_done.sem, rope_done.at(4 * b + 2 * half + 1))
                    pe.wait_ge(km_ready.sem, km_ready.at(2 * b + half + 1))
                for qt in range(QT):
                    pe.wait_ge(exp_done.sem, exp_done.at(32 * b + 4 * u + 2 * qt - 2))
                    pe.matmul(ps_s[qt][:], qT[:, half, qt * P:(qt + 1) * P],
                              km[:, half, 2 * (u % 4):2 * (u % 4) + 2, :].rearrange("p h k -> p (h k)"),
                              start=True, stop=True).then_inc(s_ps.sem, 1)

            def transpose_p(b, u):
                pe.wait_ge(prob_ready.sem, prob_ready.at(32 * b + 4 * u + 4))
                for hh in range(2):
                    read = pT_dve if hh else pT_act
                    pe.wait_ge(read.sem, read.at(8 * b + u))
                    for kt in range(2):
                        for qt in range(QT):
                            ins = pe.transpose(ps_t[hh][:, kt * S + qt * P:kt * S + (qt + 1) * P],
                                               prob[:, u % 2, qt, hh, kt * P:(kt + 1) * P], ident[:])
                    ins.then_inc(pT_ps.sem, 1)

            def values(b, g):
                if g == 0:
                    pe.wait_ge(v_ready.sem, v_ready.at(b + 1))
                pe.wait_ge(pT_act.sem, pT_act.at(8 * b + 2 * g + 2))
                pe.wait_ge(pT_dve.sem, pT_dve.at(8 * b + 2 * g + 2))
                pe.wait_ge(oT_ready.sem, oT_ready.at(4 * b + g))
                for kt in range(2):
                    for j in range(4):
                        h = 4 * g + j
                        ins = pe.matmul(ps_o[32 * j:32 * j + 32, 0:S], v[:, kt, h, :], pT[:, h % 8, kt, :],
                                        start=(kt == 0), stop=(kt == 1), skip_group_check=True)
                ins.then_inc(o_ps.sem, 1)

            def project_out(b):
                pe.wait_ge(oT_ready.sem, oT_ready.at(4 * b + 4))
                pe.wait_ge(xnT_ready.sem, xnT_ready.at(min(b + 2, B) if isinstance(b, int) else b + 2))
                for t in range(QT):
                    for g in range(4):
                        ins = pe.matmul(ps_m[:, t * D:(t + 1) * D], oT[:, g, t * P:(t + 1) * P], wout[:, g, :],
                                        start=(g == 0), stop=(g == 3), skip_group_check=True)
                ins.then_inc(out_ps.sem, 1)

            def body(b, before, more):
                for u in range(8):
                    scores(b, u)
                    if u == 0:
                        project_v(b)
                        if before:
                            project_out(b - 1)
                    if more and u in (4, 5):
                        project_qk(b + 1, u - 4)
                    if u >= 1:
                        transpose_p(b, u - 1)
                    if more and u == 2:
                        transpose_xn(b + 1)
                    if u in (3, 5, 7):
                        values(b, u // 2 - 1)
                if more:
                    project_qk(b + 1, 2)
                transpose_p(b, 7)
                if more:
                    project_qk(b + 1, 3)
                values(b, 3)

            transpose_xn(0)
            pe.wait_ge(wrot_ready.sem, 4)
            for n in range(4):
                project_qk(0, n)
            body(0, False, True)
            with pe.Fori(1, B - 1) as b:
                body(b, True, True)
            body(B - 1, True, False)
            project_out(B - 1)


def cross_attention(nc, X, C, ident, x_raw, c_raw, media_w, media_b, lat_w, lat_b, Wq, Wk, Wv, Wout):
    PAIRS = H2 // 2
    KT = KV // P
    with Env(nc, "p2") as env:
        wq = env.sb("wq", [P, 2, INNER])
        wk = env.sb("wk", [P, 2, INNER])
        wv = env.sb("wv", [P, 2, INNER])
        wout = env.sb("wout", [P, PAIRS, D])
        affine = env.sb("affine", [P, 2, 2, 2])
        mv = env.sb("mv", [P, 2, TILES, 2])
        var = env.sb("var", [P, 2 * TILES])
        rstd = env.sb("rstd", [P, 2 * TILES])
        var2 = env.sb("var2", [P, TILES])
        rstd2 = env.sb("rstd2", [P, TILES])
        ntmp = env.sb("ntmp", [P, 2 * TILES])
        xn = env.sb("xn", [P, 2, QT, D])
        kvT = env.sb("kvT", [P, 2, KV])
        qT = env.sb("qT", [P, PAIRS, S])
        km = env.sb("km", [P, PAIRS, 2, KV])
        v = env.sb("v", [P, KT, INNER])
        prob = env.sb("prob", [P, 2, QT, KV])
        nmax = env.sb("nmax", [P, 2, QT])
        rsum = env.sb("rsum", [P, 2, QT])
        rinv = env.sb("rinv", [P, 2, QT])
        pT = env.sb("pT", [P, 4, KT, S])
        oT = env.sb("oT", [P, PAIRS, S])

        ps_s = [env.psum(f"s{i}") for i in range(2)]
        ps_t = [env.psum(f"t{i}") for i in range(2)]
        ps_o = env.psum("o")
        ps_p = [env.psum(f"p{i}") for i in range(2)]
        ps_m = env.psum("m")

        loaded, zeroed = env.sem("loaded"), env.sem("zeroed")
        stats, std_ready, step = env.sem("stats"), env.sem("std_ready"), env.sem("step")
        xn_ready = env.sem("xn_ready")
        xnT_ps = env.sem("xnT_ps")
        kvT_ready = env.sem("kvT_ready", 2)
        q_ps = env.sem("q_ps")
        q_ready = env.sem("q_ready", 1)
        k_ps = env.sem("k_ps")
        k_ready = env.sem("k_ready", 2)
        v_ps = env.sem("v_ps", 4)
        v_act = env.sem("v_act", 1)
        v_dve = env.sem("v_dve", 1)
        s_ps = env.sem("s_ps", 16)
        nmax_ready = env.sem("nmax_ready")
        exp_done = env.sem("exp_done", 2)
        inv_ready = env.sem("inv_ready")
        prob_ready = env.sem("prob_ready")
        pT_ps = env.sem("pT_ps", 4)
        pT_act = env.sem("pT_act", 1)
        pT_dve = env.sem("pT_dve", 1)
        o_ps = env.sem("o_ps", 2)
        oT_ready = env.sem("oT_ready", 1)
        out_ps = env.sem("out_ps", 1)
        x_done = env.sem("x_done", 1)
        block = env.block()
        LOADS = 16 * 12

        @block.sync
        def _(sp):
            for w, src in ((wq, Wq), (wk, Wk), (wv, Wv), (wout, Wout)):
                sp.dma_start(w[:], src.rearrange("(k p) n -> p k n", p=P)).then_inc(loaded.sem, 16)
            for n, src in enumerate((media_w, media_b, lat_w, lat_b)):
                for k in range(2):
                    sp.dma_start(affine[:, n // 2, n % 2, k:k + 1],
                                 src[k * P:(k + 1) * P].rearrange("(p a) -> p a", a=1)).then_inc(loaded.sem, 16)

        @block.vector
        def _(dve):
            for c in (v_dve, pT_dve, x_done, k_ready):
                dve.sem_inc(c.sem, c.credit)
            nc.vector.memset(km[:], 0.0).then_inc(zeroed.sem, 1)
            for a, raw in enumerate((c_raw, x_raw)):
                for t in range(TILES):
                    nc.vector.bn_aggr(mv[:, a, t, :], raw[:, t, :]).then_inc(stats.sem, 1)
            dve.wait_ge(stats.sem, 2 * TILES)
            nc.vector.tensor_scalar(var[:], mv[:].rearrange("p a t s -> p (a t) s")[:, :, 1], EPS, None, ALU.add
                                    ).then_inc(stats.sem, 1)
            dve.wait_ge(std_ready.sem, 1)
            refine_rsqrt(nc, dve, rstd[:], var[:], ntmp[:], step, 0)
            nc.vector.tensor_tensor(var2[:], rstd[:, TILES:], rstd[:, TILES:], ALU.mult).then_inc(step.sem, 1)
            dve.wait_ge(step.sem, 6)
            nc.vector.tensor_tensor(var2[:], var2[:], mv[:, 1, :, 1], ALU.mult).then_inc(step.sem, 1)
            dve.wait_ge(step.sem, 7)
            nc.vector.tensor_scalar(var2[:], var2[:], EPS, None, ALU.add).then_inc(step.sem, 1)
            dve.wait_ge(std_ready.sem, 2)
            refine_rsqrt(nc, dve, rstd2[:], var2[:], ntmp[:, 0:TILES], step, 8)
            nc.vector.tensor_tensor(rstd[:, TILES:], rstd[:, TILES:], rstd2[:], ALU.mult).then_inc(step.sem, 1)
            dve.wait_ge(step.sem, 14)

            def normalise(b):
                for a, src in enumerate((C, X)):
                    for t in range(QT):
                        nc.vector.tensor_scalar(
                            xn[:, a, t, :], src[:, bass.ds(QT * b + t, 1), :].rearrange("p a d -> p (a d)"),
                            mv[:, a, bass.ds(QT * b + t, 1), 0:1].rearrange("p a d -> p (a d)"),
                            rstd[:, bass.ds(TILES * a + QT * b + t, 1)],
                            ALU.subtract, ALU.mult).then_inc(xn_ready.sem, 1)

            def spread_k(b, j):
                dve.wait_ge(k_ps.sem, k_ps.at(4 * b + j + 1))
                dve.wait_ge(s_ps.sem, s_ps.at(16 * (b - 1) + 4 * j + 4))
                for hh in range(2):
                    r = slice(DH2 * hh, DH2 * hh + DH2)
                    nc.vector.tensor_copy(km[r, j, hh, :], ps_p[1][r, :]).then_inc(k_ready.sem, 1)

            def evacuate_v(b, t):
                dve.wait_ge(v_ps.sem, v_ps.at(4 * b + t + 1))
                dve.wait_ge(o_ps.sem, o_ps.at(4 * b))
                nc.vector.tensor_copy(v[:, t, :], ps_p[1][:]).then_inc(v_dve.sem, 1)

            def maxima(b, h):
                for qt in range(QT):
                    dve.wait_ge(s_ps.sem, s_ps.at(16 * b + 2 * h + qt + 1))
                    nc.vector.tensor_reduce(nmax[:, h % 2, qt:qt + 1], ps_s[qt][:], AX, ALU.max, negate=True
                                            ).then_inc(nmax_ready.sem, 1)

            def divide(b, h):
                for qt in range(QT):
                    dve.wait_ge(exp_done.sem, exp_done.at(16 * b + 2 * h + qt + 1))
                    nc.vector.reciprocal(rinv[:, h % 2, qt:qt + 1], rsum[:, h % 2, qt:qt + 1]).then_inc(inv_ready.sem, 1)
                for qt in range(QT):
                    dve.wait_ge(inv_ready.sem, inv_ready.at(16 * b + 2 * h + qt + 1))
                    nc.vector.tensor_scalar(prob[:, h % 2, qt, :], prob[:, h % 2, qt, :], rinv[:, h % 2, qt:qt + 1],
                                            None, ALU.mult).then_inc(prob_ready.sem, 1)

            def evacuate_pT(b, h):
                dve.wait_ge(pT_ps.sem, pT_ps.at(16 * b + 2 * h + 2))
                dve.wait_ge(o_ps.sem, o_ps.at(4 * b + h // 2 - 1))
                nc.vector.tensor_copy(pT[:, h % 4, 2:4, :], ps_t[1][:].rearrange("p (k q) -> p k q", k=2)
                                      ).then_inc(pT_dve.sem, 1)

            def later_stats(b):
                for t in range(QT):
                    nc.vector.bn_stats(x_raw[:, bass.ds(QT * b + t, 1), :].rearrange("p a s -> p (a s)"),
                                       X[:, bass.ds(QT * b + t, 1), :].rearrange("p a d -> p (a d)"))

            def finish(b):
                dve.wait_ge(out_ps.sem, out_ps.at(b + 1))
                nc.vector.tensor_tensor(X[:, bass.ds(QT * b, QT), :], X[:, bass.ds(QT * b, QT), :],
                                        ps_m[:].rearrange("p (t d) -> p t d", t=QT), ALU.add).then_inc(x_done.sem, 1)

            def body(b, before, more):
                for u in range(10):
                    if 1 <= u <= 8:
                        divide(b, u - 1)
                    if u >= 2:
                        evacuate_pT(b, u - 2)
                    if u < 8:
                        maxima(b, u)
                    if before and u == 1:
                        finish(b - 1)
                    if u == 0:
                        evacuate_v(b, 1)
                    if u == 1:
                        evacuate_v(b, 3)
                    if more and u in (5, 6, 7, 9):
                        spread_k(b + 1, (5, 6, 7, 9).index(u))
                if before:
                    dve.wait_ge(x_done.sem, x_done.at(b))
                    later_stats(b - 1)

            normalise(0)
            for j in range(PAIRS):
                spread_k(0, j)
            normalise(1)
            body(0, False, True)
            normalise(2)
            with dve.Fori(1, B - 2) as b:
                body(b, True, True)
                normalise(b + 2)
            body(B - 2, True, True)
            body(B - 1, True, False)
            finish(B - 1)
            dve.wait_ge(x_done.sem, x_done.at(B))
            later_stats(B - 1)

        @block.scalar
        def _(act):
            for c in (kvT_ready, q_ready, v_act, exp_done, pT_act, oT_ready):
                act.sem_inc(c.sem, c.credit)
            act.wait_ge(stats.sem, 2 * TILES + 1)
            nc.scalar.activation(rstd[:], var[:], ACT.Sqrt).then_inc(std_ready.sem, 1)
            act.wait_ge(step.sem, 8)
            nc.scalar.activation(rstd2[:], var2[:], ACT.Sqrt).then_inc(std_ready.sem, 1)
            act.wait_ge(loaded.sem, LOADS)

            def evacuate_kvT(b, a):
                act.wait_ge(xnT_ps.sem, xnT_ps.at(2 * b + a + 1))
                act.wait_ge(v_ps.sem, v_ps.at(4 * b))
                for k in range(2):
                    nc.scalar.activation(kvT[:, k, a * S:(a + 1) * S], ps_m[:, k * S:(k + 1) * S], ACT.Identity,
                                         scale=affine[:, a, 0, k:k + 1], bias=affine[:, a, 1, k:k + 1]
                                         ).then_inc(kvT_ready.sem, 1)

            def evacuate_q(b, j):
                act.wait_ge(q_ps.sem, q_ps.at(4 * b + j + 1))
                act.wait_ge(s_ps.sem, s_ps.at(16 * (b - 1) + 4 * j + 4))
                nc.scalar.activation(qT[:, j, :], ps_p[0][:, 0:S], ACT.Copy, scale=DH2 ** -0.5).then_inc(q_ready.sem, 1)

            def evacuate_v(b, t):
                act.wait_ge(v_ps.sem, v_ps.at(4 * b + t + 1))
                act.wait_ge(o_ps.sem, o_ps.at(4 * b))
                nc.scalar.activation(v[:, t, :], ps_p[0][:], ACT.Copy).then_inc(v_act.sem, 1)

            def exponentials(b, h):
                for qt in range(QT):
                    act.wait_ge(nmax_ready.sem, nmax_ready.at(16 * b + 2 * h + qt + 1))
                    act.wait_ge(pT_ps.sem, pT_ps.at(16 * b + 2 * h - 2))
                    nc.scalar.activation(prob[:, h % 2, qt, :], ps_s[qt][:], ACT.Exp, bias=nmax[:, h % 2, qt:qt + 1],
                                         accum_out=rsum[:, h % 2, qt:qt + 1]).then_inc(exp_done.sem, 1)

            def evacuate_pT(b, h):
                act.wait_ge(pT_ps.sem, pT_ps.at(16 * b + 2 * h + 1))
                act.wait_ge(o_ps.sem, o_ps.at(4 * b + h // 2 - 1))
                nc.scalar.activation(pT[:, h % 4, 0:2, :], ps_t[0][:].rearrange("p (k q) -> p k q", k=2),
                                     ACT.Copy).then_inc(pT_act.sem, 1)

            def evacuate_o(b, j):
                act.wait_ge(o_ps.sem, o_ps.at(4 * b + j + 1))
                act.wait_ge(out_ps.sem, out_ps.at(b))
                nc.scalar.activation(oT[:, j, :], ps_o[:, 0:S], ACT.Copy).then_inc(oT_ready.sem, 1)

            def body(b, more):
                for u in range(10):
                    if u >= 2:
                        evacuate_pT(b, u - 2)
                    if u in (4, 6, 8):
                        evacuate_o(b, u // 2 - 2)
                    if u < 8:
                        exponentials(b, u)
                    if u < 2:
                        evacuate_v(b, 2 * u)
                    if more and u in (2, 3):
                        evacuate_kvT(b + 1, u - 2)
                    if more and u in (4, 5, 6, 8):
                        evacuate_q(b + 1, (4, 5, 6, 8).index(u))
                evacuate_o(b, 3)

            evacuate_kvT(0, 0)
            evacuate_kvT(0, 1)
            for j in range(PAIRS):
                evacuate_q(0, j)
            with act.Fori(0, B - 1) as b:
                body(b, True)
            body(B - 1, False)

        @block.tensor
        def _(pe):
            for c in (v_ps, s_ps, pT_ps, o_ps, out_ps):
                pe.sem_inc(c.sem, c.credit)
            pe.wait_ge(loaded.sem, LOADS)

            def transpose_xn(b, a):
                pe.wait_ge(xn_ready.sem, xn_ready.at(4 * b + 2 * a + 2))
                pe.wait_ge(x_done.sem, x_done.at(b - 1))
                pe.wait_ge(kvT_ready.sem, kvT_ready.at(4 * b + 2 * a))
                for t in range(QT):
                    for k in range(2):
                        ins = pe.transpose(ps_m[:, k * S + t * P:k * S + (t + 1) * P], xn[:, a, t, k * P:(k + 1) * P],
                                           ident[:])
                ins.then_inc(xnT_ps.sem, 1)

            def project_qk(b, j):
                pe.wait_ge(kvT_ready.sem, kvT_ready.at(4 * b + 4))
                pe.wait_ge(q_ready.sem, q_ready.at(4 * b + j))
                pe.wait_ge(v_act.sem, v_act.at(2 * b))
                for k in range(2):
                    ins = pe.matmul(ps_p[0][:, 0:S], wq[:, k, j * P:(j + 1) * P], kvT[:, k, S:KV],
                                    start=(k == 0), stop=(k == 1))
                ins.then_inc(q_ps.sem, 1)
                pe.wait_ge(k_ready.sem, k_ready.at(8 * b + 2 * j))
                pe.wait_ge(v_dve.sem, v_dve.at(2 * b))
                for k in range(2):
                    ins = pe.matmul(ps_p[1][:], wk[:, k, j * P:(j + 1) * P], kvT[:, k, :], start=(k == 0), stop=(k == 1))
                ins.then_inc(k_ps.sem, 1)

            def project_v(b, tiles):
                for t in tiles:
                    if t < 2:
                        last = k_ready if t else q_ready
                        pe.wait_ge(last.sem, last.at((8 if t else 4) * (b + 1)))
                    else:
                        read = v_dve if t % 2 else v_act
                        pe.wait_ge(read.sem, read.at(2 * b + 1))
                    for k in range(2):
                        ins = pe.matmul(ps_p[t % 2][:], kvT[:, k, t * P:(t + 1) * P], wv[:, k, :],
                                        start=(k == 0), stop=(k == 1))
                    ins.then_inc(v_ps.sem, 1)

            def scores(b, h):
                j = h // 2
                if h % 2 == 0:
                    pe.wait_ge(q_ready.sem, q_ready.at(4 * b + j + 1))
                    pe.wait_ge(k_ready.sem, k_ready.at(8 * b + 2 * j + 2))
                for qt in range(QT):
                    pe.wait_ge(exp_done.sem, exp_done.at(16 * b + 2 * h + qt - 1))
                    pe.matmul(ps_s[qt][:], qT[:, j, qt * P:(qt + 1) * P], km[:, j, h % 2, :], start=True, stop=True
                              ).then_inc(s_ps.sem, 1)

            def transpose_p(b, h):
                pe.wait_ge(prob_ready.sem, prob_ready.at(16 * b + 2 * h + 2))
                for kk in range(2):
                    read = pT_dve if kk else pT_act
                    pe.wait_ge(read.sem, read.at(8 * b + h))
                    for k in range(2):
                        for qt in range(QT):
                            kt = 2 * kk + k
                            ins = pe.transpose(ps_t[kk][:, k * S + qt * P:k * S + (qt + 1) * P],
                                               prob[:, h % 2, qt, kt * P:(kt + 1) * P], ident[:])
                    ins.then_inc(pT_ps.sem, 1)

            def values(b, j):
                if j == 0:
                    pe.wait_ge(v_act.sem, v_act.at(2 * b + 2))
                    pe.wait_ge(v_dve.sem, v_dve.at(2 * b + 2))
                pe.wait_ge(pT_act.sem, pT_act.at(8 * b + 2 * j + 2))
                pe.wait_ge(pT_dve.sem, pT_dve.at(8 * b + 2 * j + 2))
                pe.wait_ge(oT_ready.sem, oT_ready.at(4 * b + j))
                for kt in range(KT):
                    for hh in range(2):
                        h = 2 * j + hh
                        ins = pe.matmul(ps_o[DH2 * hh:DH2 * hh + DH2, 0:S], v[:, kt, h * DH2:(h + 1) * DH2],
                                        pT[:, h % 4, kt, :], start=(kt == 0), stop=(kt == KT - 1), skip_group_check=True)
                ins.then_inc(o_ps.sem, 1)

            def project_out(b):
                pe.wait_ge(oT_ready.sem, oT_ready.at(4 * b + 4))
                pe.wait_ge(kvT_ready.sem, kvT_ready.at(min(4 * b + 8, 4 * B) if isinstance(b, int) else 4 * b + 8))
                for t in range(QT):
                    for j in range(PAIRS):
                        ins = pe.matmul(ps_m[:, t * D:(t + 1) * D], oT[:, j, t * P:(t + 1) * P], wout[:, j, :],
                                        start=(j == 0), stop=(j == PAIRS - 1), skip_group_check=True)
                ins.then_inc(out_ps.sem, 1)

            def body(b, before, more):
                for u in range(8):
                    scores(b, u)
                    if u < 2:
                        project_v(b, (2 * u, 2 * u + 1))
                    if before and u == 0:
                        project_out(b - 1)
                    if more and u in (4, 5, 6):
                        project_qk(b + 1, u - 4)
                    if u >= 1:
                        transpose_p(b, u - 1)
                    if more and u in (2, 3):
                        transpose_xn(b + 1, u - 2)
                    if u in (3, 5, 7):
                        values(b, u // 2 - 1)
                if more:
                    project_qk(b + 1, 3)
                transpose_p(b, 7)
                values(b, 3)

            transpose_xn(0, 0)
            transpose_xn(0, 1)
            for j in range(PAIRS):
                project_qk(0, j)
            body(0, False, True)
            with pe.Fori(1, B - 1) as b:
                body(b, True, True)
            body(B - 1, True, False)
            project_out(B - 1)


H_SCALE, W_SCALE = 16.0, 256.0


def ffn_input(nc, X, ident, x_raw, h_parts, gates_t, Wm, bm, expert_emb, rank):
    with Env(nc, "p3") as env:
        wm = env.sb("wm", [P, 2, D])
        bias = env.sb("bias", [P, 2])
        bias_s = env.sb("bias_s", [P, 2])
        emb = env.sb("emb", [P, 4 * E])
        rk = env.sb("rk", [P, E])
        mv = env.sb("mv", [P, TILES, 2])
        var = env.sb("var", [P, TILES])
        rstd = env.sb("rstd", [P, TILES])
        ntmp = env.sb("ntmp", [P, TILES])
        xn = env.sb("xn", [P, CT_, D])
        xnT = env.sb("xnT", [P, 2, CH])
        hf = env.sb("hf", [P, 2, CH])
        hs = env.sb("hs", [P, 2, CH])
        hi = env.sb("hi", [P, 2, CH], F16)
        lo = env.sb("lo", [P, 2, CH], F16)
        G = CT_ * HF
        w = env.sb("w", [P, G, E])
        w2 = env.sb("w2", [P, G, E])
        top = env.sb("top", [P, G])
        eq = env.sb("eq", [P, G, E])
        hot = env.sb("hot", [P, 2, G, E])
        den = env.sb("den", [P, G])
        gates = env.sb("gates", [P, CT_, HF * E])
        gT = env.sb("gT", [P, CH])

        ps_t = [env.psum(f"t{k}") for k in range(2)]
        ps_h = [env.psum(f"h{m}") for m in range(2)]
        ps_l = env.psum("l")
        ps_g = env.psum("g")

        loaded, zeroed = env.sem("loaded"), env.sem("zeroed")
        stats, std_ready, step = env.sem("stats"), env.sem("std_ready"), env.sem("step")
        xn_ready = env.sem("xn_ready")
        xnT_ps = env.sem("xnT_ps")
        xnT_ready = env.sem("xnT_ready", 2)
        h_ps = env.sem("h_ps", 2)
        hf_ready = env.sem("hf_ready")
        hs_ready = env.sem("hs_ready", 2)
        hi_ready = env.sem("hi_ready")
        lo_ready = env.sem("lo_ready", 2)
        logits_ps = env.sem("logits_ps", 1)
        less_max = env.sem("less_max", 1)
        exp_done = env.sem("exp_done")
        top_step = env.sem("top_step")
        gates_ready = env.sem("gates_ready")
        gT_ps = env.sem("gT_ps", 1)
        gT_ready = env.sem("gT_ready", 1)
        hi_stored, lo_stored = env.sem("hi_stored", 16), env.sem("lo_stored", 16)
        gT_stored = env.sem("gT_stored", 16)
        block = env.block()
        LOADS = 16 * (2 + 2 + 4)
        TOP = 17

        @block.sync
        def _(sp):
            sp.wait_ge(zeroed.sem, 1)
            sp.dma_start(wm[:], Wm.rearrange("(k p) n -> p k n", p=P)).then_inc(loaded.sem, 16)
            sp.dma_start(rk[:], rank).then_inc(loaded.sem, 16)
            for m in range(2):
                sp.dma_start(bias[:, m:m + 1], bm[m * P:(m + 1) * P].rearrange("(p a) -> p a", a=1)
                             ).then_inc(loaded.sem, 16)
            for j in range(4):
                sp.dma_start(emb[HD * j:HD * (j + 1), E * j:E * (j + 1)], expert_emb).then_inc(loaded.sem, 16)

        @block.vector
        def _(dve):
            dve.sem_inc(less_max.sem, less_max.credit)
            nc.vector.memset(emb[:], 0.0).then_inc(zeroed.sem, 1)
            for t in range(TILES):
                nc.vector.bn_aggr(mv[:, t, :], x_raw[:, t, :]).then_inc(stats.sem, 1)
            dve.wait_ge(stats.sem, TILES)
            nc.vector.tensor_scalar(var[:], mv[:, :, 1], EPS, None, ALU.add).then_inc(stats.sem, 1)
            dve.wait_ge(std_ready.sem, 1)
            refine_rsqrt(nc, dve, rstd[:], var[:], ntmp[:], step, 0)
            dve.wait_ge(loaded.sem, LOADS)

            def normalise(c):
                for t in range(CT_):
                    nc.vector.tensor_scalar(xn[:, t, :], X[:, bass.ds(CT_ * c + t, 1), :].rearrange("p a d -> p (a d)"),
                                            mv[:, bass.ds(CT_ * c + t, 1), 0:1].rearrange("p a d -> p (a d)"),
                                            rstd[:, bass.ds(CT_ * c + t, 1)],
                                            ALU.subtract, ALU.mult).then_inc(xn_ready.sem, 1)

            def wide(a):
                return a.unsqueeze(2).broadcast_to([P, G, E])

            def select(c):
                made = [0]

                def then_wait(ins):
                    ins.then_inc(top_step.sem, 1)
                    made[0] += 1
                    dve.wait_ge(top_step.sem, top_step.at(TOP * c + made[0]))

                ranks = rk[:].unsqueeze(1).broadcast_to([P, G, E])
                logits = ps_l[:].rearrange("p (g e) -> p g e", e=E)
                dve.wait_ge(logits_ps.sem, logits_ps.at(c + 1))
                then_wait(nc.vector.tensor_reduce(top[:], logits, AX, ALU.max))
                nc.vector.tensor_tensor(w[:], logits, wide(top[:]), ALU.subtract).then_inc(less_max.sem, 1)
                dve.wait_ge(exp_done.sem, exp_done.at(c + 1))
                then_wait(nc.vector.tensor_reduce(den[:], w[:], AX, ALU.add))
                then_wait(nc.vector.reciprocal(den[:], den[:]))
                then_wait(nc.vector.tensor_tensor(w[:], w[:], wide(den[:]), ALU.mult))
                src = w
                for n in range(2):
                    then_wait(nc.vector.tensor_reduce(top[:], src[:], AX, ALU.max))
                    then_wait(nc.vector.tensor_tensor(eq[:], src[:], wide(top[:]), ALU.is_equal))
                    then_wait(nc.vector.tensor_tensor(eq[:], eq[:], ranks, ALU.mult))
                    then_wait(nc.vector.tensor_reduce(top[:], eq[:], AX, ALU.max))
                    then_wait(nc.vector.tensor_tensor(hot[:, n], eq[:], wide(top[:]), ALU.is_equal))
                    if n == 0:
                        then_wait(nc.vector.scalar_tensor_tensor(w2[:].rearrange("p g e -> p (g e)"),
                                                                 hot[:, 0].rearrange("p g e -> p (g e)"), -2.0,
                                                                 w[:].rearrange("p g e -> p (g e)"), ALU.mult, ALU.add))
                        src = w2
                then_wait(nc.vector.tensor_tensor(eq[:], hot[:, 0], hot[:, 1], ALU.add))
                dve.wait_ge(gT_ps.sem, gT_ps.at(c))
                then_wait(nc.vector.tensor_tensor(gates[:].rearrange("p t (h e) -> p (t h) e", e=E), eq[:], w[:],
                                                  ALU.mult))
                dve.sem_inc(gates_ready.sem, 1)
                assert made[0] == TOP

            normalise(0)
            dve.wait_ge(xnT_ps.sem, xnT_ps.at(2))
            with dve.Fori(0, CHUNKS - 1) as c:
                normalise(c + 1)
                select(c)
                dve.wait_ge(xnT_ps.sem, xnT_ps.at(2 * c + 4))
            select(CHUNKS - 1)

        @block.gpsimd
        def _(pool):
            pool.sem_inc(lo_ready.sem, lo_ready.credit)

            with pool.Fori(0, CHUNKS) as c:
                for m in range(2):
                    pool.wait_ge(hi_ready.sem, hi_ready.at(2 * c + m + 1))
                    pool.wait_ge(lo_stored.sem, lo_stored.at(16 * c))
                    nc.gpsimd.tensor_tensor(lo[:, m, :], hs[:, m, :], hi[:, m, :], ALU.subtract
                                            ).then_inc(lo_ready.sem, 1)

        @block.scalar
        def _(act):
            for c in (xnT_ready, hs_ready, gT_ready, hi_stored, lo_stored, gT_stored):
                act.sem_inc(c.sem, c.credit)
            act.wait_ge(stats.sem, TILES + 1)
            nc.scalar.activation(rstd[:], var[:], ACT.Sqrt).then_inc(std_ready.sem, 1)
            act.wait_ge(loaded.sem, LOADS)
            nc.scalar.activation(bias_s[:], bias[:], ACT.Copy, scale=H_SCALE).then_inc(std_ready.sem, 1)
            act.wait_ge(std_ready.sem, 2)

            def front(c):
                for k in range(2):
                    act.wait_ge(xnT_ps.sem, xnT_ps.at(2 * c + k + 1))
                    act.wait_ge(h_ps.sem, h_ps.at(2 * c))
                    nc.scalar.activation(xnT[:, k, :], ps_t[k][:], ACT.Copy).then_inc(xnT_ready.sem, 1)
                for m in range(2):
                    act.wait_ge(h_ps.sem, h_ps.at(2 * c + m + 1))
                    act.wait_ge(logits_ps.sem, logits_ps.at(c))
                    nc.scalar.activation(hf[:, m, :], ps_h[m][:], ACT.Identity, bias=bias[:, m:m + 1]
                                         ).then_inc(hf_ready.sem, 1)
                    act.wait_ge(lo_ready.sem, lo_ready.at(2 * c))
                    nc.scalar.activation(hs[:, m, :], ps_h[m][:], ACT.Identity, bias=bias_s[:, m:m + 1], scale=H_SCALE
                                         ).then_inc(hs_ready.sem, 1)
                    act.wait_ge(hs_ready.sem, hs_ready.at(2 * c + m + 1))
                    act.wait_ge(hi_stored.sem, hi_stored.at(16 * c))
                    nc.scalar.activation(hi[:, m, :], hs[:, m, :], ACT.Copy).then_inc(hi_ready.sem, 1)

            def store_part(c, n, buf, ready, stored):
                act.wait_ge(ready.sem, ready.at(2 * c + 2))
                act.dma_start(h_parts[n].rearrange("(m p) t -> p m t", p=P)[:, :, bass.ds(CH * c, CH)], buf[:]
                              ).then_inc(stored.sem, 16)

            def body(c, more):
                act.wait_ge(less_max.sem, less_max.at(c + 1))
                nc.scalar.activation(w[:], w[:], ACT.Exp).then_inc(exp_done.sem, 1)
                store_part(c, 0, hi, hi_ready, hi_stored)
                store_part(c, 1, lo, lo_ready, lo_stored)
                if more:
                    front(c + 1)
                act.wait_ge(gT_ps.sem, gT_ps.at(c + 1))
                act.wait_ge(gT_stored.sem, gT_stored.at(16 * c))
                nc.scalar.activation(gT[:], ps_g[:], ACT.Copy).then_inc(gT_ready.sem, 1)
                act.wait_ge(gT_ready.sem, gT_ready.at(c + 1))
                act.dma_start(gates_t[:, bass.ds(CH * c, CH)], gT[:]).then_inc(gT_stored.sem, 16)

            front(0)
            with act.Fori(0, CHUNKS - 1) as c:
                body(c, True)
            body(CHUNKS - 1, False)
            for stored in (hi_stored, lo_stored, gT_stored):
                act.wait_ge(stored.sem, stored.at(16 * CHUNKS))

        @block.tensor
        def _(pe):
            for c in (h_ps, logits_ps, gT_ps):
                pe.sem_inc(c.sem, c.credit)
            pe.wait_ge(loaded.sem, LOADS)

            def front(c):
                pe.wait_ge(xn_ready.sem, xn_ready.at(4 * c + 4))
                pe.wait_ge(xnT_ready.sem, xnT_ready.at(2 * c))
                for k in range(2):
                    for t in range(CT_):
                        ins = pe.transpose(ps_t[k][:, t * P:(t + 1) * P], xn[:, t, k * P:(k + 1) * P], ident[:])
                    ins.then_inc(xnT_ps.sem, 1)
                pe.wait_ge(xnT_ready.sem, xnT_ready.at(2 * c + 2))
                pe.wait_ge(hs_ready.sem, hs_ready.at(2 * c))
                for m in range(2):
                    for k in range(2):
                        ins = pe.matmul(ps_h[m][:], wm[:, k, m * P:(m + 1) * P], xnT[:, k, :],
                                        start=(k == 0), stop=(k == 1))
                    ins.then_inc(h_ps.sem, 1)

            def logits(c):
                pe.wait_ge(hf_ready.sem, hf_ready.at(2 * c + 2))
                pe.wait_ge(less_max.sem, less_max.at(c))
                for t in range(CT_):
                    for m in range(2):
                        ins = pe.matmul(ps_l[:, t * P + m * 64:t * P + (m + 1) * 64], hf[:, m, t * P:(t + 1) * P],
                                        emb[:], start=True, stop=True, skip_group_check=True)
                ins.then_inc(logits_ps.sem, 1)

            def transpose_gates(c):
                pe.wait_ge(top_step.sem, top_step.at(TOP * c + TOP))
                pe.wait_ge(gates_ready.sem, gates_ready.at(c + 1))
                pe.wait_ge(gT_ready.sem, gT_ready.at(c))
                for t in range(CT_):
                    ins = pe.transpose(ps_g[:, t * P:(t + 1) * P], gates[:, t, :], ident[:])
                ins.then_inc(gT_ps.sem, 1)

            front(0)
            logits(0)
            with pe.Fori(0, CHUNKS - 1) as c:
                front(c + 1)
                logits(c + 1)
                transpose_gates(c)
            transpose_gates(CHUNKS - 1)


def experts(nc, X, h_parts, gates_t, W1, b1, W2, b2, Wo, bo, fold_in, out):
    G4 = E // 4
    K1 = 3 * HD
    GROUPS = HF * G4
    with Env(nc, "p4") as env:
        w1f = env.sb("w1f", [K1, E, I])
        w1h = env.sb("w1h", [K1, E, I], F16)
        w1 = env.sb("w1", [K1 + 3, E, I], F16)
        b1f = env.sb("b1f", [1, 2, E * I])
        b1p = env.sb("b1p", [1, 3, E * I], F16)
        w2 = env.sb("w2", [P, E, HD])
        b2c = env.sb("b2c", [P, G4])
        wo = env.sb("wo", [P, 2, D])
        bob = env.sb("bob", [P, 2, D])
        fold = env.sb("fold", [P, HD])
        hx = env.sb("hx", [K1 + 3, HF, CH], F16)
        gb = env.sb("gb", [P, 2, G4, CH])
        act_out = env.sb("act_out", [P, 4, 2, CH])
        pr = env.sb("pr", [P, 2, G4, CH])
        half = env.sb("half", [P, 2, CH])
        sums = env.sb("sums", [P, 8, CH])
        comb = env.sb("comb", [P, 2, CH])
        y = env.sb("y", [P, 2, 2, D])

        ps_u = [env.psum(f"u{i}", 2) for i in range(2)]
        ps_e = [env.psum(f"e{i}") for i in range(2)]
        ps_c = env.psum("c")
        ps_y = env.psum("y")

        loaded, prep = env.sem("loaded"), env.sem("prep")
        b1_placed, w1_ready = env.sem("b1_placed"), env.sem("w1_ready")
        hx_loaded = [env.sem(f"hx_loaded{h}") for h in range(HF)]
        gb_loaded = [env.sem(f"gb_loaded{i}") for i in range(2)]
        u_ps = env.sem("u_ps", 8 * HF)
        gelu_done = env.sem("gelu_done", 2)
        e_ps = env.sem("e_ps", 2)
        pr_ready = env.sem("pr_ready", 8)
        half_ready = env.sem("half_ready")
        sum_ready = env.sem("sum_ready", 8)
        c_ps = env.sem("c_ps", 2)
        comb_ready = env.sem("comb_ready", 1)
        y_ps = env.sem("y_ps", 2)
        y_part = env.sem("y_part", 1)
        y_ready = env.sem("y_ready")
        y_stored = [env.sem(f"y_stored{i}", 16) for i in range(2)]
        block = env.block()
        LOADS = 16 * (3 + 1 + 1 + 4 + 1 + 2 + 1)

        @block.sync
        def _(sp):
            for r in range(3):
                sp.dma_start(w1f[HD * r:HD * (r + 1), :, :], W1.rearrange("e d i -> d e i")).then_inc(loaded.sem, 16)
            sp.dma_start(b1f[:, 0, :], b1.rearrange("(a e) i -> a (e i)", a=1)).then_inc(loaded.sem, 16)
            sp.dma_start(w2[:], W2.rearrange("e i o -> i e o")).then_inc(loaded.sem, 16)
            for j in range(4):
                sp.dma_start(b2c[HD * j:HD * (j + 1), :], b2.rearrange("(g j) o -> j o g", j=4)[j],
                             allow_slow_non_contiguous=True).then_inc(loaded.sem, 16)
            sp.dma_start(wo[:], Wo.rearrange("(k p) n -> p k n", p=P)).then_inc(loaded.sem, 16)
            for t in range(2):
                sp.dma_start(bob[:, t, :], bo.rearrange("(a n) -> a n", a=1).broadcast_to([P, D])
                             ).then_inc(loaded.sem, 16)
            sp.dma_start(fold[:], fold_in).then_inc(loaded.sem, 16)

            def load_h(c, h):
                for r, part in enumerate((0, 1, 0)):
                    sp.dma_start(hx[HD * r:HD * (r + 1), h, :],
                                 h_parts[part][HD * h:HD * (h + 1), bass.ds(CH * c, CH)]).then_inc(hx_loaded[h].sem, 16)

            def load_gates(c, h):
                sp.wait_ge(pr_ready.sem, pr_ready.at(GROUPS * c + G4 * (h - 1)))
                for j in range(4):
                    src = gates_t.rearrange("(h g j) t -> h j g t", h=HF, j=4)[h, j, :, bass.ds(CH * c, CH)]
                    sp.dma_start(gb[HD * j:HD * (j + 1), h % 2, :, :], src.unsqueeze(0).broadcast_to([HD, G4, CH])
                                 ).then_inc(gb_loaded[h % 2].sem, 16)

            ov = out.rearrange("b (t p) d -> p (b t) d", p=P)

            def store_y(c, n):
                sp.wait_ge(y_ready.sem, y_ready.at(2 * c + n + 1))
                sp.dma_start(ov[:, bass.ds(CT_ * c + 2 * n, 2), :], y[:, n, :, :]).then_inc(y_stored[n].sem, 16)

            for c in y_stored:
                sp.sem_inc(c.sem, c.credit)
            for h in range(HF):
                load_h(0, h)
            for r in range(3):
                sp.wait_ge(prep.sem, 3 + 2 * r)
                sp.dma_start(w1[K1 + r:K1 + r + 1, :, :], b1p[:, r, :].rearrange("a (e i) -> a e i", e=E)
                             ).then_inc(b1_placed.sem, 16)
            def body(c, before, more):
                for h in range(HF):
                    load_gates(c, h)
                    if before and h in (3, 4):
                        store_y(c - 1, h - 3)
                    if more and h >= 2:
                        sp.wait_ge(u_ps.sem, u_ps.at(8 * HF * c + 8 * (h - 1)))
                        load_h(c + 1, h - 2)
                if more:
                    for h in (HF - 2, HF - 1):
                        sp.wait_ge(u_ps.sem, u_ps.at(8 * HF * c + 8 * (h + 1)))
                        load_h(c + 1, h)

            body(0, False, True)
            with sp.Fori(1, CHUNKS - 1) as c:
                body(c, True, True)
            body(CHUNKS - 1, True, False)
            for n in range(2):
                store_y(CHUNKS - 1, n)
            for n in range(2):
                sp.wait_ge(y_stored[n].sem, y_stored[n].at(16 * CHUNKS))

        @block.gpsimd
        def _(pool):
            pool.sem_inc(sum_ready.sem, sum_ready.credit)
            with pool.Fori(0, CHUNKS) as c:
                for h in range(HF):
                    pool.wait_ge(pr_ready.sem, pr_ready.at(GROUPS * c + G4 * (h + 1)))
                    pool.wait_ge(sum_ready.sem, sum_ready.at(8 * c + h))
                    nc.gpsimd.tensor_tensor(half[:], pr[:, h % 2, 0:2, :], pr[:, h % 2, 2:4, :], ALU.add
                                            ).then_inc(half_ready.sem, 1)
                    pool.wait_ge(half_ready.sem, half_ready.at(8 * c + h + 1))
                    pool.wait_ge(c_ps.sem, c_ps.at(2 * c + h // 4 - 1))
                    nc.gpsimd.tensor_tensor(sums[:, h, :], half[:, 0, :], half[:, 1, :], ALU.add
                                            ).then_inc(sum_ready.sem, 1)

        @block.vector
        def _(dve):
            for c in (pr_ready, comb_ready, y_part):
                dve.sem_inc(c.sem, c.credit)
            dve.wait_ge(loaded.sem, LOADS)
            nc.vector.tensor_scalar(b1f[:, 0, :], b1f[:, 0, :], W_SCALE, None, ALU.mult).then_inc(prep.sem, 1)
            nc.vector.memset(hx[K1:K1 + 3, :, :], H_SCALE).then_inc(prep.sem, 1)
            dve.wait_ge(prep.sem, 2)
            for r in range(3):
                nc.vector.tensor_copy(b1p[:, r, :], b1f[:, r % 2, :]).then_inc(prep.sem, 1)
                dve.wait_ge(prep.sem, 3 + 2 * r)
                if r < 2:
                    nc.vector.tensor_tensor(b1f[:, (r + 1) % 2, :], b1f[:, r % 2, :], b1p[:, r, :], ALU.subtract
                                            ).then_inc(prep.sem, 1)
                    dve.wait_ge(prep.sem, 4 + 2 * r)
            nc.vector.tensor_scalar(w1h[:], w1f[:], W_SCALE, None, ALU.mult).then_inc(w1_ready.sem, 1)
            dve.wait_ge(w1_ready.sem, 1)
            nc.vector.tensor_copy(w1[0:2 * HD], w1h[0:2 * HD]).then_inc(w1_ready.sem, 1)
            nc.vector.scalar_tensor_tensor(w1[2 * HD:K1].rearrange("p e i -> p (e i)"),
                                           w1f[2 * HD:K1].rearrange("p e i -> p (e i)"), W_SCALE,
                                           w1h[2 * HD:K1].rearrange("p e i -> p (e i)"), ALU.mult, ALU.subtract
                                           ).then_inc(w1_ready.sem, 1)

            def gate(c, n):
                h, g = divmod(n, G4)
                dve.wait_ge(e_ps.sem, e_ps.at(GROUPS * c + n + 1))
                if g == 0:
                    dve.wait_ge(gb_loaded[h % 2].sem, 64 * (4 * c + h // 2 + 1))
                    dve.wait_ge(sum_ready.sem, sum_ready.at(8 * c + h - 1))
                nc.vector.scalar_tensor_tensor(pr[:, h % 2, g, :], ps_e[n % 2][:], b2c[:, g:g + 1], gb[:, h % 2, g, :],
                                               ALU.add, ALU.mult).then_inc(pr_ready.sem, 1)

            def evacuate_comb(c, q):
                dve.wait_ge(c_ps.sem, c_ps.at(2 * c + q + 1))
                dve.wait_ge(y_ps.sem, y_ps.at(2 * c))
                nc.vector.tensor_copy(comb[:, q, :], ps_c[:]).then_inc(comb_ready.sem, 1)

            def finish(c, n):
                dve.wait_ge(y_ps.sem, y_ps.at(2 * c + n + 1))
                dve.wait_ge(y_stored[n].sem, y_stored[n].at(16 * c))
                nc.vector.tensor_tensor(y[:, n, :, :], ps_y[:].rearrange("p (t d) -> p t d", t=2), bob[:], ALU.add
                                        ).then_inc(y_part.sem, 1)
                dve.wait_ge(y_part.sem, y_part.at(2 * c + n + 1))
                nc.vector.tensor_tensor(y[:, n, :, :], y[:, n, :, :], X[:, bass.ds(CT_ * c + 2 * n, 2), :], ALU.add
                                        ).then_inc(y_ready.sem, 1)

            def body(c, before):
                for n in range(GROUPS):
                    gate(c, n)
                    if n == 18:
                        evacuate_comb(c, 0)
                    if before and n == 2:
                        evacuate_comb(c - 1, 1)
                    if before and n in (4, 6):
                        finish(c - 1, n // 2 - 2)

            body(0, False)
            with dve.Fori(1, CHUNKS) as c:
                body(c, True)
            evacuate_comb(CHUNKS - 1, 1)
            for n in range(2):
                finish(CHUNKS - 1, n)

        @block.scalar
        def _(act):
            act.sem_inc(gelu_done.sem, gelu_done.credit)
            with act.Fori(0, CHUNKS) as c:
                for n in range(8 * HF):
                    act.wait_ge(u_ps.sem, u_ps.at(8 * HF * c + n + 1))
                    act.wait_ge(e_ps.sem, e_ps.at(GROUPS * c + n // 2 - 1))
                    nc.scalar.activation(act_out[:, n % 4, :, :], ps_u[n % 2][:], ACT.Gelu,
                                         scale=1.0 / (H_SCALE * W_SCALE)).then_inc(gelu_done.sem, 1)

        @block.tensor
        def _(pe):
            for c in (u_ps, e_ps, c_ps, y_ps):
                pe.sem_inc(c.sem, c.credit)
            pe.wait_ge(loaded.sem, LOADS)
            pe.wait_ge(prep.sem, 2)
            pe.wait_ge(b1_placed.sem, 48)
            pe.wait_ge(w1_ready.sem, 3)

            def up(c, n):
                h, e2 = divmod(n, 8)
                if e2 == 0:
                    pe.wait_ge(hx_loaded[h].sem, 48 * (c + 1))
                pe.wait_ge(gelu_done.sem, gelu_done.at(8 * HF * c + n - 1))
                for i in range(2):
                    ins = pe.matmul(ps_u[n % 2][:, i, :], w1[:, 2 * e2 + i, :], hx[:, h, :], start=True, stop=True)
                ins.then_inc(u_ps.sem, 1)

            def down(c, n):
                g = n % G4
                pe.wait_ge(gelu_done.sem, gelu_done.at(8 * HF * c + 2 * n + 2))
                pe.wait_ge(pr_ready.sem, pr_ready.at(GROUPS * c + n - 1))
                for j in range(4):
                    ins = pe.matmul(ps_e[n % 2][HD * j:HD * (j + 1), :], w2[:, 4 * g + j, :],
                                    act_out[:, (2 * n + j // 2) % 4, j % 2, :], start=True, stop=True,
                                    skip_group_check=True)
                ins.then_inc(e_ps.sem, 1)

            def combine(c, q):
                pe.wait_ge(sum_ready.sem, sum_ready.at(8 * c + 4 * q + 4))
                pe.wait_ge(comb_ready.sem, comb_ready.at(2 * c + q))
                for j in range(4):
                    ins = pe.matmul(ps_c[HD * j:HD * (j + 1), :], fold[:], sums[:, 4 * q + j, :],
                                    start=True, stop=True, skip_group_check=True)
                ins.then_inc(c_ps.sem, 1)

            def project_out(c, n):
                pe.wait_ge(comb_ready.sem, comb_ready.at(2 * c + 2))
                pe.wait_ge(y_part.sem, y_part.at(2 * c + n))
                for t in range(2):
                    for k in range(2):
                        ins = pe.matmul(ps_y[:, t * D:(t + 1) * D], comb[:, k, (2 * n + t) * P:(2 * n + t + 1) * P],
                                        wo[:, k, :], start=(k == 0), stop=(k == 1), skip_group_check=True)
                ins.then_inc(y_ps.sem, 1)

            def body(c, before):
                for n in range(GROUPS):
                    up(c, 2 * n)
                    up(c, 2 * n + 1)
                    if n >= 1:
                        down(c, n - 1)
                    elif before:
                        down(c - 1, GROUPS - 1)
                    if n == 18:
                        combine(c, 0)
                    if before and n == 2:
                        combine(c - 1, 1)
                    if before and n in (4, 6):
                        project_out(c - 1, n // 2 - 2)

            body(0, False)
            with pe.Fori(1, CHUNKS) as c:
                body(c, True)
            down(CHUNKS - 1, GROUPS - 1)
            combine(CHUNKS - 1, 1)
            for n in range(2):
                project_out(CHUNKS - 1, n)


def constants():
    p = np.arange(P)
    theta = np.float32(1.0) / np.float32(10000.0) ** (np.arange(0, DH1, 2, dtype=np.float32) / np.float32(DH1))
    angle = np.outer(np.arange(S, dtype=np.float32), theta.astype(np.float32)).astype(np.float32)
    angle = np.concatenate([angle, angle], axis=1)[:, p % DH1].T
    sign = np.where(p % DH1 < DH1 // 2, -1.0, 1.0).astype(np.float32)[:, None]
    table = np.concatenate([np.cos(angle), sign * np.sin(angle)], axis=1).astype(np.float32)
    return {
        "ident_in": np.eye(P, dtype=np.float32),
        "rope": np.stack([table * np.float32(DH1 ** -0.5), table], axis=1).astype(np.float32),
        "head_mask": (p[:, None] // DH1 == np.arange(8)[None, :]).astype(np.float32),
        "rank": np.broadcast_to(np.arange(E, 0, -1, dtype=np.float32), (P, E)).copy(),
        "fold_in": np.tile(np.eye(HD, dtype=np.float32), (P // HD, 1)),
    }


def decoder(nc, x, ctx_1024, w_qkv, w_out, b_out, media_w, media_b, lat_w, lat_b, Wq, Wk, Wv, Wout,
            Wm, bm, expert_emb, W1, b1, W2, b2, Wo, bo, ident_in, rope, head_mask, rank, fold_in, out):
    h_parts = nc.dram_tensor("h_parts", [2, D, B * S], F16).ap()
    gates_t = nc.dram_tensor("gates_t", [HF * E, B * S], F32).ap()
    with ExitStack() as ctx:
        X, ident, x_raw = (ctx.enter_context(nc.sbuf_tensor(name, shape, F32)) for name, shape in
                           (("X", [P, TILES, D]), ("ident", [P, P]), ("x_raw", [P, TILES, 6])))
        with nc.sbuf_tensor("C", [P, TILES, D], F32) as C, nc.sbuf_tensor("c_raw", [P, TILES, 6], F32) as c_raw:
            self_attention(nc, X, C, ident, x_raw, c_raw, x, ctx_1024, ident_in, w_qkv, w_out, b_out, rope, head_mask)
            cross_attention(nc, X, C, ident, x_raw, c_raw, media_w, media_b, lat_w, lat_b, Wq, Wk, Wv, Wout)
        ffn_input(nc, X, ident, x_raw, h_parts, gates_t, Wm, bm, expert_emb, rank)
        experts(nc, X, h_parts, gates_t, W1, b1, W2, b2, Wo, bo, fold_in, out)


_INS = ["x", "ctx_1024", "L0_attn_w_qkv", "L0_attn_w_out", "L0_attn_b_out",
        "L0_xattn_ln_media_w", "L0_xattn_ln_media_b", "L0_xattn_ln_lat_w", "L0_xattn_ln_lat_b",
        "L0_xattn_Wq", "L0_xattn_Wk", "L0_xattn_Wv", "L0_xattn_Wout",
        "L0_ffn_Wm", "L0_ffn_bm", "L0_ffn_expert_emb", "L0_ffn_W1", "L0_ffn_b1", "L0_ffn_W2", "L0_ffn_b2",
        "L0_ffn_Wo", "L0_ffn_bo"]


def kernel(**inputs):
    import concourse.bacc as bacc
    from concourse.bass_utils import run_bass_kernel_spmd

    nc = bacc.Bacc("TRN2", target_bir_lowering=False, num_devices=1)
    arrays, args = {}, []
    for name, a in [(n, inputs[n]) for n in _INS] + list(constants().items()):
        a = np.ascontiguousarray(a)
        arrays[f"in_{name}_dram"] = a
        args.append(nc.dram_tensor(f"in_{name}_dram", a.shape, mybir.dt.from_np(a.dtype), kind="ExternalInput").ap())
    args.append(nc.dram_tensor("out_0_dram", (B, S, D), F32, kind="ExternalOutput").ap())
    decoder(nc, *args)
    r = run_bass_kernel_spmd(nc, [arrays], core_ids=[0])
    return r.results[0]["out_0_dram"]
```

```python
from contextlib import ExitStack

import numpy as np

import concourse.bass as bass
from concourse import mybir

F32 = mybir.dt.float32
F16 = mybir.dt.float16
ALU = mybir.AluOpType
ACT = mybir.ActivationFunctionType
AX = mybir.AxisListType.X

P = 128
B, S, D = 16, 256, 256
TILES = B * S // P
QT = S // P
EPS = 1e-5
H1, DH1 = 16, 16
H2, DH2 = 8, 64
INNER = H2 * DH2
KV = 2 * S
HF, HD, E, I = 8, 32, 16, 128
CH = 512
CHUNKS = B * S // CH
CT_ = CH // P


class Count:

    def __init__(self, sem, credit):
        self.sem, self.credit = sem, credit

    def at(self, n):
        return n + self.credit


class Env:

    def __init__(self, nc, name):
        self.nc, self.name, self.ctx = nc, name, ExitStack()

    def __enter__(self):
        self.ctx.__enter__()
        return self

    def __exit__(self, *a):
        return self.ctx.__exit__(*a)

    def sb(self, name, shape, dt=F32):
        return self.ctx.enter_context(self.nc.sbuf_tensor(f"{self.name}_{name}", shape, dt))

    def psum(self, name, banks=1):
        shape = [P, 512] if banks == 1 else [P, banks, 512]
        return self.ctx.enter_context(self.nc.psum_tensor(f"{self.name}_ps_{name}", shape, F32))

    def sem(self, name, credit=0):
        return Count(self.ctx.enter_context(self.nc.semaphore(f"{self.name}_{name}")), credit)

    def block(self):
        return self.ctx.enter_context(self.nc.Block())


def ln_statistics(nc, dve, env, x, n, mean_var, done, at=0):
    raw = env.sb(f"ln_raw{at}", [P, n, 6])
    for t in range(n):
        nc.vector.bn_stats(raw[:, t, :], x(t)).then_inc(done.sem, 1)
    for t in range(n):
        dve.wait_ge(done.sem, done.at(at + t + 1))
        nc.vector.bn_aggr(mean_var[:, t, :], raw[:, t, :]).then_inc(done.sem, 1)


def refine_rsqrt(nc, dve, rstd, var, tmp, step, at):
    nc.vector.reciprocal(rstd, rstd).then_inc(step.sem, 1)
    dve.wait_ge(step.sem, at + 1)
    nc.vector.tensor_tensor(tmp, rstd, rstd, ALU.mult).then_inc(step.sem, 1)
    dve.wait_ge(step.sem, at + 2)
    nc.vector.tensor_tensor(tmp, tmp, var, ALU.mult).then_inc(step.sem, 1)
    dve.wait_ge(step.sem, at + 3)
    nc.vector.tensor_scalar(tmp, tmp, -0.5, 1.5, ALU.mult, ALU.add).then_inc(step.sem, 1)
    dve.wait_ge(step.sem, at + 4)
    nc.vector.tensor_tensor(rstd, rstd, tmp, ALU.mult).then_inc(step.sem, 1)
    dve.wait_ge(step.sem, at + 5)
    return at + 5


Q_SCALE = K_SCALE = 16.0
S_SCALE = DH1 ** -0.5 / (Q_SCALE * K_SCALE)


def self_attention(nc, X, C, ident, x_raw, c_raw, qk_parts, x_in, context, ident_in, w_qkv, w_out, b_out, rope):
    PAIRS = H1 // 2
    HP = PAIRS // 2
    with Env(nc, "p1") as env:
        wqkv = env.sb("wqkv", [P, 2, 3 * D])
        wrot = env.sb("wrot", [P, 2, 2 * D])
        wout = env.sb("wout", [P, 2, D])
        bout = env.sb("bout", [P, QT, D])
        cs = env.sb("cs", [P, 2 * S])
        mv = env.sb("mv", [P, TILES, 2])
        var = env.sb("var", [P, TILES])
        rstd = env.sb("rstd", [P, TILES])
        ntmp = env.sb("ntmp", [P, TILES])
        xn = env.sb("xn", [P, QT, D])
        xnT = env.sb("xnT", [P, 2, S])
        rt = env.sb("rt", [P, 2, 2 * S])
        qkf = env.sb("qkf", [P, 2, S])
        parts = env.sb("parts", [P, 2, 2, S], F16)
        qs = env.sb("qs", [96, PAIRS, S], F16)
        ks = env.sb("ks", [96, PAIRS, 2, S], F16)
        v = env.sb("v", [P, QT, H1, 2 * DH1])
        prob = env.sb("prob", [P, 2, QT, 2, S])
        smax = env.sb("smax", [P, 2, QT, 2])
        nmax = env.sb("nmax", [P, 2, QT, 2])
        pT = env.sb("pT", [P, 8, 2, S])
        oT = env.sb("oT", [P, 4, S])
        rinv = env.sb("rinv", [P, 2 * QT * 4])
        warm = env.sb("warm", [P, 2])
        on = env.sb("on", [P, QT, D])
        onT = env.sb("onT", [P, 2, S])
        res = env.sb("res", [P, QT, D])

        ps_s = [env.psum(f"s{i}") for i in range(2)]
        ps_t = [env.psum(f"t{i}") for i in range(2)]
        ps_o = env.psum("o")
        ps_p = [env.psum(f"p{i}") for i in range(2)]
        ps_m = env.psum("m")

        x_loaded, w_loaded, filled = env.sem("x_loaded"), env.sem("w_loaded"), env.sem("filled")
        stats, std_ready, step = env.sem("stats"), env.sem("std_ready"), env.sem("step")
        wrot_ready, c_loaded = env.sem("wrot_ready"), env.sem("c_loaded")
        xn_ready = env.sem("xn_ready")
        xnT_ps = env.sem("xnT_ps")
        xnT_ready = env.sem("xnT_ready")
        qk_ps = env.sem("qk_ps")
        qk_mul = env.sem("qk_mul", 2)
        qk_sum = env.sem("qk_sum", 2)
        hi_ready = env.sem("hi_ready")
        lo_ready = env.sem("lo_ready", 2)
        stored = env.sem("stored", 32)
        q_stacked = env.sem("q_stacked")
        k_stacked = env.sem("k_stacked")
        v_ps = env.sem("v_ps", 1)
        v_ready = env.sem("v_ready", 1)
        s_ps = env.sem("s_ps", 16)
        smax_ready = env.sem("smax_ready")
        nmax_ready = env.sem("nmax_ready")
        exp_done = env.sem("exp_done", 4)
        pT_ps = env.sem("pT_ps", 4)
        pT_act = env.sem("pT_act", 1)
        pT_dve = env.sem("pT_dve", 1)
        o_ps = env.sem("o_ps", 2)
        oT_ready = env.sem("oT_ready", 1)
        o_tok = env.sem("o_tok", 2)
        rinv_ready = env.sem("rinv_ready")
        on_ready = env.sem("on_ready", 3)
        onT_ps = env.sem("onT_ps", 1)
        onT_ready = env.sem("onT_ready")
        out_ps = env.sem("out_ps", 2)
        res_ready = env.sem("res_ready", 1)
        x_done = env.sem("x_done")
        warmed = env.sem("warmed", 1)
        block = env.block()
        W_ALL = 16 * 6
        ROPE_STEP = (1, 2, 5, 6)

        @block.sync
        def _(sp):
            sp.sem_inc(stored.sem, stored.credit)
            xv = x_in.rearrange("b (t p) d -> p (b t) d", p=P)
            for n in range(4):
                sp.dma_start(X[:, 8 * n:8 * n + 8, :], xv[:, 8 * n:8 * n + 8, :]).then_inc(x_loaded.sem, 16)
            sp.dma_start(wqkv[:], w_qkv.rearrange("(k p) n -> p k n", p=P)).then_inc(w_loaded.sem, 16)
            sp.dma_start(cs[:], rope).then_inc(w_loaded.sem, 16)
            sp.dma_start(ident[:], ident_in).then_inc(w_loaded.sem, 16)
            sp.dma_start(wout[:], w_out.rearrange("(k p) n -> p k n", p=P)).then_inc(w_loaded.sem, 16)
            for t in range(QT):
                sp.dma_start(bout[:, t, :], b_out.rearrange("(a n) -> a n", a=1).broadcast_to([P, D])
                             ).then_inc(w_loaded.sem, 16)
            cv = context.rearrange("b (t p) d -> p (b t) d", p=P)
            for n in range(4):
                sp.dma_start(C[:, 8 * n:8 * n + 8, :], cv[:, 8 * n:8 * n + 8, :]).then_inc(c_loaded.sem, 16)
            sp.wait_ge(filled.sem, 3)

            def stack(b, n):
                half = n // 2
                pairs = slice(HP * half, HP * half + HP)
                sp.wait_ge(lo_ready.sem, lo_ready.at(4 * b + n + 1))
                sp.dma_start(qk_parts[n], parts[:, n % 2, :, :]).then_inc(stored.sem, 16)
                sp.wait_ge(stored.sem, stored.at(16 * (4 * b + n + 1)))
                for r in range(3):
                    if n % 2 == 0:
                        src = qk_parts[n, :, (0, 0, 1)[r], :].rearrange("(u a) s -> a u s", u=HP)
                        sp.dma_start(qs[32 * r:32 * r + 32, pairs, :], src).then_inc(q_stacked.sem, 16)
                    else:
                        src = qk_parts[n, :, (0, 1, 0)[r], :].rearrange("(u h j) s -> h j u s", u=HP, h=2)
                        for hh in range(2):
                            row = 32 * r + DH1 * hh
                            sp.dma_start(ks[row:row + DH1, pairs, hh, :], src[hh]).then_inc(k_stacked.sem, 16)

            with sp.Fori(0, B) as b:
                for n in range(4):
                    stack(b, n)

        @block.vector
        def _(dve):
            for c in (qk_mul, pT_dve, on_ready, res_ready):
                dve.sem_inc(c.sem, c.credit)
            nc.vector.memset(warm[:], 0.0).then_inc(filled.sem, 1)
            nc.vector.memset(v[:], 1.0).then_inc(filled.sem, 1)
            nc.vector.memset(ks[:], 0.0).then_inc(filled.sem, 1)
            dve.wait_ge(x_loaded.sem, 64)
            ln_statistics(nc, dve, env, lambda t: X[:, t, :], TILES, mv, stats)
            dve.wait_ge(stats.sem, 2 * TILES)
            nc.vector.tensor_scalar(var[:], mv[:, :, 1], EPS, None, ALU.add).then_inc(stats.sem, 1)
            dve.wait_ge(std_ready.sem, 1)
            refine_rsqrt(nc, dve, rstd[:], var[:], ntmp[:], step, 0)
            dve.wait_ge(w_loaded.sem, W_ALL)
            for half in range(2):
                for k in range(2):
                    src = wqkv[:, k, 0:2 * D].rearrange("p (h j) -> p h j", j=DH1)
                    dst = wrot[:, k, :].rearrange("p (h j) -> p h j", j=DH1)
                    nc.vector.tensor_copy(dst[:, :, 8 * half:8 * half + 8],
                                          src[:, :, 8 - 8 * half:16 - 8 * half]).then_inc(wrot_ready.sem, 1)

            def later_stats(b):
                for t in range(QT):
                    nc.vector.bn_stats(x_raw[:, bass.ds(QT * b + t, 1), :].rearrange("p a s -> p (a s)"),
                                       X[:, bass.ds(QT * b + t, 1), :].rearrange("p a d -> p (a d)"))

            def context_stats(b):
                for t in range(QT):
                    nc.vector.bn_stats(c_raw[:, bass.ds(QT * b + t, 1), :].rearrange("p a s -> p (a s)"),
                                       C[:, bass.ds(QT * b + t, 1), :].rearrange("p a d -> p (a d)"))

            def normalise(b):
                if not isinstance(b, int) or b > 0:
                    dve.wait_ge(xnT_ps.sem, xnT_ps.at(b))
                for t in range(QT):
                    nc.vector.tensor_scalar(xn[:, t, :], X[:, bass.ds(QT * b + t, 1), :].rearrange("p a d -> p (a d)"),
                                            mv[:, bass.ds(QT * b + t, 1), 0:1].rearrange("p a d -> p (a d)"),
                                            rstd[:, bass.ds(QT * b + t, 1)],
                                            ALU.subtract, ALU.mult).then_inc(xn_ready.sem, 1)

            def rope_mul(b, n):
                dve.wait_ge(qk_ps.sem, qk_ps.at(4 * b + n + 1))
                dve.wait_ge(qk_sum.sem, qk_sum.at(4 * b + n - 1))
                nc.vector.tensor_tensor(rt[:, n % 2, :], ps_p[n % 2][:], cs[:], ALU.mult).then_inc(qk_mul.sem, 1)

            def maxima(b, u):
                for qt in range(QT):
                    dve.wait_ge(s_ps.sem, s_ps.at(16 * b + 2 * u + qt + 1))
                    nc.vector.tensor_reduce(smax[:, u % 2, qt, :], ps_s[qt][:].rearrange("p (h k) -> p h k", h=2),
                                            AX, ALU.max).then_inc(smax_ready.sem, 1)
                    dve.wait_ge(smax_ready.sem, smax_ready.at(16 * b + 2 * u + qt + 1))
                    nc.vector.tensor_scalar(nmax[:, u % 2, qt, :], smax[:, u % 2, qt, :], -S_SCALE, None, ALU.mult
                                            ).then_inc(nmax_ready.sem, 1)

            def evacuate_pT(b, u):
                h = 2 * u + 1
                dve.wait_ge(pT_ps.sem, pT_ps.at(16 * b + h + 1))
                dve.wait_ge(o_ps.sem, o_ps.at(4 * b + h // 4 - 1))
                nc.vector.tensor_copy(pT[:, h % 8, :, :], ps_t[1][:].rearrange("p (k q) -> p k q", k=2)
                                      ).then_inc(pT_dve.sem, 1)

            def over_sums(b, a):
                dve.wait_ge(o_tok.sem, o_tok.at(2 * b + a + 1))
                blocks = ps_m[:].rearrange("p (r c) -> p r c", c=2 * DH1)
                nc.vector.reciprocal(rinv[:], blocks[:, :, DH1]).then_inc(rinv_ready.sem, 1)
                dve.wait_ge(rinv_ready.sem, rinv_ready.at(2 * b + a + 1))
                dve.wait_ge(onT_ps.sem, onT_ps.at(b))
                for g in range(2):
                    rows = slice(QT * 4 * g, QT * 4 * (g + 1))
                    cols = slice((2 * a + g) * 4 * DH1, (2 * a + g + 1) * 4 * DH1)
                    ins = nc.vector.tensor_tensor(
                        on[:, :, cols].rearrange("p t (h j) -> p t h j", j=DH1),
                        blocks[:, rows, 0:DH1].rearrange("p (t h) j -> p t h j", t=QT),
                        rinv[:, rows].rearrange("p (t h) -> p t h", t=QT).unsqueeze(3).broadcast_to([P, QT, 4, DH1]),
                        ALU.mult)
                ins.then_inc(on_ready.sem, 1)

            def finish(b):
                dve.wait_ge(out_ps.sem, out_ps.at(b + 1))
                nc.vector.tensor_tensor(res[:], ps_m[:].rearrange("p (t d) -> p t d", t=QT), bout[:], ALU.add
                                        ).then_inc(res_ready.sem, 1)
                dve.wait_ge(res_ready.sem, res_ready.at(b + 1))
                nc.vector.tensor_tensor(X[:, bass.ds(QT * b, QT), :], X[:, bass.ds(QT * b, QT), :], res[:],
                                        ALU.add).then_inc(x_done.sem, 1)

            def body(b, before, more, ahead):
                for u in range(PAIRS):
                    maxima(b, u)
                    if u >= 1:
                        evacuate_pT(b, u - 1)
                    elif before:
                        evacuate_pT(b - 1, PAIRS - 1)
                    if before and u == 2:
                        over_sums(b - 1, 1)
                    if before and u == 4:
                        finish(b - 1)
                    if more and u in ROPE_STEP:
                        rope_mul(b + 1, ROPE_STEP.index(u))
                    if u == 0:
                        context_stats(b)
                    if u == 3 and ahead:
                        normalise(b + 2)
                    if u == 6:
                        over_sums(b, 0)
                    if before and u == 7:
                        dve.wait_ge(x_done.sem, x_done.at(b))
                        later_stats(b - 1)

            normalise(0)
            for n in range(4):
                rope_mul(0, n)
            normalise(1)
            dve.wait_ge(c_loaded.sem, 64)
            body(0, False, True, True)
            with dve.Fori(1, B - 2) as b:
                body(b, True, True, True)
            body(B - 2, True, True, False)
            body(B - 1, True, False, False)
            evacuate_pT(B - 1, PAIRS - 1)
            over_sums(B - 1, 1)
            finish(B - 1)
            dve.wait_ge(x_done.sem, x_done.at(B))
            later_stats(B - 1)

        @block.gpsimd
        def _(pool):
            for c in (qk_sum, lo_ready):
                pool.sem_inc(c.sem, c.credit)

            def rope_add(b, n):
                pool.wait_ge(qk_mul.sem, qk_mul.at(4 * b + n + 1))
                pool.wait_ge(lo_ready.sem, lo_ready.at(4 * b + n - 1))
                nc.gpsimd.tensor_tensor(qkf[:, n % 2, :], rt[:, n % 2, 0:S], rt[:, n % 2, S:2 * S], ALU.add
                                        ).then_inc(qk_sum.sem, 1)
                pool.wait_ge(s_ps.sem, s_ps.at(16 * (b - 1) + 8 * (n // 2) + 8))
                pool.wait_ge(hi_ready.sem, hi_ready.at(4 * b + n + 1))
                nc.gpsimd.tensor_tensor(parts[:, n % 2, 1, :], qkf[:, n % 2, :], parts[:, n % 2, 0, :], ALU.subtract
                                        ).then_inc(lo_ready.sem, 1)

            with pool.Fori(0, B) as b:
                for n in range(4):
                    rope_add(b, n)

        @block.scalar
        def _(act):
            for c in (v_ready, exp_done, pT_act, oT_ready, warmed):
                act.sem_inc(c.sem, c.credit)
            act.wait_ge(stats.sem, 2 * TILES + 1)
            nc.scalar.activation(rstd[:], var[:], ACT.Sqrt).then_inc(std_ready.sem, 1)
            act.wait_ge(filled.sem, 2)

            def evacuate_xnT(b):
                act.wait_ge(xnT_ps.sem, xnT_ps.at(b + 1))
                act.wait_ge(v_ps.sem, v_ps.at(b))
                nc.scalar.activation(xnT[:], ps_m[:].rearrange("p (k s) -> p k s", k=2), ACT.Copy
                                     ).then_inc(xnT_ready.sem, 1)

            def high_part(b, n):
                act.wait_ge(qk_sum.sem, qk_sum.at(4 * b + n + 1))
                act.wait_ge(stored.sem, stored.at(16 * (4 * b + n - 1)))
                nc.scalar.activation(parts[:, n % 2, 0, :], qkf[:, n % 2, :], ACT.Copy).then_inc(hi_ready.sem, 1)

            def evacuate_v(b):
                act.wait_ge(v_ps.sem, v_ps.at(b + 1))
                act.wait_ge(o_ps.sem, o_ps.at(4 * b))
                for t in range(QT):
                    ins = nc.scalar.activation(v[:, t, :, 0:DH1],
                                               ps_p[1][:, t * D:(t + 1) * D].rearrange("p (h j) -> p h j", h=H1), ACT.Copy)
                ins.then_inc(v_ready.sem, 1)

            def exponentials(b, u):
                for qt in range(QT):
                    act.wait_ge(nmax_ready.sem, nmax_ready.at(16 * b + 2 * u + qt + 1))
                    act.wait_ge(pT_ps.sem, pT_ps.at(16 * b + 2 * u - 2))
                    for hh in range(2):
                        nc.scalar.activation(prob[:, u % 2, qt, hh, :], ps_s[qt][:, hh * S:(hh + 1) * S], ACT.Exp,
                                             scale=S_SCALE, bias=nmax[:, u % 2, qt, hh:hh + 1]
                                             ).then_inc(exp_done.sem, 1)

            def evacuate_pT(b, u):
                h = 2 * u
                act.wait_ge(pT_ps.sem, pT_ps.at(16 * b + h + 1))
                act.wait_ge(o_ps.sem, o_ps.at(4 * b + h // 4 - 1))
                nc.scalar.activation(pT[:, h % 8, :, :], ps_t[0][:].rearrange("p (k q) -> p k q", k=2),
                                     ACT.Copy).then_inc(pT_act.sem, 1)

            def evacuate_o(b, g):
                act.wait_ge(o_ps.sem, o_ps.at(4 * b + g + 1))
                act.wait_ge(o_tok.sem, o_tok.at(2 * (b - 1) + g // 2 + 1))
                nc.scalar.activation(oT[:, g, :], ps_o[:, 0:S], ACT.Copy).then_inc(oT_ready.sem, 1)

            def evacuate_onT(b):
                act.wait_ge(onT_ps.sem, onT_ps.at(b + 1))
                act.wait_ge(out_ps.sem, out_ps.at(b))
                nc.scalar.activation(onT[:], ps_m[:].rearrange("p (k s) -> p k s", k=2), ACT.Copy
                                     ).then_inc(onT_ready.sem, 1)

            def load_table(b):
                act.wait_ge(warmed.sem, warmed.at(b))
                nc.scalar.activation(warm[:, 1:2], warm[:, 0:1], ACT.Exp).then_inc(warmed.sem, 1)

            def body(b, before, more):
                load_table(b)
                for u in range(PAIRS):
                    exponentials(b, u)
                    if u >= 1:
                        evacuate_pT(b, u - 1)
                    elif before:
                        evacuate_pT(b - 1, PAIRS - 1)
                    if more and u == 0:
                        evacuate_xnT(b + 1)
                    if before and u == 1:
                        evacuate_o(b - 1, 3)
                    if u == 1:
                        evacuate_v(b)
                    if before and u == 3:
                        evacuate_onT(b - 1)
                    if u in (3, 5, 7):
                        evacuate_o(b, u // 2 - 1)
                    if more and u - 1 in ROPE_STEP:
                        high_part(b + 1, ROPE_STEP.index(u - 1))

            evacuate_xnT(0)
            for n in range(4):
                high_part(0, n)
            body(0, False, True)
            with act.Fori(1, B - 1) as b:
                body(b, True, True)
            body(B - 1, True, False)
            evacuate_pT(B - 1, PAIRS - 1)
            evacuate_o(B - 1, 3)
            evacuate_onT(B - 1)

        @block.tensor
        def _(pe):
            for c in (v_ps, s_ps, pT_ps, o_ps, o_tok, onT_ps, out_ps):
                pe.sem_inc(c.sem, c.credit)
            pe.wait_ge(w_loaded.sem, W_ALL)

            def transpose_xn(b):
                pe.wait_ge(xn_ready.sem, xn_ready.at(2 * b + 2))
                pe.wait_ge(on_ready.sem, on_ready.at(2 * b - 3))
                for t in range(QT):
                    for k in range(2):
                        ins = pe.transpose(ps_m[:, k * S + t * P:k * S + (t + 1) * P], xn[:, t, k * P:(k + 1) * P],
                                           ident[:])
                ins.then_inc(xnT_ps.sem, 1)

            def project_qk(b, n):
                pe.wait_ge(qk_mul.sem, qk_mul.at(4 * b + n - 1))
                if n == 0:
                    pe.wait_ge(xnT_ready.sem, xnT_ready.at(b + 1))
                if n == 1:
                    pe.wait_ge(v_ready.sem, v_ready.at(b))
                col = (n % 2) * D + (n // 2) * P
                for j, w in enumerate((wqkv, wrot)):
                    for k in range(2):
                        ins = pe.matmul(ps_p[n % 2][:, j * S:(j + 1) * S], w[:, k, col:col + P], xnT[:, k, :],
                                        start=(k == 0), stop=(k == 1), skip_group_check=True)
                ins.then_inc(qk_ps.sem, 1)

            def project_v(b):
                pe.wait_ge(qk_mul.sem, qk_mul.at(4 * b + 4))
                for t in range(QT):
                    for k in range(2):
                        ins = pe.matmul(ps_p[1][:, t * D:(t + 1) * D], xnT[:, k, t * P:(t + 1) * P],
                                        wqkv[:, k, 2 * D:3 * D], start=(k == 0), stop=(k == 1), skip_group_check=True)
                ins.then_inc(v_ps.sem, 1)

            def scores(b, u):
                half = u // HP
                if u % HP == 0:
                    pe.wait_ge(q_stacked.sem, q_stacked.at(48 * (2 * b + half + 1)))
                    pe.wait_ge(k_stacked.sem, k_stacked.at(96 * (2 * b + half + 1)))
                for qt in range(QT):
                    pe.wait_ge(exp_done.sem, exp_done.at(32 * b + 4 * u + 2 * qt - 2))
                    pe.matmul(ps_s[qt][:], qs[:, u, qt * P:(qt + 1) * P],
                              ks[:, u, :, :].rearrange("p h k -> p (h k)"), start=True, stop=True
                              ).then_inc(s_ps.sem, 1)

            def transpose_p(b, u):
                pe.wait_ge(exp_done.sem, exp_done.at(32 * b + 4 * u + 4))
                for hh in range(2):
                    read = pT_dve if hh else pT_act
                    pe.wait_ge(read.sem, read.at(8 * b + u))
                    for kt in range(2):
                        for qt in range(QT):
                            ins = pe.transpose(ps_t[hh][:, kt * S + qt * P:kt * S + (qt + 1) * P],
                                               prob[:, u % 2, qt, hh, kt * P:(kt + 1) * P], ident[:])
                    ins.then_inc(pT_ps.sem, 1)

            def values(b, g):
                if g == 0:
                    pe.wait_ge(v_ready.sem, v_ready.at(b + 1))
                pe.wait_ge(pT_act.sem, pT_act.at(8 * b + 2 * g + 2))
                pe.wait_ge(pT_dve.sem, pT_dve.at(8 * b + 2 * g + 2))
                pe.wait_ge(oT_ready.sem, oT_ready.at(4 * b + g))
                for kt in range(2):
                    for j in range(4):
                        h = 4 * g + j
                        ins = pe.matmul(ps_o[32 * j:32 * j + 32, 0:S], v[:, kt, h, :], pT[:, h % 8, kt, :],
                                        start=(kt == 0), stop=(kt == 1), skip_group_check=True)
                ins.then_inc(o_ps.sem, 1)

            def outputs_to_tokens(b, a):
                pe.wait_ge(oT_ready.sem, oT_ready.at(4 * b + 2 * a + 2))
                if a:
                    pe.wait_ge(xnT_ready.sem, xnT_ready.at(min(b + 3, B) if isinstance(b, int) else b + 3))
                else:
                    pe.wait_ge(res_ready.sem, res_ready.at(b))
                for g in range(2):
                    for t in range(QT):
                        r = QT * g + t
                        ins = pe.transpose(ps_m[:, r * P:(r + 1) * P], oT[:, 2 * a + g, t * P:(t + 1) * P], ident[:])
                ins.then_inc(o_tok.sem, 1)

            def transpose_on(b):
                pe.wait_ge(on_ready.sem, on_ready.at(2 * b + 2))
                for t in range(QT):
                    for k in range(2):
                        ins = pe.transpose(ps_m[:, k * S + t * P:k * S + (t + 1) * P], on[:, t, k * P:(k + 1) * P],
                                           ident[:])
                ins.then_inc(onT_ps.sem, 1)

            def project_out(b):
                pe.wait_ge(onT_ready.sem, onT_ready.at(b + 1))
                for t in range(QT):
                    for k in range(2):
                        ins = pe.matmul(ps_m[:, t * D:(t + 1) * D], onT[:, k, t * P:(t + 1) * P], wout[:, k, :],
                                        start=(k == 0), stop=(k == 1), skip_group_check=True)
                ins.then_inc(out_ps.sem, 1)

            def body(b, before, more):
                for u in range(PAIRS):
                    scores(b, u)
                    if u >= 1:
                        transpose_p(b, u - 1)
                    elif before:
                        transpose_p(b - 1, PAIRS - 1)
                    if u == 0:
                        project_v(b)
                    if more and u == 0:
                        transpose_xn(b + 1)
                    if before and u == 1:
                        values(b - 1, 3)
                    if before and u == 2:
                        outputs_to_tokens(b - 1, 1)
                    if before and u == 3:
                        transpose_on(b - 1)
                    if before and u == 4:
                        project_out(b - 1)
                    if u in (3, 5, 7):
                        values(b, u // 2 - 1)
                    if more and u in ROPE_STEP:
                        project_qk(b + 1, ROPE_STEP.index(u))
                    if u == 6:
                        outputs_to_tokens(b, 0)

            transpose_xn(0)
            pe.wait_ge(wrot_ready.sem, 4)
            for n in range(4):
                project_qk(0, n)
            body(0, False, True)
            with pe.Fori(1, B - 1) as b:
                body(b, True, True)
            body(B - 1, True, False)
            transpose_p(B - 1, PAIRS - 1)
            values(B - 1, 3)
            outputs_to_tokens(B - 1, 1)
            transpose_on(B - 1)
            project_out(B - 1)


def cross_attention(nc, X, C, ident, x_raw, c_raw, media_w, media_b, lat_w, lat_b, Wq, Wk, Wv, Wout):
    PAIRS = H2 // 2
    KT = KV // P
    with Env(nc, "p2") as env:
        wq = env.sb("wq", [P, 2, INNER])
        wk = env.sb("wk", [P, 2, INNER])
        wv = env.sb("wv", [P, 2, INNER])
        wout = env.sb("wout", [P, PAIRS, D])
        affine = env.sb("affine", [P, 2, 2, 2])
        mv = env.sb("mv", [P, 2, TILES, 2])
        var = env.sb("var", [P, 2 * TILES])
        rstd = env.sb("rstd", [P, 2 * TILES])
        var2 = env.sb("var2", [P, TILES])
        rstd2 = env.sb("rstd2", [P, TILES])
        ntmp = env.sb("ntmp", [P, 2 * TILES])
        xn = env.sb("xn", [P, 2, QT, D])
        kvT = env.sb("kvT", [P, 2, KV])
        qT = env.sb("qT", [P, PAIRS, S])
        km = env.sb("km", [P, PAIRS, 2, KV])
        v = env.sb("v", [P, KT, INNER])
        prob = env.sb("prob", [P, 2, QT, KV])
        nmax = env.sb("nmax", [P, 2, QT])
        rsum = env.sb("rsum", [P, 2, QT])
        rinv = env.sb("rinv", [P, 2, QT])
        pT = env.sb("pT", [P, 4, KT, S])
        oT = env.sb("oT", [P, PAIRS, S])

        ps_s = [env.psum(f"s{i}") for i in range(2)]
        ps_t = [env.psum(f"t{i}") for i in range(2)]
        ps_o = env.psum("o")
        ps_p = [env.psum(f"p{i}") for i in range(2)]
        ps_m = env.psum("m")

        loaded, zeroed = env.sem("loaded"), env.sem("zeroed")
        stats, std_ready, step = env.sem("stats"), env.sem("std_ready"), env.sem("step")
        xn_ready = env.sem("xn_ready")
        xnT_ps = env.sem("xnT_ps")
        kvT_ready = env.sem("kvT_ready", 2)
        q_ps = env.sem("q_ps")
        q_ready = env.sem("q_ready", 1)
        k_ps = env.sem("k_ps")
        k_ready = env.sem("k_ready", 2)
        v_ps = env.sem("v_ps", 4)
        v_act = env.sem("v_act", 1)
        v_dve = env.sem("v_dve", 1)
        s_ps = env.sem("s_ps", 16)
        nmax_ready = env.sem("nmax_ready")
        exp_done = env.sem("exp_done", 2)
        inv_ready = env.sem("inv_ready")
        prob_ready = env.sem("prob_ready")
        pT_ps = env.sem("pT_ps", 4)
        pT_act = env.sem("pT_act", 1)
        pT_dve = env.sem("pT_dve", 1)
        o_ps = env.sem("o_ps", 2)
        oT_ready = env.sem("oT_ready", 1)
        out_ps = env.sem("out_ps", 1)
        x_done = env.sem("x_done", 1)
        block = env.block()
        LOADS = 16 * 12

        @block.sync
        def _(sp):
            for w, src in ((wq, Wq), (wk, Wk), (wv, Wv), (wout, Wout)):
                sp.dma_start(w[:], src.rearrange("(k p) n -> p k n", p=P)).then_inc(loaded.sem, 16)
            for n, src in enumerate((media_w, media_b, lat_w, lat_b)):
                for k in range(2):
                    sp.dma_start(affine[:, n // 2, n % 2, k:k + 1],
                                 src[k * P:(k + 1) * P].rearrange("(p a) -> p a", a=1)).then_inc(loaded.sem, 16)

        @block.vector
        def _(dve):
            for c in (v_dve, pT_dve, x_done, k_ready):
                dve.sem_inc(c.sem, c.credit)
            nc.vector.memset(km[:], 0.0).then_inc(zeroed.sem, 1)
            for a, raw in enumerate((c_raw, x_raw)):
                for t in range(TILES):
                    nc.vector.bn_aggr(mv[:, a, t, :], raw[:, t, :]).then_inc(stats.sem, 1)
            dve.wait_ge(stats.sem, 2 * TILES)
            nc.vector.tensor_scalar(var[:], mv[:].rearrange("p a t s -> p (a t) s")[:, :, 1], EPS, None, ALU.add
                                    ).then_inc(stats.sem, 1)
            dve.wait_ge(std_ready.sem, 1)
            refine_rsqrt(nc, dve, rstd[:], var[:], ntmp[:], step, 0)
            nc.vector.tensor_tensor(var2[:], rstd[:, TILES:], rstd[:, TILES:], ALU.mult).then_inc(step.sem, 1)
            dve.wait_ge(step.sem, 6)
            nc.vector.tensor_tensor(var2[:], var2[:], mv[:, 1, :, 1], ALU.mult).then_inc(step.sem, 1)
            dve.wait_ge(step.sem, 7)
            nc.vector.tensor_scalar(var2[:], var2[:], EPS, None, ALU.add).then_inc(step.sem, 1)
            dve.wait_ge(std_ready.sem, 2)
            refine_rsqrt(nc, dve, rstd2[:], var2[:], ntmp[:, 0:TILES], step, 8)
            nc.vector.tensor_tensor(rstd[:, TILES:], rstd[:, TILES:], rstd2[:], ALU.mult).then_inc(step.sem, 1)
            dve.wait_ge(step.sem, 14)

            def normalise(b):
                for a, src in enumerate((C, X)):
                    for t in range(QT):
                        nc.vector.tensor_scalar(
                            xn[:, a, t, :], src[:, bass.ds(QT * b + t, 1), :].rearrange("p a d -> p (a d)"),
                            mv[:, a, bass.ds(QT * b + t, 1), 0:1].rearrange("p a d -> p (a d)"),
                            rstd[:, bass.ds(TILES * a + QT * b + t, 1)],
                            ALU.subtract, ALU.mult).then_inc(xn_ready.sem, 1)

            def spread_k(b, j):
                dve.wait_ge(k_ps.sem, k_ps.at(4 * b + j + 1))
                dve.wait_ge(s_ps.sem, s_ps.at(16 * (b - 1) + 4 * j + 4))
                for hh in range(2):
                    r = slice(DH2 * hh, DH2 * hh + DH2)
                    nc.vector.tensor_copy(km[r, j, hh, :], ps_p[1][r, :]).then_inc(k_ready.sem, 1)

            def evacuate_v(b, t):
                dve.wait_ge(v_ps.sem, v_ps.at(4 * b + t + 1))
                dve.wait_ge(o_ps.sem, o_ps.at(4 * b))
                nc.vector.tensor_copy(v[:, t, :], ps_p[1][:]).then_inc(v_dve.sem, 1)

            def maxima(b, h):
                for qt in range(QT):
                    dve.wait_ge(s_ps.sem, s_ps.at(16 * b + 2 * h + qt + 1))
                    nc.vector.tensor_reduce(nmax[:, h % 2, qt:qt + 1], ps_s[qt][:], AX, ALU.max, negate=True
                                            ).then_inc(nmax_ready.sem, 1)

            def divide(b, h):
                for qt in range(QT):
                    dve.wait_ge(exp_done.sem, exp_done.at(16 * b + 2 * h + qt + 1))
                    nc.vector.reciprocal(rinv[:, h % 2, qt:qt + 1], rsum[:, h % 2, qt:qt + 1]).then_inc(inv_ready.sem, 1)
                for qt in range(QT):
                    dve.wait_ge(inv_ready.sem, inv_ready.at(16 * b + 2 * h + qt + 1))
                    nc.vector.tensor_scalar(prob[:, h % 2, qt, :], prob[:, h % 2, qt, :], rinv[:, h % 2, qt:qt + 1],
                                            None, ALU.mult).then_inc(prob_ready.sem, 1)

            def evacuate_pT(b, h):
                dve.wait_ge(pT_ps.sem, pT_ps.at(16 * b + 2 * h + 2))
                dve.wait_ge(o_ps.sem, o_ps.at(4 * b + h // 2 - 1))
                nc.vector.tensor_copy(pT[:, h % 4, 2:4, :], ps_t[1][:].rearrange("p (k q) -> p k q", k=2)
                                      ).then_inc(pT_dve.sem, 1)

            def later_stats(b):
                for t in range(QT):
                    nc.vector.bn_stats(x_raw[:, bass.ds(QT * b + t, 1), :].rearrange("p a s -> p (a s)"),
                                       X[:, bass.ds(QT * b + t, 1), :].rearrange("p a d -> p (a d)"))

            def finish(b):
                dve.wait_ge(out_ps.sem, out_ps.at(b + 1))
                nc.vector.tensor_tensor(X[:, bass.ds(QT * b, QT), :], X[:, bass.ds(QT * b, QT), :],
                                        ps_m[:].rearrange("p (t d) -> p t d", t=QT), ALU.add).then_inc(x_done.sem, 1)

            def body(b, before, more):
                for u in range(10):
                    if 1 <= u <= 8:
                        divide(b, u - 1)
                    if u >= 2:
                        evacuate_pT(b, u - 2)
                    if u < 8:
                        maxima(b, u)
                    if before and u == 1:
                        finish(b - 1)
                    if u == 0:
                        evacuate_v(b, 1)
                    if u == 1:
                        evacuate_v(b, 3)
                    if more and u in (5, 6, 7, 9):
                        spread_k(b + 1, (5, 6, 7, 9).index(u))
                if before:
                    dve.wait_ge(x_done.sem, x_done.at(b))
                    later_stats(b - 1)

            normalise(0)
            for j in range(PAIRS):
                spread_k(0, j)
            normalise(1)
            body(0, False, True)
            normalise(2)
            with dve.Fori(1, B - 2) as b:
                body(b, True, True)
                normalise(b + 2)
            body(B - 2, True, True)
            body(B - 1, True, False)
            finish(B - 1)
            dve.wait_ge(x_done.sem, x_done.at(B))
            later_stats(B - 1)

        @block.scalar
        def _(act):
            for c in (kvT_ready, q_ready, v_act, exp_done, pT_act, oT_ready):
                act.sem_inc(c.sem, c.credit)
            act.wait_ge(stats.sem, 2 * TILES + 1)
            nc.scalar.activation(rstd[:], var[:], ACT.Sqrt).then_inc(std_ready.sem, 1)
            act.wait_ge(step.sem, 8)
            nc.scalar.activation(rstd2[:], var2[:], ACT.Sqrt).then_inc(std_ready.sem, 1)
            act.wait_ge(loaded.sem, LOADS)

            def evacuate_kvT(b, a):
                act.wait_ge(xnT_ps.sem, xnT_ps.at(2 * b + a + 1))
                act.wait_ge(v_ps.sem, v_ps.at(4 * b))
                for k in range(2):
                    nc.scalar.activation(kvT[:, k, a * S:(a + 1) * S], ps_m[:, k * S:(k + 1) * S], ACT.Identity,
                                         scale=affine[:, a, 0, k:k + 1], bias=affine[:, a, 1, k:k + 1]
                                         ).then_inc(kvT_ready.sem, 1)

            def evacuate_q(b, j):
                act.wait_ge(q_ps.sem, q_ps.at(4 * b + j + 1))
                act.wait_ge(s_ps.sem, s_ps.at(16 * (b - 1) + 4 * j + 4))
                nc.scalar.activation(qT[:, j, :], ps_p[0][:, 0:S], ACT.Copy, scale=DH2 ** -0.5).then_inc(q_ready.sem, 1)

            def evacuate_v(b, t):
                act.wait_ge(v_ps.sem, v_ps.at(4 * b + t + 1))
                act.wait_ge(o_ps.sem, o_ps.at(4 * b))
                nc.scalar.activation(v[:, t, :], ps_p[0][:], ACT.Copy).then_inc(v_act.sem, 1)

            def exponentials(b, h):
                for qt in range(QT):
                    act.wait_ge(nmax_ready.sem, nmax_ready.at(16 * b + 2 * h + qt + 1))
                    act.wait_ge(pT_ps.sem, pT_ps.at(16 * b + 2 * h - 2))
                    nc.scalar.activation(prob[:, h % 2, qt, :], ps_s[qt][:], ACT.Exp, bias=nmax[:, h % 2, qt:qt + 1],
                                         accum_out=rsum[:, h % 2, qt:qt + 1]).then_inc(exp_done.sem, 1)

            def evacuate_pT(b, h):
                act.wait_ge(pT_ps.sem, pT_ps.at(16 * b + 2 * h + 1))
                act.wait_ge(o_ps.sem, o_ps.at(4 * b + h // 2 - 1))
                nc.scalar.activation(pT[:, h % 4, 0:2, :], ps_t[0][:].rearrange("p (k q) -> p k q", k=2),
                                     ACT.Copy).then_inc(pT_act.sem, 1)

            def evacuate_o(b, j):
                act.wait_ge(o_ps.sem, o_ps.at(4 * b + j + 1))
                act.wait_ge(out_ps.sem, out_ps.at(b))
                nc.scalar.activation(oT[:, j, :], ps_o[:, 0:S], ACT.Copy).then_inc(oT_ready.sem, 1)

            def body(b, more):
                for u in range(10):
                    if u >= 2:
                        evacuate_pT(b, u - 2)
                    if u in (4, 6, 8):
                        evacuate_o(b, u // 2 - 2)
                    if u < 8:
                        exponentials(b, u)
                    if u < 2:
                        evacuate_v(b, 2 * u)
                    if more and u in (2, 3):
                        evacuate_kvT(b + 1, u - 2)
                    if more and u in (4, 5, 6, 8):
                        evacuate_q(b + 1, (4, 5, 6, 8).index(u))
                evacuate_o(b, 3)

            evacuate_kvT(0, 0)
            evacuate_kvT(0, 1)
            for j in range(PAIRS):
                evacuate_q(0, j)
            with act.Fori(0, B - 1) as b:
                body(b, True)
            body(B - 1, False)

        @block.tensor
        def _(pe):
            for c in (v_ps, s_ps, pT_ps, o_ps, out_ps):
                pe.sem_inc(c.sem, c.credit)
            pe.wait_ge(loaded.sem, LOADS)

            def transpose_xn(b, a):
                pe.wait_ge(xn_ready.sem, xn_ready.at(4 * b + 2 * a + 2))
                pe.wait_ge(x_done.sem, x_done.at(b - 1))
                pe.wait_ge(kvT_ready.sem, kvT_ready.at(4 * b + 2 * a))
                for t in range(QT):
                    for k in range(2):
                        ins = pe.transpose(ps_m[:, k * S + t * P:k * S + (t + 1) * P], xn[:, a, t, k * P:(k + 1) * P],
                                           ident[:])
                ins.then_inc(xnT_ps.sem, 1)

            def project_qk(b, j):
                pe.wait_ge(kvT_ready.sem, kvT_ready.at(4 * b + 4))
                pe.wait_ge(q_ready.sem, q_ready.at(4 * b + j))
                pe.wait_ge(v_act.sem, v_act.at(2 * b))
                for k in range(2):
                    ins = pe.matmul(ps_p[0][:, 0:S], wq[:, k, j * P:(j + 1) * P], kvT[:, k, S:KV],
                                    start=(k == 0), stop=(k == 1))
                ins.then_inc(q_ps.sem, 1)
                pe.wait_ge(k_ready.sem, k_ready.at(8 * b + 2 * j))
                pe.wait_ge(v_dve.sem, v_dve.at(2 * b))
                for k in range(2):
                    ins = pe.matmul(ps_p[1][:], wk[:, k, j * P:(j + 1) * P], kvT[:, k, :], start=(k == 0), stop=(k == 1))
                ins.then_inc(k_ps.sem, 1)

            def project_v(b, tiles):
                for t in tiles:
                    if t < 2:
                        last = k_ready if t else q_ready
                        pe.wait_ge(last.sem, last.at((8 if t else 4) * (b + 1)))
                    else:
                        read = v_dve if t % 2 else v_act
                        pe.wait_ge(read.sem, read.at(2 * b + 1))
                    for k in range(2):
                        ins = pe.matmul(ps_p[t % 2][:], kvT[:, k, t * P:(t + 1) * P], wv[:, k, :],
                                        start=(k == 0), stop=(k == 1))
                    ins.then_inc(v_ps.sem, 1)

            def scores(b, h):
                j = h // 2
                if h % 2 == 0:
                    pe.wait_ge(q_ready.sem, q_ready.at(4 * b + j + 1))
                    pe.wait_ge(k_ready.sem, k_ready.at(8 * b + 2 * j + 2))
                for qt in range(QT):
                    pe.wait_ge(exp_done.sem, exp_done.at(16 * b + 2 * h + qt - 1))
                    pe.matmul(ps_s[qt][:], qT[:, j, qt * P:(qt + 1) * P], km[:, j, h % 2, :], start=True, stop=True
                              ).then_inc(s_ps.sem, 1)

            def transpose_p(b, h):
                pe.wait_ge(prob_ready.sem, prob_ready.at(16 * b + 2 * h + 2))
                for kk in range(2):
                    read = pT_dve if kk else pT_act
                    pe.wait_ge(read.sem, read.at(8 * b + h))
                    for k in range(2):
                        for qt in range(QT):
                            kt = 2 * kk + k
                            ins = pe.transpose(ps_t[kk][:, k * S + qt * P:k * S + (qt + 1) * P],
                                               prob[:, h % 2, qt, kt * P:(kt + 1) * P], ident[:])
                    ins.then_inc(pT_ps.sem, 1)

            def values(b, j):
                if j == 0:
                    pe.wait_ge(v_act.sem, v_act.at(2 * b + 2))
                    pe.wait_ge(v_dve.sem, v_dve.at(2 * b + 2))
                pe.wait_ge(pT_act.sem, pT_act.at(8 * b + 2 * j + 2))
                pe.wait_ge(pT_dve.sem, pT_dve.at(8 * b + 2 * j + 2))
                pe.wait_ge(oT_ready.sem, oT_ready.at(4 * b + j))
                for kt in range(KT):
                    for hh in range(2):
                        h = 2 * j + hh
                        ins = pe.matmul(ps_o[DH2 * hh:DH2 * hh + DH2, 0:S], v[:, kt, h * DH2:(h + 1) * DH2],
                                        pT[:, h % 4, kt, :], start=(kt == 0), stop=(kt == KT - 1), skip_group_check=True)
                ins.then_inc(o_ps.sem, 1)

            def project_out(b):
                pe.wait_ge(oT_ready.sem, oT_ready.at(4 * b + 4))
                pe.wait_ge(kvT_ready.sem, kvT_ready.at(min(4 * b + 8, 4 * B) if isinstance(b, int) else 4 * b + 8))
                for t in range(QT):
                    for j in range(PAIRS):
                        ins = pe.matmul(ps_m[:, t * D:(t + 1) * D], oT[:, j, t * P:(t + 1) * P], wout[:, j, :],
                                        start=(j == 0), stop=(j == PAIRS - 1), skip_group_check=True)
                ins.then_inc(out_ps.sem, 1)

            def body(b, before, more):
                for u in range(8):
                    scores(b, u)
                    if u < 2:
                        project_v(b, (2 * u, 2 * u + 1))
                    if before and u == 0:
                        project_out(b - 1)
                    if more and u in (4, 5, 6):
                        project_qk(b + 1, u - 4)
                    if u >= 1:
                        transpose_p(b, u - 1)
                    if more and u in (2, 3):
                        transpose_xn(b + 1, u - 2)
                    if u in (3, 5, 7):
                        values(b, u // 2 - 1)
                if more:
                    project_qk(b + 1, 3)
                transpose_p(b, 7)
                values(b, 3)

            transpose_xn(0, 0)
            transpose_xn(0, 1)
            for j in range(PAIRS):
                project_qk(0, j)
            body(0, False, True)
            with pe.Fori(1, B - 1) as b:
                body(b, True, True)
            body(B - 1, True, False)
            project_out(B - 1)


H_SCALE, W_SCALE = 16.0, 256.0


def ffn(nc, X, ident, x_raw, h_parts, gates_t, Wm, bm, expert_emb, rank, W1, b1, W2, b2, Wo, bo, fold_in, out):
    G4 = E // 4
    K1 = 3 * HD
    GROUPS = HF * G4
    HIDDEN = HF * E
    G = CT_ * HF
    with Env(nc, "p3") as env:
        wm = env.sb("wm", [P, 2, D])
        bias = env.sb("bias", [P, 2])
        bias_s = env.sb("bias_s", [P, 2])
        emb = env.sb("emb", [P, 4 * E])
        rk = env.sb("rk", [P, E])
        mv = env.sb("mv", [P, TILES, 2])
        var = env.sb("var", [P, TILES])
        rstd = env.sb("rstd", [P, TILES])
        ntmp = env.sb("ntmp", [P, TILES])
        xn = env.sb("xn", [P, CT_, D])
        xnT = env.sb("xnT", [P, 2, CH])
        hf = env.sb("hf", [P, 2, CH])
        hs = env.sb("hs", [P, 2, CH])
        hi = env.sb("hi", [P, 2, CH], F16)
        lo = env.sb("lo", [P, 2, CH], F16)
        w = env.sb("w", [P, G, E])
        w_rest = env.sb("w_rest", [P, G, E])
        top = env.sb("top", [P, G])
        eq = env.sb("eq", [P, G, E])
        hot = env.sb("hot", [P, 2, G, E])
        den = env.sb("den", [P, G])
        gates = env.sb("gates", [P, CT_, HF * E])
        gT = env.sb("gT", [P, CH])

        w1h = env.sb("w1h", [K1, E, I], F16)
        w1 = env.sb("w1", [K1 + 3, E, I], F16)
        b1p = env.sb("b1p", [1, 3, E * I], F16)
        w2 = env.sb("w2", [P, E, HD])
        b2c = env.sb("b2c", [P, G4])
        wo = env.sb("wo", [P, 2, D])
        bob = env.sb("bob", [P, 2, D])
        fold = env.sb("fold", [P, HD])
        hx = env.sb("hx", [K1 + 3, HF, CH], F16)
        gb = env.sb("gb", [P, 2, G4, CH])
        act_out = env.sb("act_out", [P, 8, CH])
        pr = env.sb("pr", [P, 2, G4, CH])
        half = env.sb("half", [P, 2, CH])
        sums = env.sb("sums", [P, 8, CH])
        comb = env.sb("comb", [P, 2, CH])
        y = env.sb("y", [P, 2, 2, D])
        b1f = pr[0:1].rearrange("p a g t -> p a (g t)")
        w1f = sums[0:K1, 0:E * I // CH].rearrange("p a (e i) -> p (a e) i", i=I)

        ps_f = env.psum("f")
        ps_u = [env.psum(f"u{i}") for i in range(4)]
        ps_e = [env.psum(f"e{i}") for i in range(2)]
        ps_y = env.psum("y")

        loaded, zeroed = env.sem("loaded"), env.sem("zeroed")
        stats, std_ready, step = env.sem("stats"), env.sem("std_ready"), env.sem("step")
        xn_ready = env.sem("xn_ready")
        xnT_ps = env.sem("xnT_ps")
        xnT_ready = env.sem("xnT_ready")
        h_ps = env.sem("h_ps", 2)
        hf_ready = env.sem("hf_ready")
        hs_ready = env.sem("hs_ready")
        hi_ready = env.sem("hi_ready")
        lo_ready = env.sem("lo_ready", 2)
        logits_ps = env.sem("logits_ps", 1)
        less_max = env.sem("less_max", 1)
        exp_done = env.sem("exp_done")
        top_step = env.sem("top_step")
        gT_ps = env.sem("gT_ps", 1)
        gT_ready = env.sem("gT_ready", 1)
        hi_stored, lo_stored = env.sem("hi_stored", 16), env.sem("lo_stored", 16)
        gT_stored = env.sem("gT_stored", 16)

        w_loaded, prep = env.sem("w_loaded"), env.sem("prep")
        b1_placed, w1_ready = env.sem("b1_placed"), env.sem("w1_ready")
        hx_loaded = [env.sem(f"hx_loaded{h}") for h in range(HF)]
        gb_loaded = [env.sem(f"gb_loaded{i}") for i in range(2)]
        u_ps = env.sem("u_ps")
        gelu_done = env.sem("gelu_done", 4)
        e_ps = env.sem("e_ps", 2)
        pr_ready = env.sem("pr_ready", 8)
        half_ready = env.sem("half_ready")
        sum_ready = env.sem("sum_ready", 8)
        c_ps = env.sem("c_ps", 2)
        comb_ready = env.sem("comb_ready", 1)
        y_ps = env.sem("y_ps", 2)
        y_part = env.sem("y_part", 1)
        y_ready = env.sem("y_ready")
        y_stored = [env.sem(f"y_stored{i}", 16) for i in range(2)]
        block = env.block()
        LOADS = 16 * (2 + 2 + 4)
        W_LOADS = 16 * (3 + 1 + 1 + 4 + 1 + 2 + 1)
        TOP = 17

        @block.sync
        def _(sp):
            sp.wait_ge(zeroed.sem, 1)
            sp.dma_start(wm[:], Wm.rearrange("(k p) n -> p k n", p=P)).then_inc(loaded.sem, 16)
            sp.dma_start(rk[:], rank).then_inc(loaded.sem, 16)
            for m in range(2):
                sp.dma_start(bias[:, m:m + 1], bm[m * P:(m + 1) * P].rearrange("(p a) -> p a", a=1)
                             ).then_inc(loaded.sem, 16)
            for j in range(4):
                sp.dma_start(emb[HD * j:HD * (j + 1), E * j:E * (j + 1)], expert_emb).then_inc(loaded.sem, 16)
            for r in range(3):
                sp.dma_start(w1f[HD * r:HD * (r + 1), :, :], W1.rearrange("e d i -> d e i")).then_inc(w_loaded.sem, 16)
            sp.dma_start(b1f[:, 0, :], b1.rearrange("(a e) i -> a (e i)", a=1)).then_inc(w_loaded.sem, 16)
            sp.dma_start(w2[:], W2.rearrange("e i o -> i e o")).then_inc(w_loaded.sem, 16)
            for j in range(4):
                sp.dma_start(b2c[HD * j:HD * (j + 1), :], b2.rearrange("(g j) o -> j o g", j=4)[j],
                             allow_slow_non_contiguous=True).then_inc(w_loaded.sem, 16)
            sp.dma_start(wo[:], Wo.rearrange("(k p) n -> p k n", p=P)).then_inc(w_loaded.sem, 16)
            for t in range(2):
                sp.dma_start(bob[:, t, :], bo.rearrange("(a n) -> a n", a=1).broadcast_to([P, D])
                             ).then_inc(w_loaded.sem, 16)
            sp.dma_start(fold[:], fold_in).then_inc(w_loaded.sem, 16)

            def load_h(c, h):
                for r, part in enumerate((0, 1, 0)):
                    if h == 0 and r < 2:
                        stored = (hi_stored, lo_stored)[r]
                        sp.wait_ge(stored.sem, stored.at(16 * (c + 1)))
                    sp.dma_start(hx[HD * r:HD * (r + 1), h, :],
                                 h_parts[part][HD * h:HD * (h + 1), bass.ds(CH * c, CH)]).then_inc(hx_loaded[h].sem, 16)

            def load_gates(c, h):
                sp.wait_ge(pr_ready.sem, pr_ready.at(GROUPS * c + G4 * (h - 1)))
                for j in range(4):
                    src = gates_t.rearrange("(h g j) t -> h j g t", h=HF, j=4)[h, j, :, bass.ds(CH * c, CH)]
                    sp.dma_start(gb[HD * j:HD * (j + 1), h % 2, :, :], src.unsqueeze(0).broadcast_to([HD, G4, CH])
                                 ).then_inc(gb_loaded[h % 2].sem, 16)

            ov = out.rearrange("b (t p) d -> p (b t) d", p=P)

            def store_y(c, n):
                sp.wait_ge(y_ready.sem, y_ready.at(2 * c + n + 1))
                sp.dma_start(ov[:, bass.ds(CT_ * c + 2 * n, 2), :], y[:, n, :, :]).then_inc(y_stored[n].sem, 16)

            for c in y_stored:
                sp.sem_inc(c.sem, c.credit)
            for r in range(3):
                sp.wait_ge(prep.sem, 3 + 2 * r)
                sp.dma_start(w1[K1 + r:K1 + r + 1, :, :], b1p[:, r, :].rearrange("a (e i) -> a e i", e=E)
                             ).then_inc(b1_placed.sem, 16)
            for h in range(HF):
                load_h(0, h)

            def body(c, before, more):
                for h in range(HF):
                    load_gates(c, h)
                    if before and h < 2:
                        load_h(c, HF - 2 + h)
                    if more and h >= 4:
                        if h == 4:
                            load_h(c + 1, 0)
                            load_h(c + 1, 1)
                        if h == HF - 1:
                            sp.wait_ge(gT_stored.sem, gT_stored.at(16 * (c + 2)))
                        load_h(c + 1, h - 2)
                    if before and h in (5, 6):
                        store_y(c - 1, h - 5)

            sp.wait_ge(gT_stored.sem, gT_stored.at(16))
            body(0, False, True)
            with sp.Fori(1, CHUNKS - 1) as c:
                body(c, True, True)
            body(CHUNKS - 1, True, False)
            for n in range(2):
                store_y(CHUNKS - 1, n)
            for n in range(2):
                sp.wait_ge(y_stored[n].sem, y_stored[n].at(16 * CHUNKS))

        @block.gpsimd
        def _(pool):
            for c in (lo_ready, sum_ready):
                pool.sem_inc(c.sem, c.credit)

            def low_parts(c):
                for m in range(2):
                    pool.wait_ge(hi_ready.sem, hi_ready.at(2 * c + m + 1))
                    pool.wait_ge(lo_stored.sem, lo_stored.at(16 * c))
                    nc.gpsimd.tensor_tensor(lo[:, m, :], hs[:, m, :], hi[:, m, :], ALU.subtract
                                            ).then_inc(lo_ready.sem, 1)

            def add_groups(c, h):
                pool.wait_ge(pr_ready.sem, pr_ready.at(GROUPS * c + G4 * (h + 1)))
                pool.wait_ge(sum_ready.sem, sum_ready.at(8 * c + h))
                nc.gpsimd.tensor_tensor(half[:], pr[:, h % 2, 0:2, :], pr[:, h % 2, 2:4, :], ALU.add
                                        ).then_inc(half_ready.sem, 1)
                pool.wait_ge(half_ready.sem, half_ready.at(8 * c + h + 1))
                pool.wait_ge(c_ps.sem, c_ps.at(2 * c + h // 4 - 1))
                nc.gpsimd.tensor_tensor(sums[:, h, :], half[:, 0, :], half[:, 1, :], ALU.add
                                        ).then_inc(sum_ready.sem, 1)

            def body(c, more):
                for h in range(HF):
                    add_groups(c, h)
                    if more and h == 1:
                        low_parts(c + 1)

            low_parts(0)
            with pool.Fori(0, CHUNKS - 1) as c:
                body(c, True)
            body(CHUNKS - 1, False)

        @block.vector
        def _(dve):
            for c in (less_max, pr_ready, comb_ready, y_part):
                dve.sem_inc(c.sem, c.credit)
            nc.vector.memset(emb[:], 0.0).then_inc(zeroed.sem, 1)
            for t in range(TILES):
                nc.vector.bn_aggr(mv[:, t, :], x_raw[:, t, :]).then_inc(stats.sem, 1)
            dve.wait_ge(stats.sem, TILES)
            nc.vector.tensor_scalar(var[:], mv[:, :, 1], EPS, None, ALU.add).then_inc(stats.sem, 1)
            dve.wait_ge(std_ready.sem, 1)
            refine_rsqrt(nc, dve, rstd[:], var[:], ntmp[:], step, 0)

            def normalise(c, tiles):
                for t in tiles:
                    nc.vector.tensor_scalar(xn[:, t, :], X[:, bass.ds(CT_ * c + t, 1), :].rearrange("p a d -> p (a d)"),
                                            mv[:, bass.ds(CT_ * c + t, 1), 0:1].rearrange("p a d -> p (a d)"),
                                            rstd[:, bass.ds(CT_ * c + t, 1)],
                                            ALU.subtract, ALU.mult).then_inc(xn_ready.sem, 1)

            def wide(a):
                return a.unsqueeze(2).broadcast_to([P, G, E])

            def selected(c, n):
                dve.wait_ge(top_step.sem, top_step.at(TOP * c + n))

            def less_maximum(c):
                logits = ps_f[:].rearrange("p (g e) -> p g e", e=E)
                dve.wait_ge(logits_ps.sem, logits_ps.at(c + 1))
                nc.vector.tensor_reduce(top[:], logits, AX, ALU.max).then_inc(top_step.sem, 1)
                selected(c, 1)
                nc.vector.tensor_tensor(w[:], logits, wide(top[:]), ALU.subtract).then_inc(less_max.sem, 1)

            def softmax(c):
                dve.wait_ge(exp_done.sem, exp_done.at(c + 1))
                nc.vector.tensor_reduce(den[:], w[:], AX, ALU.add).then_inc(top_step.sem, 1)
                selected(c, 2)
                nc.vector.reciprocal(den[:], den[:]).then_inc(top_step.sem, 1)
                selected(c, 3)
                nc.vector.tensor_tensor(w[:], w[:], wide(den[:]), ALU.mult).then_inc(top_step.sem, 1)
                selected(c, 4)

            def mark_largest(c, n):
                at = 4 + 6 * n
                src = w_rest if n else w
                nc.vector.tensor_reduce(top[:], src[:], AX, ALU.max).then_inc(top_step.sem, 1)
                selected(c, at + 1)
                nc.vector.tensor_tensor(eq[:], src[:], wide(top[:]), ALU.is_equal).then_inc(top_step.sem, 1)
                selected(c, at + 2)
                nc.vector.tensor_tensor(eq[:], eq[:], rk[:].unsqueeze(1).broadcast_to([P, G, E]), ALU.mult
                                        ).then_inc(top_step.sem, 1)
                selected(c, at + 3)

            def choose(c, n):
                at = 7 + 6 * n
                nc.vector.tensor_reduce(top[:], eq[:], AX, ALU.max).then_inc(top_step.sem, 1)
                selected(c, at + 1)
                nc.vector.tensor_tensor(hot[:, n], eq[:], wide(top[:]), ALU.is_equal).then_inc(top_step.sem, 1)
                selected(c, at + 2)
                if n == 0:
                    nc.vector.scalar_tensor_tensor(w_rest[:].rearrange("p g e -> p (g e)"),
                                                   hot[:, 0].rearrange("p g e -> p (g e)"), -2.0,
                                                   w[:].rearrange("p g e -> p (g e)"), ALU.mult, ALU.add
                                                   ).then_inc(top_step.sem, 1)
                    selected(c, at + 3)

            def make_gates(c):
                nc.vector.tensor_tensor(eq[:], hot[:, 0], hot[:, 1], ALU.add).then_inc(top_step.sem, 1)
                selected(c, TOP - 1)
                dve.wait_ge(gT_ps.sem, gT_ps.at(c))
                nc.vector.tensor_tensor(gates[:].rearrange("p t (h e) -> p (t h) e", e=E), eq[:], w[:], ALU.mult
                                        ).then_inc(top_step.sem, 1)
                selected(c, TOP)

            def gate(c, n):
                h, g = divmod(n, G4)
                dve.wait_ge(e_ps.sem, e_ps.at(GROUPS * c + n + 1))
                if g == 0:
                    dve.wait_ge(gb_loaded[h % 2].sem, 64 * (4 * c + h // 2 + 1))
                    dve.wait_ge(sum_ready.sem, sum_ready.at(8 * c + h - 1))
                nc.vector.scalar_tensor_tensor(pr[:, h % 2, g, :], ps_e[n % 2][:], b2c[:, g:g + 1], gb[:, h % 2, g, :],
                                               ALU.add, ALU.mult).then_inc(pr_ready.sem, 1)

            def evacuate_comb(c, q):
                dve.wait_ge(c_ps.sem, c_ps.at(2 * c + q + 1))
                dve.wait_ge(y_ps.sem, y_ps.at(2 * c))
                nc.vector.tensor_copy(comb[:, q, :], ps_y[:]).then_inc(comb_ready.sem, 1)

            def finish(c, n):
                dve.wait_ge(y_ps.sem, y_ps.at(2 * c + n + 1))
                dve.wait_ge(y_stored[n].sem, y_stored[n].at(16 * c))
                nc.vector.tensor_tensor(y[:, n, :, :], ps_y[:].rearrange("p (t d) -> p t d", t=2), bob[:], ALU.add
                                        ).then_inc(y_part.sem, 1)
                dve.wait_ge(y_part.sem, y_part.at(2 * c + n + 1))
                nc.vector.tensor_tensor(y[:, n, :, :], y[:, n, :, :], X[:, bass.ds(CT_ * c + 2 * n, 2), :], ALU.add
                                        ).then_inc(y_ready.sem, 1)

            def body(c, before, more):
                for n in range(GROUPS):
                    gate(c, n)
                    if more:
                        if n in (0, 1):
                            if n == 0:
                                dve.wait_ge(xnT_ps.sem, xnT_ps.at(2 * c + 2))
                            normalise(c + 1, (2 * n, 2 * n + 1))
                        if n == 13:
                            less_maximum(c + 1)
                        if n == 15:
                            softmax(c + 1)
                        if n in (17, 20):
                            mark_largest(c + 1, (n - 17) // 3)
                        if n in (18, 22):
                            choose(c + 1, (n - 18) // 4)
                        if n == 24:
                            make_gates(c + 1)
                    if before and n == 3:
                        evacuate_comb(c - 1, 1)
                    if before and n in (16, 19):
                        finish(c - 1, (n - 16) // 3)
                    if n == 21:
                        evacuate_comb(c, 0)

            normalise(0, range(CT_))
            dve.wait_ge(w_loaded.sem, W_LOADS)
            nc.vector.tensor_scalar(b1f[:, 0, :], b1f[:, 0, :], W_SCALE, None, ALU.mult).then_inc(prep.sem, 1)
            nc.vector.memset(hx[K1:K1 + 3, :, :], H_SCALE).then_inc(prep.sem, 1)
            dve.wait_ge(prep.sem, 2)
            for r in range(3):
                nc.vector.tensor_copy(b1p[:, r, :], b1f[:, r % 2, :]).then_inc(prep.sem, 1)
                dve.wait_ge(prep.sem, 3 + 2 * r)
                if r < 2:
                    nc.vector.tensor_tensor(b1f[:, (r + 1) % 2, :], b1f[:, r % 2, :], b1p[:, r, :], ALU.subtract
                                            ).then_inc(prep.sem, 1)
                    dve.wait_ge(prep.sem, 4 + 2 * r)
            nc.vector.tensor_scalar(w1h[:], w1f[:], W_SCALE, None, ALU.mult).then_inc(w1_ready.sem, 1)
            dve.wait_ge(w1_ready.sem, 1)
            nc.vector.tensor_copy(w1[0:2 * HD], w1h[0:2 * HD]).then_inc(w1_ready.sem, 1)
            nc.vector.scalar_tensor_tensor(w1[2 * HD:K1].rearrange("p e i -> p (e i)"),
                                           w1f[2 * HD:K1].rearrange("p e i -> p (e i)"), W_SCALE,
                                           w1h[2 * HD:K1].rearrange("p e i -> p (e i)"), ALU.mult, ALU.subtract
                                           ).then_inc(w1_ready.sem, 1)
            dve.wait_ge(w1_ready.sem, 3)
            dve.wait_ge(loaded.sem, LOADS)
            less_maximum(0)
            softmax(0)
            for n in range(2):
                mark_largest(0, n)
                choose(0, n)
            make_gates(0)
            body(0, False, True)
            with dve.Fori(1, CHUNKS - 1) as c:
                body(c, True, True)
            body(CHUNKS - 1, True, False)
            evacuate_comb(CHUNKS - 1, 1)
            for n in range(2):
                finish(CHUNKS - 1, n)

        @block.scalar
        def _(act):
            for c in (gT_ready, hi_stored, lo_stored, gT_stored, gelu_done):
                act.sem_inc(c.sem, c.credit)
            act.wait_ge(stats.sem, TILES + 1)
            nc.scalar.activation(rstd[:], var[:], ACT.Sqrt).then_inc(std_ready.sem, 1)
            act.wait_ge(loaded.sem, LOADS)
            nc.scalar.activation(bias_s[:], bias[:], ACT.Copy, scale=H_SCALE).then_inc(std_ready.sem, 1)
            act.wait_ge(std_ready.sem, 2)

            def evacuate_xnT(c, k):
                act.wait_ge(xnT_ps.sem, xnT_ps.at(2 * c + k + 1))
                act.wait_ge(h_ps.sem, h_ps.at(2 * c))
                nc.scalar.activation(xnT[:, k, :], ps_f[:], ACT.Copy).then_inc(xnT_ready.sem, 1)

            def evacuate_h(c, m):
                act.wait_ge(h_ps.sem, h_ps.at(2 * c + m + 1))
                act.wait_ge(logits_ps.sem, logits_ps.at(c))
                nc.scalar.activation(hf[:, m, :], ps_f[:], ACT.Identity, bias=bias[:, m:m + 1]).then_inc(hf_ready.sem, 1)
                act.wait_ge(lo_ready.sem, lo_ready.at(2 * c))
                nc.scalar.activation(hs[:, m, :], ps_f[:], ACT.Identity, bias=bias_s[:, m:m + 1], scale=H_SCALE
                                     ).then_inc(hs_ready.sem, 1)

            def high_part(c, m):
                act.wait_ge(hs_ready.sem, hs_ready.at(2 * c + m + 1))
                act.wait_ge(hi_stored.sem, hi_stored.at(16 * c))
                nc.scalar.activation(hi[:, m, :], hs[:, m, :], ACT.Copy).then_inc(hi_ready.sem, 1)

            def store_part(c, n):
                buf, ready, stored = ((hi, hi_ready, hi_stored), (lo, lo_ready, lo_stored))[n]
                act.wait_ge(ready.sem, ready.at(2 * c + 2))
                act.dma_start(h_parts[n].rearrange("(m p) t -> p m t", p=P)[:, :, bass.ds(CH * c, CH)], buf[:]
                              ).then_inc(stored.sem, 16)

            def exponentials(c):
                act.wait_ge(less_max.sem, less_max.at(c + 1))
                nc.scalar.activation(w[:], w[:], ACT.Exp).then_inc(exp_done.sem, 1)

            def store_gates(c):
                act.wait_ge(gT_ps.sem, gT_ps.at(c + 1))
                act.wait_ge(gT_stored.sem, gT_stored.at(16 * c))
                nc.scalar.activation(gT[:], ps_f[:], ACT.Copy).then_inc(gT_ready.sem, 1)
                act.wait_ge(gT_ready.sem, gT_ready.at(c + 1))
                act.dma_start(gates_t[:, bass.ds(CH * c, CH)], gT[:]).then_inc(gT_stored.sem, 16)

            def gelu(c, i):
                act.wait_ge(u_ps.sem, u_ps.at(HIDDEN * c + i + 1))
                act.wait_ge(e_ps.sem, e_ps.at(GROUPS * c + i // 4 - 1))
                nc.scalar.activation(act_out[:, i % 8, :], ps_u[i % 4][:], ACT.Gelu,
                                     scale=1.0 / (H_SCALE * W_SCALE)).then_inc(gelu_done.sem, 1)

            def body(c, more):
                for n in range(GROUPS):
                    for i in range(4 * n, 4 * n + 4):
                        gelu(c, i)
                    if more:
                        if n in (3, 5):
                            evacuate_xnT(c + 1, (n - 3) // 2)
                        if n in (7, 10):
                            evacuate_h(c + 1, (n - 7) // 3)
                        if n in (8, 11):
                            high_part(c + 1, (n - 8) // 3)
                        if n == 12:
                            store_part(c + 1, 0)
                        if n == 14:
                            store_part(c + 1, 1)
                            exponentials(c + 1)
                        if n == 26:
                            store_gates(c + 1)

            for k in range(2):
                evacuate_xnT(0, k)
            for m in range(2):
                evacuate_h(0, m)
                high_part(0, m)
            store_part(0, 0)
            store_part(0, 1)
            exponentials(0)
            store_gates(0)
            with act.Fori(0, CHUNKS - 1) as c:
                body(c, True)
            body(CHUNKS - 1, False)

        @block.tensor
        def _(pe):
            for c in (h_ps, logits_ps, gT_ps, e_ps, c_ps, y_ps):
                pe.sem_inc(c.sem, c.credit)

            def transpose_xn(c, k):
                pe.wait_ge(xn_ready.sem, xn_ready.at(4 * c + 4))
                if k == 0:
                    pe.wait_ge(gT_ready.sem, gT_ready.at(c))
                else:
                    pe.wait_ge(xnT_ready.sem, xnT_ready.at(2 * c + 1))
                for t in range(CT_):
                    ins = pe.transpose(ps_f[:, t * P:(t + 1) * P], xn[:, t, k * P:(k + 1) * P], ident[:])
                ins.then_inc(xnT_ps.sem, 1)

            def project_h(c, m, k):
                if k == 0:
                    pe.wait_ge(xnT_ready.sem, xnT_ready.at(2 * c + 2))
                    if m == 1:
                        pe.wait_ge(hs_ready.sem, hs_ready.at(2 * c + 1))
                ins = pe.matmul(ps_f[:], wm[:, k, m * P:(m + 1) * P], xnT[:, k, :], start=(k == 0), stop=(k == 1),
                                skip_group_check=True)
                if k == 1:
                    ins.then_inc(h_ps.sem, 1)

            def logits(c):
                pe.wait_ge(hf_ready.sem, hf_ready.at(2 * c + 2))
                pe.wait_ge(hs_ready.sem, hs_ready.at(2 * c + 2))
                for t in range(CT_):
                    for m in range(2):
                        ins = pe.matmul(ps_f[:, t * P + m * 64:t * P + (m + 1) * 64], hf[:, m, t * P:(t + 1) * P],
                                        emb[:], start=True, stop=True, skip_group_check=True)
                ins.then_inc(logits_ps.sem, 1)

            def transpose_gates(c):
                pe.wait_ge(top_step.sem, top_step.at(TOP * c + TOP))
                pe.wait_ge(less_max.sem, less_max.at(c + 1))
                for t in range(CT_):
                    ins = pe.transpose(ps_f[:, t * P:(t + 1) * P], gates[:, t, :], ident[:])
                ins.then_inc(gT_ps.sem, 1)

            def up(c, i):
                h, e = divmod(i, E)
                if e == 0:
                    pe.wait_ge(hx_loaded[h].sem, 48 * (c + 1))
                pe.wait_ge(gelu_done.sem, gelu_done.at(HIDDEN * c + i - 3))
                pe.matmul(ps_u[i % 4][:], w1[:, e, :], hx[:, h, :], start=True, stop=True).then_inc(u_ps.sem, 1)

            def down(c, n):
                g = n % G4
                pe.wait_ge(gelu_done.sem, gelu_done.at(HIDDEN * c + 4 * n + 4))
                pe.wait_ge(pr_ready.sem, pr_ready.at(GROUPS * c + n - 1))
                for j in range(4):
                    ins = pe.matmul(ps_e[n % 2][HD * j:HD * (j + 1), :], w2[:, 4 * g + j, :],
                                    act_out[:, (4 * n + j) % 8, :], start=True, stop=True, skip_group_check=True)
                ins.then_inc(e_ps.sem, 1)

            def combine(c, q):
                pe.wait_ge(sum_ready.sem, sum_ready.at(8 * c + 4 * q + 4))
                pe.wait_ge(comb_ready.sem, comb_ready.at(2 * c + q))
                pe.wait_ge(y_part.sem, y_part.at(2 * c))
                for j in range(4):
                    ins = pe.matmul(ps_y[HD * j:HD * (j + 1), :], fold[:], sums[:, 4 * q + j, :],
                                    start=True, stop=True, skip_group_check=True)
                ins.then_inc(c_ps.sem, 1)

            def project_out(c, n, t):
                pe.wait_ge(comb_ready.sem, comb_ready.at(2 * c + 2))
                pe.wait_ge(y_part.sem, y_part.at(2 * c + n))
                for k in range(2):
                    ins = pe.matmul(ps_y[:, t * D:(t + 1) * D], comb[:, k, (2 * n + t) * P:(2 * n + t + 1) * P],
                                    wo[:, k, :], start=(k == 0), stop=(k == 1), skip_group_check=True)
                if t == 1:
                    ins.then_inc(y_ps.sem, 1)

            def body(c, before, more):
                for n in range(GROUPS):
                    for i in range(4 * n, 4 * n + 4):
                        up(c, i)
                    if n >= 1:
                        down(c, n - 1)
                    elif before:
                        down(c - 1, GROUPS - 1)
                    if more:
                        if n in (2, 4):
                            transpose_xn(c + 1, (n - 2) // 2)
                        if n in (6, 9):
                            project_h(c + 1, (n - 6) // 3, 0)
                        if n in (7, 10):
                            project_h(c + 1, (n - 7) // 3, 1)
                        if n == 12:
                            logits(c + 1)
                        if n == 25:
                            transpose_gates(c + 1)
                    if before and n == 3:
                        combine(c - 1, 1)
                    if before and n in (14, 15, 17, 18):
                        project_out(c - 1, (n - 14) // 3, (n - 14) % 3)
                    if n == 20:
                        combine(c, 0)

            pe.wait_ge(loaded.sem, LOADS)
            for k in range(2):
                transpose_xn(0, k)
            for m in range(2):
                for k in range(2):
                    project_h(0, m, k)
            logits(0)
            transpose_gates(0)
            pe.wait_ge(w_loaded.sem, W_LOADS)
            pe.wait_ge(prep.sem, 2)
            pe.wait_ge(b1_placed.sem, 48)
            pe.wait_ge(w1_ready.sem, 3)
            body(0, False, True)
            with pe.Fori(1, CHUNKS - 1) as c:
                body(c, True, True)
            body(CHUNKS - 1, True, False)
            down(CHUNKS - 1, GROUPS - 1)
            combine(CHUNKS - 1, 1)
            for n in range(2):
                for t in range(2):
                    project_out(CHUNKS - 1, n, t)


def constants():
    p = np.arange(P)
    theta = np.float32(1.0) / np.float32(10000.0) ** (np.arange(0, DH1, 2, dtype=np.float32) / np.float32(DH1))
    angle = np.outer(np.arange(S, dtype=np.float32), theta.astype(np.float32)).astype(np.float32)
    angle = np.concatenate([angle, angle], axis=1)[:, p % DH1].T
    sign = np.where(p % DH1 < DH1 // 2, -1.0, 1.0).astype(np.float32)[:, None]
    table = np.concatenate([np.cos(angle), sign * np.sin(angle)], axis=1).astype(np.float32)
    return {
        "ident_in": np.eye(P, dtype=np.float32),
        "rope": (table * np.float32(Q_SCALE)).astype(np.float32),
        "rank": np.broadcast_to(np.arange(E, 0, -1, dtype=np.float32), (P, E)).copy(),
        "fold_in": np.tile(np.eye(HD, dtype=np.float32), (P // HD, 1)),
    }


def decoder(nc, x, ctx_1024, w_qkv, w_out, b_out, media_w, media_b, lat_w, lat_b, Wq, Wk, Wv, Wout,
            Wm, bm, expert_emb, W1, b1, W2, b2, Wo, bo, ident_in, rope, rank, fold_in, out):
    qk_parts = nc.dram_tensor("qk_parts", [4, P, 2, S], F16).ap()
    h_parts = nc.dram_tensor("h_parts", [2, D, B * S], F16).ap()
    gates_t = nc.dram_tensor("gates_t", [HF * E, B * S], F32).ap()
    with ExitStack() as ctx:
        X, ident, x_raw = (ctx.enter_context(nc.sbuf_tensor(name, shape, F32)) for name, shape in
                           (("X", [P, TILES, D]), ("ident", [P, P]), ("x_raw", [P, TILES, 6])))
        with nc.sbuf_tensor("C", [P, TILES, D], F32) as C, nc.sbuf_tensor("c_raw", [P, TILES, 6], F32) as c_raw:
            self_attention(nc, X, C, ident, x_raw, c_raw, qk_parts, x, ctx_1024, ident_in, w_qkv, w_out, b_out, rope)
            cross_attention(nc, X, C, ident, x_raw, c_raw, media_w, media_b, lat_w, lat_b, Wq, Wk, Wv, Wout)
        ffn(nc, X, ident, x_raw, h_parts, gates_t, Wm, bm, expert_emb, rank, W1, b1, W2, b2, Wo, bo, fold_in, out)


_INS = ["x", "ctx_1024", "L0_attn_w_qkv", "L0_attn_w_out", "L0_attn_b_out",
        "L0_xattn_ln_media_w", "L0_xattn_ln_media_b", "L0_xattn_ln_lat_w", "L0_xattn_ln_lat_b",
        "L0_xattn_Wq", "L0_xattn_Wk", "L0_xattn_Wv", "L0_xattn_Wout",
        "L0_ffn_Wm", "L0_ffn_bm", "L0_ffn_expert_emb", "L0_ffn_W1", "L0_ffn_b1", "L0_ffn_W2", "L0_ffn_b2",
        "L0_ffn_Wo", "L0_ffn_bo"]


def kernel(**inputs):
    import concourse.bacc as bacc
    from concourse.bass_utils import run_bass_kernel_spmd

    nc = bacc.Bacc("TRN2", target_bir_lowering=False, num_devices=1)
    arrays, args = {}, []
    for name, a in [(n, inputs[n]) for n in _INS] + list(constants().items()):
        a = np.ascontiguousarray(a)
        arrays[f"in_{name}_dram"] = a
        args.append(nc.dram_tensor(f"in_{name}_dram", a.shape, mybir.dt.from_np(a.dtype), kind="ExternalInput").ap())
    args.append(nc.dram_tensor("out_0_dram", (B, S, D), F32, kind="ExternalOutput").ap())
    decoder(nc, *args)
    r = run_bass_kernel_spmd(nc, [arrays], core_ids=[0])
    return r.results[0]["out_0_dram"]
```

```python
from contextlib import ExitStack

import numpy as np

import concourse.bass as bass
from concourse import mybir

F32 = mybir.dt.float32
F16 = mybir.dt.float16
ALU = mybir.AluOpType
ACT = mybir.ActivationFunctionType
AX = mybir.AxisListType.X

P = 128
B, S, D = 16, 256, 256
TILES = B * S // P
QT = S // P
EPS = 1e-5
H1, DH1 = 16, 16
H2, DH2 = 8, 64
INNER = H2 * DH2
KV = 2 * S
HF, HD, E, I = 8, 32, 16, 128
CH = 512
CHUNKS = B * S // CH
CT_ = CH // P


class Count:

    def __init__(self, sem, credit):
        self.sem, self.credit = sem, credit

    def at(self, n):
        return n + self.credit


class Env:

    def __init__(self, nc, name):
        self.nc, self.name, self.ctx = nc, name, ExitStack()

    def __enter__(self):
        self.ctx.__enter__()
        return self

    def __exit__(self, *a):
        return self.ctx.__exit__(*a)

    def sb(self, name, shape, dt=F32):
        return self.ctx.enter_context(self.nc.sbuf_tensor(f"{self.name}_{name}", shape, dt))

    def psum(self, name, banks=1):
        shape = [P, 512] if banks == 1 else [P, banks, 512]
        return self.ctx.enter_context(self.nc.psum_tensor(f"{self.name}_ps_{name}", shape, F32))

    def sem(self, name, credit=0):
        return Count(self.ctx.enter_context(self.nc.semaphore(f"{self.name}_{name}")), credit)

    def block(self):
        return self.ctx.enter_context(self.nc.Block())


def ln_statistics(nc, dve, env, x, n, mean_var, done, at=0):
    raw = env.sb(f"ln_raw{at}", [P, n, 6])
    for t in range(n):
        nc.vector.bn_stats(raw[:, t, :], x(t)).then_inc(done.sem, 1)
    for t in range(n):
        dve.wait_ge(done.sem, done.at(at + t + 1))
        nc.vector.bn_aggr(mean_var[:, t, :], raw[:, t, :]).then_inc(done.sem, 1)


def refine_rsqrt(nc, dve, rstd, var, tmp, step, at):
    nc.vector.reciprocal(rstd, rstd).then_inc(step.sem, 1)
    dve.wait_ge(step.sem, at + 1)
    nc.vector.tensor_tensor(tmp, rstd, rstd, ALU.mult).then_inc(step.sem, 1)
    dve.wait_ge(step.sem, at + 2)
    nc.vector.tensor_tensor(tmp, tmp, var, ALU.mult).then_inc(step.sem, 1)
    dve.wait_ge(step.sem, at + 3)
    nc.vector.tensor_scalar(tmp, tmp, -0.5, 1.5, ALU.mult, ALU.add).then_inc(step.sem, 1)
    dve.wait_ge(step.sem, at + 4)
    nc.vector.tensor_tensor(rstd, rstd, tmp, ALU.mult).then_inc(step.sem, 1)
    dve.wait_ge(step.sem, at + 5)
    return at + 5


W_SCALE = 256.0
A_SCALE = 16.0
PROJECTED = 1.0 / (A_SCALE * W_SCALE)
Q_SCALE = K_SCALE = 16.0
S_SCALE = DH1 ** -0.5 / (Q_SCALE * K_SCALE)


def self_attention(nc, X, C, ident, x_raw, c_raw, qk_parts, x_in, context, ident_in, w_qkv, w_out, b_out, rope):
    PAIRS = H1 // 2
    HP = PAIRS // 2
    with Env(nc, "p1") as env:
        wf = env.sb("wf", [P, 2, 5 * D])
        wh = env.sb("wh", [P, 2, 5 * D], F16)
        wl = env.sb("wl", [P, 2, 5 * D], F16)
        wout = env.sb("wout", [P, 2, D])
        bout = env.sb("bout", [P, QT, D])
        cs = env.sb("cs", [P, 2 * S])
        mv = env.sb("mv", [P, TILES, 2])
        var = env.sb("var", [P, TILES])
        rstd = env.sb("rstd", [P, TILES])
        ntmp = env.sb("ntmp", [P, TILES])
        xn = env.sb("xn", [P, QT, D])
        xh = env.sb("xh", [P, 2, S], F16)
        xl = env.sb("xl", [P, 2, S], F16)
        rt = env.sb("rt", [P, 2, 2 * S])
        qkf = env.sb("qkf", [P, 2, S])
        parts = env.sb("parts", [P, 2, 2, S], F16)
        qs = env.sb("qs", [96, PAIRS, S], F16)
        ks = env.sb("ks", [96, PAIRS, 2, S], F16)
        v = env.sb("v", [P, QT, H1, 2 * DH1])
        prob = env.sb("prob", [P, 2, QT, 2, S])
        smax = env.sb("smax", [P, 2, QT, 2])
        nmax = env.sb("nmax", [P, 2, QT, 2])
        pT = env.sb("pT", [P, 8, 2, S])
        oT = env.sb("oT", [P, 4, S])
        rinv = env.sb("rinv", [P, 2 * QT * 4])
        warm = env.sb("warm", [P, 2])
        on = env.sb("on", [P, QT, D])
        onT = env.sb("onT", [P, 2, S])
        res = env.sb("res", [P, QT, D])

        ps_s = [env.psum(f"s{i}") for i in range(2)]
        ps_t = [env.psum(f"t{i}") for i in range(2)]
        ps_o = env.psum("o")
        ps_p = [env.psum(f"p{i}") for i in range(2)]
        ps_m = env.psum("m")

        x_first, x_loaded, w_loaded = env.sem("x_first"), env.sem("x_loaded"), env.sem("w_loaded")
        wf_loaded, filled = env.sem("wf_loaded"), env.sem("filled")
        stats, std_ready, step = env.sem("stats"), env.sem("std_ready"), env.sem("step")
        wh_ready, wl_ready = env.sem("wh_ready"), env.sem("wl_ready")
        wrot_ready, c_loaded = env.sem("wrot_ready"), env.sem("c_loaded")
        xn_ready = env.sem("xn_ready")
        xnT_ps = env.sem("xnT_ps")
        xh_ready = env.sem("xh_ready")
        xT_ready = env.sem("xT_ready")
        qk_ps = env.sem("qk_ps")
        qk_mul = env.sem("qk_mul", 2)
        qk_sum = env.sem("qk_sum", 2)
        hi_ready = env.sem("hi_ready")
        lo_ready = env.sem("lo_ready", 2)
        stored = env.sem("stored", 32)
        q_stacked = env.sem("q_stacked")
        k_stacked = env.sem("k_stacked")
        v_ps = env.sem("v_ps", 1)
        v_ready = env.sem("v_ready", 1)
        s_ps = env.sem("s_ps", 16)
        smax_ready = env.sem("smax_ready")
        nmax_ready = env.sem("nmax_ready")
        exp_done = env.sem("exp_done", 4)
        pT_ps = env.sem("pT_ps", 4)
        pT_act = env.sem("pT_act", 1)
        pT_dve = env.sem("pT_dve", 1)
        o_ps = env.sem("o_ps", 2)
        oT_ready = env.sem("oT_ready", 1)
        o_tok = env.sem("o_tok", 2)
        rinv_ready = env.sem("rinv_ready")
        on_ready = env.sem("on_ready", 3)
        onT_ps = env.sem("onT_ps", 1)
        onT_ready = env.sem("onT_ready")
        out_ps = env.sem("out_ps", 2)
        res_ready = env.sem("res_ready", 1)
        x_done = env.sem("x_done")
        warmed = env.sem("warmed", 1)
        block = env.block()
        W_ALL = 16 * 5
        FIRST = 8
        ROPE_STEP = (2, 3, 5, 6)

        @block.sync
        def _(sp):
            sp.sem_inc(stored.sem, stored.credit)
            xv = x_in.rearrange("b (t p) d -> p (b t) d", p=P)
            sp.dma_start(X[:, 0:FIRST, :], xv[:, 0:FIRST, :]).then_inc(x_first.sem, 16)
            sp.dma_start(wf[:, :, 0:3 * D], w_qkv.rearrange("(k p) n -> p k n", p=P)).then_inc(wf_loaded.sem, 16)
            sp.dma_start(ident[:], ident_in).then_inc(w_loaded.sem, 16)
            sp.dma_start(cs[:], rope).then_inc(w_loaded.sem, 16)
            for n in range(FIRST, TILES, FIRST):
                sp.dma_start(X[:, n:n + FIRST, :], xv[:, n:n + FIRST, :]).then_inc(x_loaded.sem, 16)
            sp.dma_start(wout[:], w_out.rearrange("(k p) n -> p k n", p=P)).then_inc(w_loaded.sem, 16)
            for t in range(QT):
                sp.dma_start(bout[:, t, :], b_out.rearrange("(a n) -> a n", a=1).broadcast_to([P, D])
                             ).then_inc(w_loaded.sem, 16)
            cv = context.rearrange("b (t p) d -> p (b t) d", p=P)
            for n in range(4):
                sp.dma_start(C[:, 8 * n:8 * n + 8, :], cv[:, 8 * n:8 * n + 8, :]).then_inc(c_loaded.sem, 16)
            sp.wait_ge(filled.sem, 3)

            def stack(b, n):
                half = n // 2
                pairs = slice(HP * half, HP * half + HP)
                sp.wait_ge(lo_ready.sem, lo_ready.at(4 * b + n + 1))
                sp.dma_start(qk_parts[n], parts[:, n % 2, :, :]).then_inc(stored.sem, 16)
                sp.wait_ge(stored.sem, stored.at(16 * (4 * b + n + 1)))
                for r in range(3):
                    if n % 2 == 0:
                        src = qk_parts[n, :, (0, 0, 1)[r], :].rearrange("(u a) s -> a u s", u=HP)
                        sp.dma_start(qs[32 * r:32 * r + 32, pairs, :], src).then_inc(q_stacked.sem, 16)
                    else:
                        src = qk_parts[n, :, (0, 1, 0)[r], :].rearrange("(u h j) s -> h j u s", u=HP, h=2)
                        for hh in range(2):
                            row = 32 * r + DH1 * hh
                            sp.dma_start(ks[row:row + DH1, pairs, hh, :], src[hh]).then_inc(k_stacked.sem, 16)

            with sp.Fori(0, B) as b:
                for n in range(4):
                    stack(b, n)

        @block.vector
        def _(dve):
            for c in (qk_mul, pT_dve, on_ready, res_ready):
                dve.sem_inc(c.sem, c.credit)
            nc.vector.memset(warm[:], 0.0).then_inc(filled.sem, 1)
            nc.vector.memset(v[:], 1.0).then_inc(filled.sem, 1)
            nc.vector.memset(ks[:], 0.0).then_inc(filled.sem, 1)

            def statistics(tiles, at, step_at):
                first, n = tiles.start, len(tiles)
                ln_statistics(nc, dve, env, lambda t: X[:, first + t, :], n, mv[:, first:first + n], stats, at)
                dve.wait_ge(stats.sem, at + 2 * n)
                own = slice(first, first + n)
                nc.vector.tensor_scalar(var[:, own], mv[:, own, 1], EPS, None, ALU.add).then_inc(stats.sem, 1)
                dve.wait_ge(std_ready.sem, 1 + (at > 0))
                refine_rsqrt(nc, dve, rstd[:, own], var[:, own], ntmp[:, own], step, step_at)

            dve.wait_ge(wf_loaded.sem, 16)
            for half in range(2):
                for k in range(2):
                    src = wf[:, k, 0:2 * D].rearrange("p (h j) -> p h j", j=DH1)
                    dst = wf[:, k, 3 * D:].rearrange("p (h j) -> p h j", j=DH1)
                    nc.vector.tensor_copy(dst[:, :, 8 * half:8 * half + 8],
                                          src[:, :, 8 - 8 * half:16 - 8 * half]).then_inc(wrot_ready.sem, 1)
            dve.wait_ge(x_first.sem, 16)
            statistics(range(FIRST), 0, 0)

            def split_weights():
                dve.wait_ge(wh_ready.sem, 1)
                nc.vector.scalar_tensor_tensor(wl[:].rearrange("p k n -> p (k n)"), wf[:].rearrange("p k n -> p (k n)"),
                                               W_SCALE, wh[:].rearrange("p k n -> p (k n)"), ALU.mult, ALU.subtract
                                               ).then_inc(wl_ready.sem, 1)

            def later_stats(b):
                for t in range(QT):
                    nc.vector.bn_stats(x_raw[:, bass.ds(QT * b + t, 1), :].rearrange("p a s -> p (a s)"),
                                       X[:, bass.ds(QT * b + t, 1), :].rearrange("p a d -> p (a d)"))

            def context_stats(b):
                for t in range(QT):
                    nc.vector.bn_stats(c_raw[:, bass.ds(QT * b + t, 1), :].rearrange("p a s -> p (a s)"),
                                       C[:, bass.ds(QT * b + t, 1), :].rearrange("p a d -> p (a d)"))

            def normalise(b):
                if not isinstance(b, int) or b > 0:
                    dve.wait_ge(xnT_ps.sem, xnT_ps.at(b))
                for t in range(QT):
                    nc.vector.tensor_scalar(xn[:, t, :], X[:, bass.ds(QT * b + t, 1), :].rearrange("p a d -> p (a d)"),
                                            mv[:, bass.ds(QT * b + t, 1), 0:1].rearrange("p a d -> p (a d)"),
                                            rstd[:, bass.ds(QT * b + t, 1)],
                                            ALU.subtract, ALU.mult).then_inc(xn_ready.sem, 1)

            def rope_mul(b, n):
                dve.wait_ge(qk_ps.sem, qk_ps.at(4 * b + n + 1))
                dve.wait_ge(qk_sum.sem, qk_sum.at(4 * b + n - 1))
                nc.vector.tensor_tensor(rt[:, n % 2, :], ps_p[n % 2][:], cs[:], ALU.mult).then_inc(qk_mul.sem, 1)

            def low_x(b):
                dve.wait_ge(xh_ready.sem, xh_ready.at(b + 1))
                nc.vector.scalar_tensor_tensor(xl[:].rearrange("p k s -> p (k s)"), ps_m[:], A_SCALE,
                                               xh[:].rearrange("p k s -> p (k s)"), ALU.mult, ALU.subtract
                                               ).then_inc(xT_ready.sem, 1)

            def maxima(b, u):
                for qt in range(QT):
                    dve.wait_ge(s_ps.sem, s_ps.at(16 * b + 2 * u + qt + 1))
                    nc.vector.tensor_reduce(smax[:, u % 2, qt, :], ps_s[qt][:].rearrange("p (h k) -> p h k", h=2),
                                            AX, ALU.max).then_inc(smax_ready.sem, 1)
                    dve.wait_ge(smax_ready.sem, smax_ready.at(16 * b + 2 * u + qt + 1))
                    nc.vector.tensor_scalar(nmax[:, u % 2, qt, :], smax[:, u % 2, qt, :], -S_SCALE, None, ALU.mult
                                            ).then_inc(nmax_ready.sem, 1)

            def evacuate_pT(b, u):
                h = 2 * u + 1
                dve.wait_ge(pT_ps.sem, pT_ps.at(16 * b + h + 1))
                dve.wait_ge(o_ps.sem, o_ps.at(4 * b + h // 4 - 1))
                nc.vector.tensor_copy(pT[:, h % 8, :, :], ps_t[1][:].rearrange("p (k q) -> p k q", k=2)
                                      ).then_inc(pT_dve.sem, 1)

            def over_sums(b, a):
                dve.wait_ge(o_tok.sem, o_tok.at(2 * b + a + 1))
                blocks = ps_m[:].rearrange("p (r c) -> p r c", c=2 * DH1)
                nc.vector.reciprocal(rinv[:], blocks[:, :, DH1]).then_inc(rinv_ready.sem, 1)
                dve.wait_ge(rinv_ready.sem, rinv_ready.at(2 * b + a + 1))
                dve.wait_ge(onT_ps.sem, onT_ps.at(b))
                for g in range(2):
                    rows = slice(QT * 4 * g, QT * 4 * (g + 1))
                    cols = slice((2 * a + g) * 4 * DH1, (2 * a + g + 1) * 4 * DH1)
                    ins = nc.vector.tensor_tensor(
                        on[:, :, cols].rearrange("p t (h j) -> p t h j", j=DH1),
                        blocks[:, rows, 0:DH1].rearrange("p (t h) j -> p t h j", t=QT),
                        rinv[:, rows].rearrange("p (t h) -> p t h", t=QT).unsqueeze(3).broadcast_to([P, QT, 4, DH1]),
                        ALU.mult)
                ins.then_inc(on_ready.sem, 1)

            def finish(b):
                dve.wait_ge(out_ps.sem, out_ps.at(b + 1))
                nc.vector.tensor_tensor(res[:], ps_m[:].rearrange("p (t d) -> p t d", t=QT), bout[:], ALU.add
                                        ).then_inc(res_ready.sem, 1)
                dve.wait_ge(res_ready.sem, res_ready.at(b + 1))
                nc.vector.tensor_tensor(X[:, bass.ds(QT * b, QT), :], X[:, bass.ds(QT * b, QT), :], res[:],
                                        ALU.add).then_inc(x_done.sem, 1)

            def body(b, before, more, ahead):
                for u in range(PAIRS):
                    maxima(b, u)
                    if u >= 1:
                        evacuate_pT(b, u - 1)
                    elif before:
                        evacuate_pT(b - 1, PAIRS - 1)
                    if more and u == 1:
                        low_x(b + 1)
                    if before and u == 2:
                        over_sums(b - 1, 1)
                    if before and u == 4:
                        finish(b - 1)
                    if more and u in ROPE_STEP:
                        rope_mul(b + 1, ROPE_STEP.index(u))
                    if u == 0:
                        context_stats(b)
                    if u == 3 and ahead:
                        normalise(b + 2)
                    if u == 6:
                        over_sums(b, 0)
                    if before and u == 7:
                        dve.wait_ge(x_done.sem, x_done.at(b))
                        later_stats(b - 1)

            normalise(0)
            split_weights()
            low_x(0)
            dve.wait_ge(w_loaded.sem, W_ALL)
            for n in range(4):
                rope_mul(0, n)
            normalise(1)
            dve.wait_ge(x_loaded.sem, 16 * (TILES // FIRST - 1))
            statistics(range(FIRST, TILES), 2 * FIRST + 1, 5)
            dve.wait_ge(c_loaded.sem, 64)
            body(0, False, True, True)
            with dve.Fori(1, B - 2) as b:
                body(b, True, True, True)
            body(B - 2, True, True, False)
            body(B - 1, True, False, False)
            evacuate_pT(B - 1, PAIRS - 1)
            over_sums(B - 1, 1)
            finish(B - 1)
            dve.wait_ge(x_done.sem, x_done.at(B))
            later_stats(B - 1)

        @block.gpsimd
        def _(pool):
            for c in (qk_sum, lo_ready):
                pool.sem_inc(c.sem, c.credit)

            def rope_add(b, n):
                pool.wait_ge(qk_mul.sem, qk_mul.at(4 * b + n + 1))
                pool.wait_ge(lo_ready.sem, lo_ready.at(4 * b + n - 1))
                nc.gpsimd.tensor_tensor(qkf[:, n % 2, :], rt[:, n % 2, 0:S], rt[:, n % 2, S:2 * S], ALU.add
                                        ).then_inc(qk_sum.sem, 1)
                pool.wait_ge(s_ps.sem, s_ps.at(16 * (b - 1) + 8 * (n // 2) + 8))
                pool.wait_ge(hi_ready.sem, hi_ready.at(4 * b + n + 1))
                nc.gpsimd.tensor_tensor(parts[:, n % 2, 1, :], qkf[:, n % 2, :], parts[:, n % 2, 0, :], ALU.subtract
                                        ).then_inc(lo_ready.sem, 1)

            with pool.Fori(0, B) as b:
                for n in range(4):
                    rope_add(b, n)

        @block.scalar
        def _(act):
            for c in (v_ready, exp_done, pT_act, oT_ready, warmed):
                act.sem_inc(c.sem, c.credit)

            def roots(tiles, at):
                act.wait_ge(stats.sem, at)
                nc.scalar.activation(rstd[:, tiles], var[:, tiles], ACT.Sqrt).then_inc(std_ready.sem, 1)

            act.wait_ge(wrot_ready.sem, 4)
            nc.scalar.activation(wh[:], wf[:], ACT.Copy, scale=W_SCALE).then_inc(wh_ready.sem, 1)
            roots(slice(0, FIRST), 2 * FIRST + 1)
            act.wait_ge(filled.sem, 2)

            def high_x(b):
                act.wait_ge(xnT_ps.sem, xnT_ps.at(b + 1))
                act.wait_ge(v_ps.sem, v_ps.at(b))
                nc.scalar.activation(xh[:], ps_m[:].rearrange("p (k s) -> p k s", k=2), ACT.Copy, scale=A_SCALE
                                     ).then_inc(xh_ready.sem, 1)

            def high_part(b, n):
                act.wait_ge(qk_sum.sem, qk_sum.at(4 * b + n + 1))
                act.wait_ge(stored.sem, stored.at(16 * (4 * b + n - 1)))
                nc.scalar.activation(parts[:, n % 2, 0, :], qkf[:, n % 2, :], ACT.Copy).then_inc(hi_ready.sem, 1)

            def evacuate_v(b):
                act.wait_ge(v_ps.sem, v_ps.at(b + 1))
                act.wait_ge(o_ps.sem, o_ps.at(4 * b))
                for t in range(QT):
                    ins = nc.scalar.activation(v[:, t, :, 0:DH1],
                                               ps_p[1][:, t * D:(t + 1) * D].rearrange("p (h j) -> p h j", h=H1), ACT.Copy,
                                               scale=PROJECTED)
                ins.then_inc(v_ready.sem, 1)

            def exponentials(b, u):
                for qt in range(QT):
                    act.wait_ge(nmax_ready.sem, nmax_ready.at(16 * b + 2 * u + qt + 1))
                    act.wait_ge(pT_ps.sem, pT_ps.at(16 * b + 2 * u - 2))
                    for hh in range(2):
                        nc.scalar.activation(prob[:, u % 2, qt, hh, :], ps_s[qt][:, hh * S:(hh + 1) * S], ACT.Exp,
                                             scale=S_SCALE, bias=nmax[:, u % 2, qt, hh:hh + 1]
                                             ).then_inc(exp_done.sem, 1)

            def evacuate_pT(b, u):
                h = 2 * u
                act.wait_ge(pT_ps.sem, pT_ps.at(16 * b + h + 1))
                act.wait_ge(o_ps.sem, o_ps.at(4 * b + h // 4 - 1))
                nc.scalar.activation(pT[:, h % 8, :, :], ps_t[0][:].rearrange("p (k q) -> p k q", k=2),
                                     ACT.Copy).then_inc(pT_act.sem, 1)

            def evacuate_o(b, g):
                act.wait_ge(o_ps.sem, o_ps.at(4 * b + g + 1))
                act.wait_ge(o_tok.sem, o_tok.at(2 * (b - 1) + g // 2 + 1))
                nc.scalar.activation(oT[:, g, :], ps_o[:, 0:S], ACT.Copy).then_inc(oT_ready.sem, 1)

            def evacuate_onT(b):
                act.wait_ge(onT_ps.sem, onT_ps.at(b + 1))
                act.wait_ge(out_ps.sem, out_ps.at(b))
                nc.scalar.activation(onT[:], ps_m[:].rearrange("p (k s) -> p k s", k=2), ACT.Copy
                                     ).then_inc(onT_ready.sem, 1)

            def load_table(b):
                act.wait_ge(warmed.sem, warmed.at(b))
                nc.scalar.activation(warm[:, 1:2], warm[:, 0:1], ACT.Exp).then_inc(warmed.sem, 1)

            def body(b, before, more):
                load_table(b)
                for u in range(PAIRS):
                    exponentials(b, u)
                    if u >= 1:
                        evacuate_pT(b, u - 1)
                    elif before:
                        evacuate_pT(b - 1, PAIRS - 1)
                    if more and u == 0:
                        high_x(b + 1)
                    if before and u == 1:
                        evacuate_o(b - 1, 3)
                    if u == 1:
                        evacuate_v(b)
                    if before and u == 3:
                        evacuate_onT(b - 1)
                    if u in (3, 5, 7):
                        evacuate_o(b, u // 2 - 1)
                    if more and u - 1 in ROPE_STEP:
                        high_part(b + 1, ROPE_STEP.index(u - 1))

            high_x(0)
            for n in range(4):
                high_part(0, n)
            roots(slice(FIRST, TILES), 2 * TILES + 2)
            body(0, False, True)
            with act.Fori(1, B - 1) as b:
                body(b, True, True)
            body(B - 1, True, False)
            evacuate_pT(B - 1, PAIRS - 1)
            evacuate_o(B - 1, 3)
            evacuate_onT(B - 1)

        @block.tensor
        def _(pe):
            for c in (v_ps, s_ps, pT_ps, o_ps, o_tok, onT_ps, out_ps):
                pe.sem_inc(c.sem, c.credit)
            pe.wait_ge(w_loaded.sem, W_ALL)

            def transpose_xn(b):
                pe.wait_ge(xn_ready.sem, xn_ready.at(2 * b + 2))
                pe.wait_ge(on_ready.sem, on_ready.at(2 * b - 3))
                for t in range(QT):
                    for k in range(2):
                        ins = pe.transpose(ps_m[:, k * S + t * P:k * S + (t + 1) * P], xn[:, t, k * P:(k + 1) * P],
                                           ident[:])
                ins.then_inc(xnT_ps.sem, 1)

            def project_qk(b, n):
                pe.wait_ge(qk_mul.sem, qk_mul.at(4 * b + n - 1))
                if n == 0:
                    pe.wait_ge(xT_ready.sem, xT_ready.at(b + 1))
                if n == 1:
                    pe.wait_ge(v_ready.sem, v_ready.at(b))
                col = (n % 2) * D + (n // 2) * P
                for j, first in enumerate((col, 3 * D + col)):
                    for part, (w, x) in enumerate(((wh, xh), (wl, xh), (wh, xl))):
                        for k in range(2):
                            ins = pe.matmul(ps_p[n % 2][:, j * S:(j + 1) * S], w[:, k, first:first + P], x[:, k, :],
                                            start=(part == 0 and k == 0), stop=(part == 2 and k == 1),
                                            skip_group_check=True)
                ins.then_inc(qk_ps.sem, 1)

            def project_v(b):
                pe.wait_ge(qk_mul.sem, qk_mul.at(4 * b + 4))
                for t in range(QT):
                    for part, (w, x) in enumerate(((wh, xh), (wl, xh), (wh, xl))):
                        for k in range(2):
                            ins = pe.matmul(ps_p[1][:, t * D:(t + 1) * D], x[:, k, t * P:(t + 1) * P],
                                            w[:, k, 2 * D:3 * D], start=(part == 0 and k == 0),
                                            stop=(part == 2 and k == 1), skip_group_check=True)
                ins.then_inc(v_ps.sem, 1)

            def scores(b, u, qt):
                half = u // HP
                if u % HP == 0 and qt == 0:
                    pe.wait_ge(q_stacked.sem, q_stacked.at(48 * (2 * b + half + 1)))
                    pe.wait_ge(k_stacked.sem, k_stacked.at(96 * (2 * b + half + 1)))
                pe.wait_ge(exp_done.sem, exp_done.at(32 * b + 4 * u + 2 * qt - 2))
                pe.matmul(ps_s[qt][:], qs[:, u, qt * P:(qt + 1) * P], ks[:, u, :, :].rearrange("p h k -> p (h k)"),
                          start=True, stop=True).then_inc(s_ps.sem, 1)

            def transpose_p(b, u, qt):
                pe.wait_ge(exp_done.sem, exp_done.at(32 * b + 4 * u + 2 * qt + 2))
                for hh in range(2):
                    if qt == 0:
                        read = pT_dve if hh else pT_act
                        pe.wait_ge(read.sem, read.at(8 * b + u))
                    for kt in range(2):
                        ins = pe.transpose(ps_t[hh][:, kt * S + qt * P:kt * S + (qt + 1) * P],
                                           prob[:, u % 2, qt, hh, kt * P:(kt + 1) * P], ident[:])
                    if qt == QT - 1:
                        ins.then_inc(pT_ps.sem, 1)

            def values(b, g):
                if g == 0:
                    pe.wait_ge(v_ready.sem, v_ready.at(b + 1))
                pe.wait_ge(pT_act.sem, pT_act.at(8 * b + 2 * g + 2))
                pe.wait_ge(pT_dve.sem, pT_dve.at(8 * b + 2 * g + 2))
                pe.wait_ge(oT_ready.sem, oT_ready.at(4 * b + g))
                for kt in range(2):
                    for j in range(4):
                        h = 4 * g + j
                        ins = pe.matmul(ps_o[32 * j:32 * j + 32, 0:S], v[:, kt, h, :], pT[:, h % 8, kt, :],
                                        start=(kt == 0), stop=(kt == 1), skip_group_check=True)
                ins.then_inc(o_ps.sem, 1)

            def outputs_to_tokens(b, a):
                pe.wait_ge(oT_ready.sem, oT_ready.at(4 * b + 2 * a + 2))
                if a:
                    pe.wait_ge(xT_ready.sem, xT_ready.at(min(b + 3, B) if isinstance(b, int) else b + 3))
                else:
                    pe.wait_ge(res_ready.sem, res_ready.at(b))
                for g in range(2):
                    for t in range(QT):
                        r = QT * g + t
                        ins = pe.transpose(ps_m[:, r * P:(r + 1) * P], oT[:, 2 * a + g, t * P:(t + 1) * P], ident[:])
                ins.then_inc(o_tok.sem, 1)

            def transpose_on(b):
                pe.wait_ge(on_ready.sem, on_ready.at(2 * b + 2))
                for t in range(QT):
                    for k in range(2):
                        ins = pe.transpose(ps_m[:, k * S + t * P:k * S + (t + 1) * P], on[:, t, k * P:(k + 1) * P],
                                           ident[:])
                ins.then_inc(onT_ps.sem, 1)

            def project_out(b):
                pe.wait_ge(onT_ready.sem, onT_ready.at(b + 1))
                for t in range(QT):
                    for k in range(2):
                        ins = pe.matmul(ps_m[:, t * D:(t + 1) * D], onT[:, k, t * P:(t + 1) * P], wout[:, k, :],
                                        start=(k == 0), stop=(k == 1), skip_group_check=True)
                ins.then_inc(out_ps.sem, 1)

            def body(b, before, more):
                for u in range(PAIRS):
                    for qt in range(QT):
                        scores(b, u, qt)
                    for qt in range(QT):
                        if u >= 1:
                            transpose_p(b, u - 1, qt)
                        elif before:
                            transpose_p(b - 1, PAIRS - 1, qt)
                    if u == 0:
                        project_v(b)
                    if more and u == 0:
                        transpose_xn(b + 1)
                    if before and u == 1:
                        values(b - 1, 3)
                    if before and u == 2:
                        outputs_to_tokens(b - 1, 1)
                    if before and u == 3:
                        transpose_on(b - 1)
                    if before and u == 4:
                        project_out(b - 1)
                    if u in (3, 5, 7):
                        values(b, u // 2 - 1)
                    if more and u in ROPE_STEP:
                        project_qk(b + 1, ROPE_STEP.index(u))
                    if u == 6:
                        outputs_to_tokens(b, 0)

            transpose_xn(0)
            pe.wait_ge(wl_ready.sem, 1)
            for n in range(4):
                project_qk(0, n)
            body(0, False, True)
            with pe.Fori(1, B - 1) as b:
                body(b, True, True)
            body(B - 1, True, False)
            for qt in range(QT):
                transpose_p(B - 1, PAIRS - 1, qt)
            values(B - 1, 3)
            outputs_to_tokens(B - 1, 1)
            transpose_on(B - 1)
            project_out(B - 1)


def cross_attention(nc, X, C, ident, x_raw, c_raw, media_w, media_b, lat_w, lat_b, Wq, Wk, Wv, Wout):
    PAIRS = H2 // 2
    S_SCALE2 = DH2 ** -0.5 / (Q_SCALE * K_SCALE)
    KT = KV // P
    with Env(nc, "p2") as env:
        wf = env.sb("wf", [P, 3, 2, INNER])
        wh = env.sb("wh", [P, 3, 2, INNER], F16)
        wl = env.sb("wl", [P, 3, 2, INNER], F16)
        wout = env.sb("wout", [P, PAIRS, D])
        woh = env.sb("woh", [P, PAIRS, D], F16)
        wol = env.sb("wol", [P, PAIRS, D], F16)
        affine = env.sb("affine", [P, 2, 2, 2])
        affine_s = env.sb("affine_s", [P, 2, 2, 2])
        warm = env.sb("warm", [P, 2])
        mv = env.sb("mv", [P, 2, TILES, 2])
        var = env.sb("var", [P, 2 * TILES])
        rstd = env.sb("rstd", [P, 2 * TILES])
        var2 = env.sb("var2", [P, TILES])
        rstd2 = env.sb("rstd2", [P, TILES])
        ntmp = env.sb("ntmp", [P, 2 * TILES])
        xn = env.sb("xn", [P, 2, QT, D])
        kvT = env.sb("kvT", [P, 2, KV])
        kvh = env.sb("kvh", [P, 2, KV], F16)
        kvl = env.sb("kvl", [P, 2, KV], F16)
        qp = env.sb("qp", [P, PAIRS, 2, S], F16)
        kp = env.sb("kp", [P, PAIRS, 2, KV], F16)
        qs = env.sb("qs", [P, H2, S], F16)
        ks = env.sb("ks", [P, H2, 2, KV], F16)
        v = env.sb("v", [P, KT, INNER])
        prob = env.sb("prob", [P, 2, QT, KV])
        smax = env.sb("smax", [P, 2, QT])
        nmax = env.sb("nmax", [P, 2, QT])
        rsum = env.sb("rsum", [P, 2, QT])
        rinv = env.sb("rinv", [P, 2, QT])
        pT = env.sb("pT", [P, 4, KT, S])
        oh = env.sb("oh", [P, PAIRS, S], F16)
        ol = env.sb("ol", [P, PAIRS, S], F16)

        ps_s = [env.psum(f"s{i}") for i in range(2)]
        ps_t = [env.psum(f"t{i}") for i in range(2)]
        ps_o = env.psum("o")
        ps_p = [env.psum(f"p{i}") for i in range(2)]
        ps_m = env.psum("m")

        loaded, zeroed = env.sem("loaded"), env.sem("zeroed")
        stats, std_ready, step = env.sem("stats"), env.sem("std_ready"), env.sem("step")
        xn_ready = env.sem("xn_ready")
        xnT_ps = env.sem("xnT_ps")
        kvT_ready = env.sem("kvT_ready", 2)
        kvh_ready = env.sem("kvh_ready")
        kvl_ready = env.sem("kvl_ready")
        q_ps = env.sem("q_ps")
        q_high = env.sem("q_high")
        q_low = env.sem("q_low", 1)
        k_ps = env.sem("k_ps")
        k_high = env.sem("k_high")
        k_low = env.sem("k_low", 1)
        stacked = [env.sem(f"stacked{g}", 128) for g in range(2)]
        v_ps = env.sem("v_ps", 4)
        v_ready = env.sem("v_ready", 1)
        smax_ready = env.sem("smax_ready")
        w_high, w_low = env.sem("w_high"), env.sem("w_low")
        warmed = env.sem("warmed", 1)
        s_ps = env.sem("s_ps", 16)
        nmax_ready = env.sem("nmax_ready")
        exp_done = env.sem("exp_done", 2)
        inv_ready = env.sem("inv_ready")
        prob_ready = env.sem("prob_ready")
        pT_ps = env.sem("pT_ps", 4)
        pT_act = env.sem("pT_act", 1)
        pT_dve = env.sem("pT_dve", 1)
        o_ps = env.sem("o_ps", 2)
        oh_ready = env.sem("oh_ready")
        oT_ready = env.sem("oT_ready", 1)
        out_ps = env.sem("out_ps", 1)
        x_done = env.sem("x_done", 2)
        block = env.block()
        LOADS = 16 * 12
        QK_STEPS = (3, 5, 6, 7)

        @block.sync
        def _(sp):
            for c in stacked:
                sp.sem_inc(c.sem, c.credit)
            for w, src in ((wf[:, 0], Wq), (wf[:, 1], Wk), (wf[:, 2], Wv), (wout[:], Wout)):
                sp.dma_start(w, src.rearrange("(k p) n -> p k n", p=P)).then_inc(loaded.sem, 16)
            for n, src in enumerate((media_w, media_b, lat_w, lat_b)):
                for k in range(2):
                    sp.dma_start(affine[:, n // 2, n % 2, k:k + 1],
                                 src[k * P:(k + 1) * P].rearrange("(p a) -> p a", a=1)).then_inc(loaded.sem, 16)

            def stack(b, g):
                sp.wait_ge(k_low.sem, k_low.at(4 * b + 2 * g + 2))
                for hh in range(2):
                    own = slice(DH2 * hh, DH2 * hh + DH2)
                    for r in range(2):
                        rows = slice(DH2 * r, DH2 * r + DH2)
                        to_q = qs[rows, 4 * g:4 * g + 4, :].rearrange("p (j h) s -> p h j s", h=2)[:, hh]
                        to_k = ks[rows, 4 * g:4 * g + 4, :, :].rearrange("p (j h) a s -> p h j (a s)", h=2)[:, hh]
                        sp.dma_start(to_q, qp[own, 2 * g:2 * g + 2, r, :]).then_inc(stacked[g].sem, 16)
                        sp.dma_start(to_k, kp[own, 2 * g:2 * g + 2, :, :].rearrange("p j a s -> p j (a s)")
                                     ).then_inc(stacked[g].sem, 16)

            with sp.Fori(0, B) as b:
                for g in range(2):
                    stack(b, g)

        @block.vector
        def _(dve):
            for c in (pT_dve, x_done, q_low, k_low, oT_ready):
                dve.sem_inc(c.sem, c.credit)
            nc.vector.memset(warm[:], 0.0).then_inc(zeroed.sem, 1)
            for a, raw in enumerate((c_raw, x_raw)):
                for t in range(TILES):
                    nc.vector.bn_aggr(mv[:, a, t, :], raw[:, t, :]).then_inc(stats.sem, 1)
            dve.wait_ge(stats.sem, 2 * TILES)
            nc.vector.tensor_scalar(var[:], mv[:].rearrange("p a t s -> p (a t) s")[:, :, 1], EPS, None, ALU.add
                                    ).then_inc(stats.sem, 1)
            dve.wait_ge(std_ready.sem, 1)
            refine_rsqrt(nc, dve, rstd[:], var[:], ntmp[:], step, 0)
            nc.vector.tensor_tensor(var2[:], rstd[:, TILES:], rstd[:, TILES:], ALU.mult).then_inc(step.sem, 1)
            dve.wait_ge(step.sem, 6)
            nc.vector.tensor_tensor(var2[:], var2[:], mv[:, 1, :, 1], ALU.mult).then_inc(step.sem, 1)
            dve.wait_ge(step.sem, 7)
            nc.vector.tensor_scalar(var2[:], var2[:], EPS, None, ALU.add).then_inc(step.sem, 1)
            dve.wait_ge(std_ready.sem, 2)
            refine_rsqrt(nc, dve, rstd2[:], var2[:], ntmp[:, 0:TILES], step, 8)
            nc.vector.tensor_tensor(rstd[:, TILES:], rstd[:, TILES:], rstd2[:], ALU.mult).then_inc(step.sem, 1)
            dve.wait_ge(step.sem, 14)

            def normalise(b):
                if not isinstance(b, int) or b > 0:
                    dve.wait_ge(xnT_ps.sem, xnT_ps.at(2 * b))
                for a, src in enumerate((C, X)):
                    for t in range(QT):
                        nc.vector.tensor_scalar(
                            xn[:, a, t, :], src[:, bass.ds(QT * b + t, 1), :].rearrange("p a d -> p (a d)"),
                            mv[:, a, bass.ds(QT * b + t, 1), 0:1].rearrange("p a d -> p (a d)"),
                            rstd[:, bass.ds(TILES * a + QT * b + t, 1)],
                            ALU.subtract, ALU.mult).then_inc(xn_ready.sem, 1)

            def low_parts(b, j):
                for ps, high, low, buf, psum, width, scale in (
                        (q_ps, q_high, q_low, qp, ps_p[0], S, Q_SCALE), (k_ps, k_high, k_low, kp, ps_p[1], KV, K_SCALE)):
                    dve.wait_ge(ps.sem, ps.at(4 * b + j + 1))
                    dve.wait_ge(high.sem, high.at(4 * b + j + 1))
                    nc.vector.scalar_tensor_tensor(buf[:, j, 1, :], psum[:, 0:width], PROJECTED * scale, buf[:, j, 0, :],
                                                   ALU.mult, ALU.subtract).then_inc(low.sem, 1)

            def maxima(b, h):
                for qt in range(QT):
                    dve.wait_ge(s_ps.sem, s_ps.at(16 * b + 2 * h + qt + 1))
                    nc.vector.tensor_reduce(smax[:, h % 2, qt:qt + 1], ps_s[qt][:], AX, ALU.max
                                            ).then_inc(smax_ready.sem, 1)
                    dve.wait_ge(smax_ready.sem, smax_ready.at(16 * b + 2 * h + qt + 1))
                    nc.vector.tensor_scalar(nmax[:, h % 2, qt:qt + 1], smax[:, h % 2, qt:qt + 1], -S_SCALE2, None, ALU.mult
                                            ).then_inc(nmax_ready.sem, 1)

            def divide(b, h):
                for qt in range(QT):
                    dve.wait_ge(exp_done.sem, exp_done.at(16 * b + 2 * h + qt + 1))
                    nc.vector.reciprocal(rinv[:, h % 2, qt:qt + 1], rsum[:, h % 2, qt:qt + 1]).then_inc(inv_ready.sem, 1)
                    dve.wait_ge(inv_ready.sem, inv_ready.at(16 * b + 2 * h + qt + 1))
                    nc.vector.tensor_scalar(prob[:, h % 2, qt, :], prob[:, h % 2, qt, :], rinv[:, h % 2, qt:qt + 1],
                                            None, ALU.mult).then_inc(prob_ready.sem, 1)

            def evacuate_pT(b, h):
                dve.wait_ge(pT_ps.sem, pT_ps.at(16 * b + 2 * h + 2))
                dve.wait_ge(o_ps.sem, o_ps.at(4 * b + h // 2 - 1))
                nc.vector.tensor_copy(pT[:, h % 4, 2:4, :], ps_t[1][:].rearrange("p (k q) -> p k q", k=2)
                                      ).then_inc(pT_dve.sem, 1)

            def low_output(b, j):
                dve.wait_ge(oh_ready.sem, oh_ready.at(4 * b + j + 1))
                nc.vector.scalar_tensor_tensor(ol[:, j, :], ps_o[:, 0:S], A_SCALE, oh[:, j, :], ALU.mult, ALU.subtract
                                               ).then_inc(oT_ready.sem, 1)

            def later_stats(b):
                for t in range(QT):
                    nc.vector.bn_stats(x_raw[:, bass.ds(QT * b + t, 1), :].rearrange("p a s -> p (a s)"),
                                       X[:, bass.ds(QT * b + t, 1), :].rearrange("p a d -> p (a d)"))

            def finish(b):
                dve.wait_ge(out_ps.sem, out_ps.at(b + 1))
                xb = X[:, bass.ds(QT * b, QT), :].rearrange("p t d -> p (t d)")
                nc.vector.scalar_tensor_tensor(xb, ps_m[:], PROJECTED, xb, ALU.mult, ALU.add).then_inc(x_done.sem, 1)

            def body(b, before, more, ahead):
                for u in range(H2):
                    maxima(b, u)
                    if before and u < 2:
                        low_output(b - 1, 2 + u)
                    if u == 6:
                        low_output(b, 1)
                    if u >= 1:
                        evacuate_pT(b, u - 1)
                    elif before:
                        evacuate_pT(b - 1, H2 - 1)
                    divide(b, u)
                    if ahead and u == 3:
                        normalise(b + 2)
                    if before and u == 4:
                        finish(b - 1)
                    if u == 4:
                        low_output(b, 0)
                    if more and u in QK_STEPS:
                        low_parts(b + 1, QK_STEPS.index(u))
                    if before and u == 6:
                        dve.wait_ge(x_done.sem, x_done.at(b))
                        later_stats(b - 1)

            normalise(0)
            dve.wait_ge(w_high.sem, 5)
            nc.vector.scalar_tensor_tensor(wl[:].rearrange("p w k n -> p (w k n)"), wf[:].rearrange("p w k n -> p (w k n)"),
                                           W_SCALE, wh[:].rearrange("p w k n -> p (w k n)"), ALU.mult, ALU.subtract
                                           ).then_inc(w_low.sem, 1)
            nc.vector.scalar_tensor_tensor(wol[:].rearrange("p j n -> p (j n)"), wout[:].rearrange("p j n -> p (j n)"),
                                           W_SCALE, woh[:].rearrange("p j n -> p (j n)"), ALU.mult, ALU.subtract
                                           ).then_inc(w_low.sem, 1)
            for j in range(PAIRS):
                low_parts(0, j)
            normalise(1)
            body(0, False, True, True)
            with dve.Fori(1, B - 2) as b:
                body(b, True, True, True)
            body(B - 2, True, True, False)
            body(B - 1, True, False, False)
            evacuate_pT(B - 1, H2 - 1)
            for j in (2, 3):
                low_output(B - 1, j)
            finish(B - 1)
            dve.wait_ge(x_done.sem, x_done.at(B))
            later_stats(B - 1)

        @block.gpsimd
        def _(pool):
            def low_part(b, a):
                cols = slice(a * S, (a + 1) * S)
                pool.wait_ge(kvh_ready.sem, kvh_ready.at(2 * b + a + 1))
                nc.gpsimd.tensor_tensor(kvl[:, :, cols], kvT[:, :, cols], kvh[:, :, cols], ALU.subtract
                                        ).then_inc(kvl_ready.sem, 1)

            with pool.Fori(0, B) as b:
                for a in range(2):
                    low_part(b, a)

        @block.scalar
        def _(act):
            for c in (kvT_ready, v_ready, exp_done, pT_act, warmed):
                act.sem_inc(c.sem, c.credit)
            act.wait_ge(stats.sem, 2 * TILES + 1)
            nc.scalar.activation(rstd[:], var[:], ACT.Sqrt).then_inc(std_ready.sem, 1)
            act.wait_ge(step.sem, 8)
            nc.scalar.activation(rstd2[:], var2[:], ACT.Sqrt).then_inc(std_ready.sem, 1)
            act.wait_ge(loaded.sem, LOADS)
            for n in range(3):
                nc.scalar.activation(wh[:, n], wf[:, n], ACT.Copy, scale=W_SCALE).then_inc(w_high.sem, 1)
            nc.scalar.activation(affine_s[:], affine[:], ACT.Copy, scale=A_SCALE).then_inc(w_high.sem, 1)
            nc.scalar.activation(woh[:], wout[:], ACT.Copy, scale=W_SCALE).then_inc(w_high.sem, 1)
            act.wait_ge(w_high.sem, 5)
            act.wait_ge(zeroed.sem, 1)

            def evacuate_kvT(b, a):
                act.wait_ge(xnT_ps.sem, xnT_ps.at(2 * b + a + 1))
                act.wait_ge(v_ps.sem, v_ps.at(4 * b))
                for k in range(2):
                    nc.scalar.activation(kvT[:, k, a * S:(a + 1) * S], ps_m[:, k * S:(k + 1) * S], ACT.Identity,
                                         scale=affine_s[:, a, 0, k:k + 1], bias=affine_s[:, a, 1, k:k + 1]
                                         ).then_inc(kvT_ready.sem, 1)
                act.wait_ge(kvT_ready.sem, kvT_ready.at(4 * b + 2 * a + 2))
                nc.scalar.activation(kvh[:, :, a * S:(a + 1) * S], kvT[:, :, a * S:(a + 1) * S], ACT.Copy
                                     ).then_inc(kvh_ready.sem, 1)

            def high_parts(b, j):
                for ps, high, buf, psum, width, scale in ((q_ps, q_high, qp, ps_p[0], S, Q_SCALE),
                                                          (k_ps, k_high, kp, ps_p[1], KV, K_SCALE)):
                    act.wait_ge(ps.sem, ps.at(4 * b + j + 1))
                    act.wait_ge(stacked[j // 2].sem, stacked[j // 2].at(128 * b))
                    nc.scalar.activation(buf[:, j, 0, :], psum[:, 0:width], ACT.Copy, scale=PROJECTED * scale
                                         ).then_inc(high.sem, 1)

            def evacuate_v(b, t):
                act.wait_ge(v_ps.sem, v_ps.at(4 * b + t + 1))
                act.wait_ge(o_ps.sem, o_ps.at(4 * b))
                nc.scalar.activation(v[:, t, :], ps_p[t % 2][:], ACT.Copy, scale=PROJECTED).then_inc(v_ready.sem, 1)

            def exponentials(b, h):
                for qt in range(QT):
                    act.wait_ge(nmax_ready.sem, nmax_ready.at(16 * b + 2 * h + qt + 1))
                    act.wait_ge(pT_ps.sem, pT_ps.at(16 * b + 2 * h - 2))
                    nc.scalar.activation(prob[:, h % 2, qt, :], ps_s[qt][:], ACT.Exp, scale=S_SCALE2, bias=nmax[:, h % 2, qt:qt + 1],
                                         accum_out=rsum[:, h % 2, qt:qt + 1]).then_inc(exp_done.sem, 1)

            def evacuate_pT(b, h):
                act.wait_ge(pT_ps.sem, pT_ps.at(16 * b + 2 * h + 1))
                act.wait_ge(o_ps.sem, o_ps.at(4 * b + h // 2 - 1))
                nc.scalar.activation(pT[:, h % 4, 0:2, :], ps_t[0][:].rearrange("p (k q) -> p k q", k=2),
                                     ACT.Copy).then_inc(pT_act.sem, 1)

            def evacuate_o(b, j):
                act.wait_ge(o_ps.sem, o_ps.at(4 * b + j + 1))
                act.wait_ge(out_ps.sem, out_ps.at(b))
                nc.scalar.activation(oh[:, j, :], ps_o[:, 0:S], ACT.Copy, scale=A_SCALE).then_inc(oh_ready.sem, 1)

            def load_table(b):
                act.wait_ge(warmed.sem, warmed.at(b))
                nc.scalar.activation(warm[:, 1:2], warm[:, 0:1], ACT.Exp).then_inc(warmed.sem, 1)

            def body(b, before, more):
                load_table(b)
                for u in range(H2):
                    exponentials(b, u)
                    if u >= 1:
                        evacuate_pT(b, u - 1)
                    elif before:
                        evacuate_pT(b - 1, H2 - 1)
                        evacuate_o(b - 1, 3)
                    if u < 2:
                        evacuate_v(b, 2 * u)
                        evacuate_v(b, 2 * u + 1)
                    if u in (5, 7):
                        evacuate_o(b, u // 2 - 1)
                    if more and u in (1, 2):
                        evacuate_kvT(b + 1, u - 1)
                    if more and u in QK_STEPS:
                        high_parts(b + 1, QK_STEPS.index(u))
                    if u == 4:
                        evacuate_o(b, 0)

            evacuate_kvT(0, 0)
            evacuate_kvT(0, 1)
            for j in range(PAIRS):
                high_parts(0, j)
            body(0, False, True)
            with act.Fori(1, B - 1) as b:
                body(b, True, True)
            body(B - 1, True, False)
            evacuate_pT(B - 1, H2 - 1)
            evacuate_o(B - 1, 3)

        @block.tensor
        def _(pe):
            for c in (v_ps, s_ps, pT_ps, o_ps, out_ps):
                pe.sem_inc(c.sem, c.credit)
            pe.wait_ge(loaded.sem, LOADS)

            def transpose_xn(b, a):
                pe.wait_ge(xn_ready.sem, xn_ready.at(4 * b + 2 * a + 2))
                pe.wait_ge(x_done.sem, x_done.at(b - 2))
                pe.wait_ge(kvT_ready.sem, kvT_ready.at(4 * b + 2 * a))
                for t in range(QT):
                    for k in range(2):
                        ins = pe.transpose(ps_m[:, k * S + t * P:k * S + (t + 1) * P], xn[:, a, t, k * P:(k + 1) * P],
                                           ident[:])
                ins.then_inc(xnT_ps.sem, 1)

            def project_qk(b, j):
                pairs = slice(j * P, (j + 1) * P)
                pe.wait_ge(kvh_ready.sem, kvh_ready.at(2 * b + 2))
                pe.wait_ge(kvl_ready.sem, kvl_ready.at(2 * b + 2))
                pe.wait_ge(q_low.sem, q_low.at(4 * b + j))
                pe.wait_ge(v_ready.sem, v_ready.at(4 * b))
                for n, (w, x) in enumerate(((wh, kvh), (wl, kvh), (wh, kvl))):
                    for k in range(2):
                        ins = pe.matmul(ps_p[0][:, 0:S], w[:, 0, k, pairs], x[:, k, S:KV],
                                        start=(n == 0 and k == 0), stop=(n == 2 and k == 1))
                ins.then_inc(q_ps.sem, 1)
                pe.wait_ge(k_low.sem, k_low.at(4 * b + j))
                for n, (w, x) in enumerate(((wh, kvh), (wl, kvh), (wh, kvl))):
                    for k in range(2):
                        ins = pe.matmul(ps_p[1][:], w[:, 1, k, pairs], x[:, k, :],
                                        start=(n == 0 and k == 0), stop=(n == 2 and k == 1))
                ins.then_inc(k_ps.sem, 1)

            def project_v(b, tiles):
                for t in tiles:
                    if t < 2:
                        last = k_low if t else q_low
                        pe.wait_ge(last.sem, last.at(4 * (b + 1)))
                    else:
                        pe.wait_ge(v_ready.sem, v_ready.at(4 * b + t - 1))
                    for n, (w, x) in enumerate(((wh, kvh), (wl, kvh), (wh, kvl))):
                        for k in range(2):
                            ins = pe.matmul(ps_p[t % 2][:], x[:, k, t * P:(t + 1) * P], w[:, 2, k, :],
                                            start=(n == 0 and k == 0), stop=(n == 2 and k == 1))
                    ins.then_inc(v_ps.sem, 1)

            def scores(b, h, qt):
                if h % 4 == 0 and qt == 0:
                    pe.wait_ge(stacked[h // 4].sem, stacked[h // 4].at(128 * (b + 1)))
                pe.wait_ge(exp_done.sem, exp_done.at(16 * b + 2 * h + qt - 1))
                for part in range(2):
                    ins = pe.matmul(ps_s[qt][:], qs[:, h, qt * P:(qt + 1) * P], ks[:, h, part, :],
                                    start=(part == 0), stop=(part == 1))
                ins.then_inc(s_ps.sem, 1)

            def transpose_p(b, h, qt):
                pe.wait_ge(prob_ready.sem, prob_ready.at(16 * b + 2 * h + qt + 1))
                for kk in range(2):
                    if qt == 0:
                        read = pT_dve if kk else pT_act
                        pe.wait_ge(read.sem, read.at(8 * b + h))
                    for k in range(2):
                        kt = 2 * kk + k
                        ins = pe.transpose(ps_t[kk][:, k * S + qt * P:k * S + (qt + 1) * P],
                                           prob[:, h % 2, qt, kt * P:(kt + 1) * P], ident[:])
                    if qt == QT - 1:
                        ins.then_inc(pT_ps.sem, 1)

            def values(b, j):
                if j == 0:
                    pe.wait_ge(v_ready.sem, v_ready.at(4 * b + 4))
                pe.wait_ge(pT_act.sem, pT_act.at(8 * b + 2 * j + 2))
                pe.wait_ge(pT_dve.sem, pT_dve.at(8 * b + 2 * j + 2))
                pe.wait_ge(oT_ready.sem, oT_ready.at(4 * b + j))
                for kt in range(KT):
                    for hh in range(2):
                        h = 2 * j + hh
                        ins = pe.matmul(ps_o[DH2 * hh:DH2 * hh + DH2, 0:S], v[:, kt, h * DH2:(h + 1) * DH2],
                                        pT[:, h % 4, kt, :], start=(kt == 0), stop=(kt == KT - 1), skip_group_check=True)
                ins.then_inc(o_ps.sem, 1)

            def project_out(b):
                pe.wait_ge(oT_ready.sem, oT_ready.at(4 * b + 4))
                pe.wait_ge(kvT_ready.sem, kvT_ready.at(min(4 * b + 8, 4 * B) if isinstance(b, int) else 4 * b + 8))
                for t in range(QT):
                    for j in range(PAIRS):
                        for n, (w, x) in enumerate(((woh, oh), (wol, oh), (woh, ol))):
                            ins = pe.matmul(ps_m[:, t * D:(t + 1) * D], x[:, j, t * P:(t + 1) * P], w[:, j, :],
                                            start=(j == 0 and n == 0), stop=(j == PAIRS - 1 and n == 2),
                                            skip_group_check=True)
                ins.then_inc(out_ps.sem, 1)

            def body(b, before, more):
                for u in range(H2):
                    for qt in range(QT):
                        scores(b, u, qt)
                        if more and u == 2 and qt == 1:
                            transpose_xn(b + 1, 1)
                        if u >= 1:
                            transpose_p(b, u - 1, qt)
                        elif before:
                            transpose_p(b - 1, H2 - 1, qt)
                    if u < 2:
                        project_v(b, (2 * u, 2 * u + 1))
                    if before and u == 0:
                        values(b - 1, 3)
                    if more and u == 1:
                        transpose_xn(b + 1, 0)
                    if before and u == 4:
                        project_out(b - 1)
                    if u in (3, 5, 7):
                        values(b, u // 2 - 1)
                    if more and u in QK_STEPS:
                        project_qk(b + 1, QK_STEPS.index(u))

            transpose_xn(0, 0)
            transpose_xn(0, 1)
            pe.wait_ge(w_low.sem, 2)
            for j in range(PAIRS):
                project_qk(0, j)
            body(0, False, True)
            with pe.Fori(1, B - 1) as b:
                body(b, True, True)
            body(B - 1, True, False)
            for qt in range(QT):
                transpose_p(B - 1, H2 - 1, qt)
            values(B - 1, 3)
            project_out(B - 1)


H_SCALE = 16.0


def ffn(nc, X, ident, x_raw, b1_parts, h_parts, gates_t, Wm, bm, expert_emb, rank, W1, b1, W2, b2, Wo, bo, fold_in, out):
    G4 = E // 4
    K1 = 3 * HD
    GROUPS = HF * G4
    HIDDEN = HF * E
    G = CT_ * HF
    with Env(nc, "p3") as env:
        wm = env.sb("wm", [P, 2, D])
        bias = env.sb("bias", [P, 2])
        bias_s = env.sb("bias_s", [P, 2])
        emb = env.sb("emb", [P, 4 * E])
        rk = env.sb("rk", [P, E])
        mv = env.sb("mv", [P, TILES, 2])
        var = env.sb("var", [P, TILES])
        rstd = env.sb("rstd", [P, TILES])
        ntmp = env.sb("ntmp", [P, TILES])
        xn = env.sb("xn", [P, CT_, D])
        xnT = env.sb("xnT", [P, 2, CH])
        hf = env.sb("hf", [P, 2, CH])
        hs = env.sb("hs", [P, 2, CH])
        hi = env.sb("hi", [P, 2, CH], F16)
        lo = env.sb("lo", [P, 2, CH], F16)
        w = env.sb("w", [P, G, E])
        w_rest = env.sb("w_rest", [P, G, E])
        top = env.sb("top", [P, G])
        eq = env.sb("eq", [P, G, E])
        hot = env.sb("hot", [P, 2, G, E])
        den = env.sb("den", [P, G])
        gates = env.sb("gates", [P, CT_, HF * E])
        gT = env.sb("gT", [P, CH])

        w1h = env.sb("w1h", [K1, E, I], F16)
        w1 = env.sb("w1", [K1 + 3, E, I], F16)
        b1f = env.sb("b1f", [E, 2, I])
        b1p = env.sb("b1p", [E, 3, I], F16)
        w2 = env.sb("w2", [P, E, HD])
        b2c = env.sb("b2c", [P, G4])
        wo = env.sb("wo", [P, 2, D])
        bob = env.sb("bob", [P, 2, D])
        fold = env.sb("fold", [P, HD])
        hx = env.sb("hx", [K1 + 3, HF, CH], F16)
        gb = env.sb("gb", [P, 2, G4, CH])
        act_out = env.sb("act_out", [P, 8, CH])
        pr = env.sb("pr", [P, 2, G4, CH])
        half = env.sb("half", [P, 2, CH])
        sums = env.sb("sums", [P, 8, CH])
        comb = env.sb("comb", [P, 2, CH])
        y = env.sb("y", [P, 2, 2, D])
        w1f = sums[0:K1, 0:E * I // CH].rearrange("p a (e i) -> p (a e) i", i=I)

        ps_f = env.psum("f")
        ps_u = [env.psum(f"u{i}") for i in range(4)]
        ps_e = [env.psum(f"e{i}") for i in range(2)]
        ps_y = env.psum("y")

        loaded, zeroed = env.sem("loaded"), env.sem("zeroed")
        stats, std_ready, step = env.sem("stats"), env.sem("std_ready"), env.sem("step")
        xn_ready = env.sem("xn_ready")
        xnT_ps = env.sem("xnT_ps")
        xnT_ready = env.sem("xnT_ready")
        h_ps = env.sem("h_ps", 2)
        hf_ready = env.sem("hf_ready")
        hs_ready = env.sem("hs_ready")
        hi_ready = env.sem("hi_ready")
        lo_ready = env.sem("lo_ready", 2)
        logits_ps = env.sem("logits_ps", 1)
        less_max = env.sem("less_max", 1)
        exp_done = env.sem("exp_done")
        top_step = env.sem("top_step")
        gT_ps = env.sem("gT_ps", 1)
        gT_ready = env.sem("gT_ready", 1)
        hi_stored, lo_stored = env.sem("hi_stored", 16), env.sem("lo_stored", 16)
        gT_stored = env.sem("gT_stored", 16)

        w_loaded, prep = env.sem("w_loaded"), env.sem("prep")
        b1_stored, b1_placed = env.sem("b1_stored"), env.sem("b1_placed")
        w1_high, w1_low, ones_ready = env.sem("w1_high"), env.sem("w1_low"), env.sem("ones_ready")
        hx_loaded = [env.sem(f"hx_loaded{h}") for h in range(HF)]
        gb_loaded = [env.sem(f"gb_loaded{i}") for i in range(2)]
        u_ps = env.sem("u_ps")
        gelu_done = env.sem("gelu_done", 4)
        e_ps = env.sem("e_ps", 2)
        pr_ready = env.sem("pr_ready", 8)
        half_ready = env.sem("half_ready")
        sum_ready = env.sem("sum_ready", 8)
        c_ps = env.sem("c_ps", 2)
        comb_ready = env.sem("comb_ready", 1)
        y_ps = env.sem("y_ps", 2)
        y_part = env.sem("y_part", 1)
        y_ready = env.sem("y_ready")
        y_stored = [env.sem(f"y_stored{i}", 16) for i in range(2)]
        block = env.block()
        LOADS = 16 * (2 + 2 + 4)
        W_LOADS = 16 * (3 + 1 + 1 + 4 + 1 + 2 + 1)
        TOP = 17
        OUT_STEPS = (16, 16, 16, 16, 20, 21, 22, 23)

        @block.sync
        def _(sp):
            sp.wait_ge(zeroed.sem, 1)
            sp.dma_start(wm[:], Wm.rearrange("(k p) n -> p k n", p=P)).then_inc(loaded.sem, 16)
            sp.dma_start(rk[:], rank).then_inc(loaded.sem, 16)
            for m in range(2):
                sp.dma_start(bias[:, m:m + 1], bm[m * P:(m + 1) * P].rearrange("(p a) -> p a", a=1)
                             ).then_inc(loaded.sem, 16)
            for j in range(4):
                sp.dma_start(emb[HD * j:HD * (j + 1), E * j:E * (j + 1)], expert_emb).then_inc(loaded.sem, 16)
            for r in range(3):
                sp.dma_start(w1f[HD * r:HD * (r + 1), :, :], W1.rearrange("e d i -> d e i")).then_inc(w_loaded.sem, 16)
            sp.dma_start(b1f[:, 0, :], b1).then_inc(w_loaded.sem, 16)
            sp.dma_start(w2[:], W2.rearrange("e i o -> i e o")).then_inc(w_loaded.sem, 16)
            for j in range(4):
                sp.dma_start(b2c[HD * j:HD * (j + 1), :], b2.rearrange("(g j) o -> j o g", j=4)[j],
                             allow_slow_non_contiguous=True).then_inc(w_loaded.sem, 16)
            sp.dma_start(wo[:], Wo.rearrange("(k p) n -> p k n", p=P)).then_inc(w_loaded.sem, 16)
            for t in range(2):
                sp.dma_start(bob[:, t, :], bo.rearrange("(a n) -> a n", a=1).broadcast_to([P, D])
                             ).then_inc(w_loaded.sem, 16)
            sp.dma_start(fold[:], fold_in).then_inc(w_loaded.sem, 16)

            def store_h(c):
                for n, (buf, ready, stored) in enumerate(((hi, hi_ready, hi_stored), (lo, lo_ready, lo_stored))):
                    sp.wait_ge(ready.sem, ready.at(2 * c + 2))
                    sp.dma_start(h_parts[n].rearrange("(m p) t -> p m t", p=P)[:, :, bass.ds(CH * c, CH)], buf[:]
                                 ).then_inc(stored.sem, 16)

            def load_h(c, h):
                for r, part in enumerate((0, 1, 0)):
                    if h == 0 and r < 2:
                        stored = (hi_stored, lo_stored)[r]
                        sp.wait_ge(stored.sem, stored.at(16 * (c + 1)))
                    sp.dma_start(hx[HD * r:HD * (r + 1), h, :],
                                 h_parts[part][HD * h:HD * (h + 1), bass.ds(CH * c, CH)]).then_inc(hx_loaded[h].sem, 16)

            def load_gates(c, h):
                sp.wait_ge(pr_ready.sem, pr_ready.at(GROUPS * c + G4 * (h - 1)))
                for j in range(4):
                    src = gates_t.rearrange("(h g j) t -> h j g t", h=HF, j=4)[h, j, :, bass.ds(CH * c, CH)]
                    sp.dma_start(gb[HD * j:HD * (j + 1), h % 2, :, :], src.unsqueeze(0).broadcast_to([HD, G4, CH])
                                 ).then_inc(gb_loaded[h % 2].sem, 16)

            ov = out.rearrange("b (t p) d -> p (b t) d", p=P)

            def store_y(c, n):
                sp.wait_ge(y_ready.sem, y_ready.at(2 * c + n + 1))
                sp.dma_start(ov[:, bass.ds(CT_ * c + 2 * n, 2), :], y[:, n, :, :]).then_inc(y_stored[n].sem, 16)

            for c in (*y_stored, hi_stored, lo_stored):
                sp.sem_inc(c.sem, c.credit)
            sp.wait_ge(prep.sem, 6)
            sp.dma_start(b1_parts.rearrange("r e i -> e r i"), b1p[:]).then_inc(b1_stored.sem, 16)
            sp.wait_ge(b1_stored.sem, 16)
            sp.dma_start(w1[K1:K1 + 3, :, :], b1_parts).then_inc(b1_placed.sem, 16)
            store_h(0)
            for h in range(HF):
                load_h(0, h)

            def body(c, before, more):
                for h in range(HF):
                    load_gates(c, h)
                    if before and h < 2:
                        load_h(c, HF - 2 + h)
                    if more and h >= 4:
                        if h == 4:
                            store_h(c + 1)
                            load_h(c + 1, 0)
                            load_h(c + 1, 1)
                        if h == HF - 1:
                            sp.wait_ge(gT_stored.sem, gT_stored.at(16 * (c + 2)))
                        load_h(c + 1, h - 2)
                    if before and h in (5, 6):
                        store_y(c - 1, h - 5)

            sp.wait_ge(gT_stored.sem, gT_stored.at(16))
            body(0, False, True)
            with sp.Fori(1, CHUNKS - 1) as c:
                body(c, True, True)
            body(CHUNKS - 1, True, False)
            for n in range(2):
                store_y(CHUNKS - 1, n)
            for n in range(2):
                sp.wait_ge(y_stored[n].sem, y_stored[n].at(16 * CHUNKS))

        @block.gpsimd
        def _(pool):
            for c in (lo_ready, sum_ready):
                pool.sem_inc(c.sem, c.credit)

            def low_parts(c):
                for m in range(2):
                    pool.wait_ge(hi_ready.sem, hi_ready.at(2 * c + m + 1))
                    pool.wait_ge(lo_stored.sem, lo_stored.at(16 * c))
                    nc.gpsimd.tensor_tensor(lo[:, m, :], hs[:, m, :], hi[:, m, :], ALU.subtract
                                            ).then_inc(lo_ready.sem, 1)

            def add_groups(c, h):
                pool.wait_ge(pr_ready.sem, pr_ready.at(GROUPS * c + G4 * (h + 1)))
                pool.wait_ge(sum_ready.sem, sum_ready.at(8 * c + h))
                nc.gpsimd.tensor_tensor(half[:], pr[:, h % 2, 0:2, :], pr[:, h % 2, 2:4, :], ALU.add
                                        ).then_inc(half_ready.sem, 1)
                pool.wait_ge(half_ready.sem, half_ready.at(8 * c + h + 1))
                pool.wait_ge(c_ps.sem, c_ps.at(2 * c + h // 4 - 1))
                nc.gpsimd.tensor_tensor(sums[:, h, :], half[:, 0, :], half[:, 1, :], ALU.add
                                        ).then_inc(sum_ready.sem, 1)

            def body(c, more):
                for h in range(HF):
                    add_groups(c, h)
                    if more and h == 1:
                        low_parts(c + 1)

            nc.gpsimd.memset(hx[K1:K1 + 3, :, :], H_SCALE).then_inc(ones_ready.sem, 1)
            pool.wait_ge(ones_ready.sem, 1)
            low_parts(0)
            with pool.Fori(0, CHUNKS - 1) as c:
                body(c, True)
            body(CHUNKS - 1, False)

        @block.vector
        def _(dve):
            for c in (less_max, pr_ready, comb_ready, y_part):
                dve.sem_inc(c.sem, c.credit)
            nc.vector.memset(emb[:], 0.0).then_inc(zeroed.sem, 1)
            for t in range(TILES):
                nc.vector.bn_aggr(mv[:, t, :], x_raw[:, t, :]).then_inc(stats.sem, 1)
            dve.wait_ge(stats.sem, TILES)
            nc.vector.tensor_scalar(var[:], mv[:, :, 1], EPS, None, ALU.add).then_inc(stats.sem, 1)
            dve.wait_ge(std_ready.sem, 1)
            refine_rsqrt(nc, dve, rstd[:], var[:], ntmp[:], step, 0)

            def normalise(c, tiles):
                if not isinstance(c, int) or c > 0:
                    dve.wait_ge(xnT_ps.sem, xnT_ps.at(2 * c))
                for t in tiles:
                    nc.vector.tensor_scalar(xn[:, t, :], X[:, bass.ds(CT_ * c + t, 1), :].rearrange("p a d -> p (a d)"),
                                            mv[:, bass.ds(CT_ * c + t, 1), 0:1].rearrange("p a d -> p (a d)"),
                                            rstd[:, bass.ds(CT_ * c + t, 1)],
                                            ALU.subtract, ALU.mult).then_inc(xn_ready.sem, 1)

            def wide(a):
                return a.unsqueeze(2).broadcast_to([P, G, E])

            def selected(c, n):
                dve.wait_ge(top_step.sem, top_step.at(TOP * c + n))

            def less_maximum(c):
                logits = ps_f[:].rearrange("p (g e) -> p g e", e=E)
                dve.wait_ge(logits_ps.sem, logits_ps.at(c + 1))
                nc.vector.tensor_reduce(top[:], logits, AX, ALU.max).then_inc(top_step.sem, 1)
                selected(c, 1)
                nc.vector.tensor_tensor(w[:], logits, wide(top[:]), ALU.subtract).then_inc(less_max.sem, 1)

            def softmax(c):
                dve.wait_ge(exp_done.sem, exp_done.at(c + 1))
                nc.vector.tensor_reduce(den[:], w[:], AX, ALU.add).then_inc(top_step.sem, 1)
                selected(c, 2)
                nc.vector.reciprocal(den[:], den[:]).then_inc(top_step.sem, 1)
                selected(c, 3)
                nc.vector.tensor_tensor(w[:], w[:], wide(den[:]), ALU.mult).then_inc(top_step.sem, 1)
                selected(c, 4)

            def mark_largest(c, n):
                at = 4 + 6 * n
                src = w_rest if n else w
                nc.vector.tensor_reduce(top[:], src[:], AX, ALU.max).then_inc(top_step.sem, 1)
                selected(c, at + 1)
                nc.vector.tensor_tensor(eq[:], src[:], wide(top[:]), ALU.is_equal).then_inc(top_step.sem, 1)
                selected(c, at + 2)
                nc.vector.tensor_tensor(eq[:], eq[:], rk[:].unsqueeze(1).broadcast_to([P, G, E]), ALU.mult
                                        ).then_inc(top_step.sem, 1)
                selected(c, at + 3)

            def choose(c, n):
                at = 7 + 6 * n
                nc.vector.tensor_reduce(top[:], eq[:], AX, ALU.max).then_inc(top_step.sem, 1)
                selected(c, at + 1)
                nc.vector.tensor_tensor(hot[:, n], eq[:], wide(top[:]), ALU.is_equal).then_inc(top_step.sem, 1)
                selected(c, at + 2)
                if n == 0:
                    nc.vector.scalar_tensor_tensor(w_rest[:].rearrange("p g e -> p (g e)"),
                                                   hot[:, 0].rearrange("p g e -> p (g e)"), -2.0,
                                                   w[:].rearrange("p g e -> p (g e)"), ALU.mult, ALU.add
                                                   ).then_inc(top_step.sem, 1)
                    selected(c, at + 3)

            def make_gates(c):
                nc.vector.tensor_tensor(eq[:], hot[:, 0], hot[:, 1], ALU.add).then_inc(top_step.sem, 1)
                selected(c, TOP - 1)
                dve.wait_ge(gT_ps.sem, gT_ps.at(c))
                nc.vector.tensor_tensor(gates[:].rearrange("p t (h e) -> p (t h) e", e=E), eq[:], w[:], ALU.mult
                                        ).then_inc(top_step.sem, 1)
                selected(c, TOP)

            def gate(c, n):
                h, g = divmod(n, G4)
                dve.wait_ge(e_ps.sem, e_ps.at(GROUPS * c + n + 1))
                if g == 0:
                    dve.wait_ge(gb_loaded[h % 2].sem, 64 * (4 * c + h // 2 + 1))
                    dve.wait_ge(sum_ready.sem, sum_ready.at(8 * c + h - 1))
                nc.vector.scalar_tensor_tensor(pr[:, h % 2, g, :], ps_e[n % 2][:], b2c[:, g:g + 1], gb[:, h % 2, g, :],
                                               ALU.add, ALU.mult).then_inc(pr_ready.sem, 1)

            def evacuate_comb(c, q):
                dve.wait_ge(c_ps.sem, c_ps.at(2 * c + q + 1))
                dve.wait_ge(y_ps.sem, y_ps.at(2 * c))
                nc.vector.tensor_copy(comb[:, q, :], ps_y[:]).then_inc(comb_ready.sem, 1)

            def finish(c, n):
                dve.wait_ge(y_ps.sem, y_ps.at(2 * c + n + 1))
                dve.wait_ge(y_stored[n].sem, y_stored[n].at(16 * c))
                nc.vector.tensor_tensor(y[:, n, :, :], ps_y[:].rearrange("p (t d) -> p t d", t=2), bob[:], ALU.add
                                        ).then_inc(y_part.sem, 1)
                dve.wait_ge(y_part.sem, y_part.at(2 * c + n + 1))
                nc.vector.tensor_tensor(y[:, n, :, :], y[:, n, :, :], X[:, bass.ds(CT_ * c + 2 * n, 2), :], ALU.add
                                        ).then_inc(y_ready.sem, 1)

            def body(c, before, more, ahead):
                for n in range(GROUPS):
                    gate(c, n)
                    if more:
                        if ahead and n == 28:
                            normalise(c + 2, range(CT_))
                        if n == 14:
                            less_maximum(c + 1)
                        if n == 16:
                            softmax(c + 1)
                        if n in (17, 21):
                            mark_largest(c + 1, (n - 17) // 4)
                        if n in (19, 23):
                            choose(c + 1, (n - 19) // 4)
                        if n == 25:
                            make_gates(c + 1)
                    if before and n == 12:
                        evacuate_comb(c - 1, 1)
                    if before and n in (18, 23):
                        finish(c - 1, (n - 18) // 5)
                    if n == 26:
                        evacuate_comb(c, 0)

            normalise(0, range(CT_))
            dve.wait_ge(w_loaded.sem, W_LOADS)
            nc.vector.tensor_scalar(b1f[:, 0, :], b1f[:, 0, :], W_SCALE, None, ALU.mult).then_inc(prep.sem, 1)
            dve.wait_ge(prep.sem, 1)
            for r in range(3):
                nc.vector.tensor_copy(b1p[:, r, :], b1f[:, r % 2, :]).then_inc(prep.sem, 1)
                dve.wait_ge(prep.sem, 2 + 2 * r)
                if r < 2:
                    nc.vector.tensor_tensor(b1f[:, (r + 1) % 2, :], b1f[:, r % 2, :], b1p[:, r, :], ALU.subtract
                                            ).then_inc(prep.sem, 1)
                    dve.wait_ge(prep.sem, 3 + 2 * r)
            dve.wait_ge(w1_high.sem, 2)
            nc.vector.scalar_tensor_tensor(w1[2 * HD:K1].rearrange("p e i -> p (e i)"),
                                           w1f[2 * HD:K1].rearrange("p e i -> p (e i)"), W_SCALE,
                                           w1h[2 * HD:K1].rearrange("p e i -> p (e i)"), ALU.mult, ALU.subtract
                                           ).then_inc(w1_low.sem, 1)
            dve.wait_ge(w1_low.sem, 1)
            dve.wait_ge(loaded.sem, LOADS)
            less_maximum(0)
            softmax(0)
            for n in range(2):
                mark_largest(0, n)
                choose(0, n)
            make_gates(0)
            normalise(1, range(CT_))
            body(0, False, True, True)
            with dve.Fori(1, CHUNKS - 2) as c:
                body(c, True, True, True)
            body(CHUNKS - 2, True, True, False)
            body(CHUNKS - 1, True, False, False)
            evacuate_comb(CHUNKS - 1, 1)
            for n in range(2):
                finish(CHUNKS - 1, n)

        @block.scalar
        def _(act):
            for c in (gT_ready, gT_stored, gelu_done):
                act.sem_inc(c.sem, c.credit)
            act.wait_ge(stats.sem, TILES + 1)
            nc.scalar.activation(rstd[:], var[:], ACT.Sqrt).then_inc(std_ready.sem, 1)
            act.wait_ge(loaded.sem, LOADS)
            nc.scalar.activation(bias_s[:], bias[:], ACT.Copy, scale=H_SCALE).then_inc(std_ready.sem, 1)
            act.wait_ge(std_ready.sem, 2)

            def evacuate_xnT(c, k):
                act.wait_ge(xnT_ps.sem, xnT_ps.at(2 * c + k + 1))
                act.wait_ge(h_ps.sem, h_ps.at(2 * c))
                nc.scalar.activation(xnT[:, k, :], ps_f[:], ACT.Copy).then_inc(xnT_ready.sem, 1)

            def evacuate_h(c, m):
                act.wait_ge(h_ps.sem, h_ps.at(2 * c + m + 1))
                act.wait_ge(logits_ps.sem, logits_ps.at(c))
                nc.scalar.activation(hf[:, m, :], ps_f[:], ACT.Identity, bias=bias[:, m:m + 1]).then_inc(hf_ready.sem, 1)
                act.wait_ge(lo_ready.sem, lo_ready.at(2 * c))
                nc.scalar.activation(hs[:, m, :], ps_f[:], ACT.Identity, bias=bias_s[:, m:m + 1], scale=H_SCALE
                                     ).then_inc(hs_ready.sem, 1)

            def high_part(c, m):
                act.wait_ge(hs_ready.sem, hs_ready.at(2 * c + m + 1))
                act.wait_ge(hi_stored.sem, hi_stored.at(16 * c))
                nc.scalar.activation(hi[:, m, :], hs[:, m, :], ACT.Copy).then_inc(hi_ready.sem, 1)

            def exponentials(c):
                act.wait_ge(less_max.sem, less_max.at(c + 1))
                nc.scalar.activation(w[:], w[:], ACT.Exp).then_inc(exp_done.sem, 1)

            def evacuate_gates(c):
                act.wait_ge(gT_ps.sem, gT_ps.at(c + 1))
                act.wait_ge(gT_stored.sem, gT_stored.at(16 * c))
                nc.scalar.activation(gT[:], ps_f[:], ACT.Copy).then_inc(gT_ready.sem, 1)

            def store_gates(c):
                act.wait_ge(gT_ready.sem, gT_ready.at(c + 1))
                act.dma_start(gates_t[:, bass.ds(CH * c, CH)], gT[:]).then_inc(gT_stored.sem, 16)

            def gelu(c, i):
                act.wait_ge(u_ps.sem, u_ps.at(HIDDEN * c + i + 1))
                act.wait_ge(e_ps.sem, e_ps.at(GROUPS * c + i // 4 - 1))
                nc.scalar.activation(act_out[:, i % 8, :], ps_u[i % 4][:], ACT.Gelu,
                                     scale=1.0 / (H_SCALE * W_SCALE)).then_inc(gelu_done.sem, 1)

            def body(c, first, more):
                for n in range(GROUPS):
                    if first and n == 1:
                        evacuate_gates(0)
                        store_gates(0)
                    for i in range(4 * n, 4 * n + 4):
                        gelu(c, i)
                        if more and i == 4 * 28:
                            store_gates(c + 1)
                    if more:
                        if n in (2, 3):
                            evacuate_xnT(c + 1, n - 2)
                        if n in (7, 11):
                            evacuate_h(c + 1, n // 4 - 1)
                        if n in (8, 12):
                            high_part(c + 1, n // 4 - 2)
                        if n == 16:
                            exponentials(c + 1)
                        if n == 27:
                            evacuate_gates(c + 1)

            for k in range(2):
                evacuate_xnT(0, k)
            act.wait_ge(w_loaded.sem, W_LOADS)
            for rows, dst in ((slice(0, 2 * HD), w1), (slice(2 * HD, K1), w1h)):
                nc.scalar.activation(dst[rows], w1f[rows], ACT.Copy, scale=W_SCALE).then_inc(w1_high.sem, 1)
            for m in range(2):
                evacuate_h(0, m)
                high_part(0, m)
            exponentials(0)
            body(0, True, True)
            with act.Fori(1, CHUNKS - 1) as c:
                body(c, False, True)
            body(CHUNKS - 1, False, False)

        @block.tensor
        def _(pe):
            for c in (h_ps, logits_ps, gT_ps, e_ps, c_ps, y_ps):
                pe.sem_inc(c.sem, c.credit)

            def transpose_xn(c, k):
                pe.wait_ge(xn_ready.sem, xn_ready.at(4 * c + 4))
                if k == 0:
                    pe.wait_ge(gT_ready.sem, gT_ready.at(c))
                else:
                    pe.wait_ge(xnT_ready.sem, xnT_ready.at(2 * c + 1))
                for t in range(CT_):
                    ins = pe.transpose(ps_f[:, t * P:(t + 1) * P], xn[:, t, k * P:(k + 1) * P], ident[:])
                ins.then_inc(xnT_ps.sem, 1)

            def project_h(c, m, part):
                tok, k = divmod(part, 2)
                cols = slice(tok * CH // 2, (tok + 1) * CH // 2)
                if part == 0:
                    pe.wait_ge(xnT_ready.sem, xnT_ready.at(2 * c + 2))
                    if m == 1:
                        pe.wait_ge(hs_ready.sem, hs_ready.at(2 * c + 1))
                ins = pe.matmul(ps_f[:, cols], wm[:, k, m * P:(m + 1) * P], xnT[:, k, cols], start=(k == 0), stop=(k == 1),
                                skip_group_check=True)
                if part == 3:
                    ins.then_inc(h_ps.sem, 1)

            def logits(c, tiles):
                pe.wait_ge(hf_ready.sem, hf_ready.at(2 * c + 2))
                pe.wait_ge(hs_ready.sem, hs_ready.at(2 * c + 2))
                for t in tiles:
                    for m in range(2):
                        ins = pe.matmul(ps_f[:, t * P + m * 64:t * P + (m + 1) * 64], hf[:, m, t * P:(t + 1) * P],
                                        emb[:], start=True, stop=True, skip_group_check=True)
                if CT_ - 1 in tiles:
                    ins.then_inc(logits_ps.sem, 1)

            def transpose_gates(c):
                pe.wait_ge(top_step.sem, top_step.at(TOP * c + TOP))
                pe.wait_ge(less_max.sem, less_max.at(c + 1))
                for t in range(CT_):
                    ins = pe.transpose(ps_f[:, t * P:(t + 1) * P], gates[:, t, :], ident[:])
                ins.then_inc(gT_ps.sem, 1)

            def up(c, i):
                h, e = divmod(i, E)
                if e == 0:
                    pe.wait_ge(hx_loaded[h].sem, 48 * (c + 1))
                pe.wait_ge(gelu_done.sem, gelu_done.at(HIDDEN * c + i - 3))
                pe.matmul(ps_u[i % 4][:], w1[:, e, :], hx[:, h, :], start=True, stop=True).then_inc(u_ps.sem, 1)

            def down(c, n):
                g = n % G4
                pe.wait_ge(gelu_done.sem, gelu_done.at(HIDDEN * c + 4 * n + 4))
                pe.wait_ge(pr_ready.sem, pr_ready.at(GROUPS * c + n - 1))
                for j in range(4):
                    ins = pe.matmul(ps_e[n % 2][HD * j:HD * (j + 1), :], w2[:, 4 * g + j, :],
                                    act_out[:, (4 * n + j) % 8, :], start=True, stop=True, skip_group_check=True)
                ins.then_inc(e_ps.sem, 1)

            def combine(c, q):
                pe.wait_ge(sum_ready.sem, sum_ready.at(8 * c + 4 * q + 4))
                pe.wait_ge(comb_ready.sem, comb_ready.at(2 * c + q))
                pe.wait_ge(y_part.sem, y_part.at(2 * c))
                for j in range(4):
                    ins = pe.matmul(ps_y[HD * j:HD * (j + 1), :], fold[:], sums[:, 4 * q + j, :],
                                    start=True, stop=True, skip_group_check=True)
                ins.then_inc(c_ps.sem, 1)

            def project_out(c, n, t, k):
                pe.wait_ge(comb_ready.sem, comb_ready.at(2 * c + 2))
                pe.wait_ge(y_part.sem, y_part.at(2 * c + n))
                ins = pe.matmul(ps_y[:, t * D:(t + 1) * D], comb[:, k, (2 * n + t) * P:(2 * n + t + 1) * P],
                                wo[:, k, :], start=(k == 0), stop=(k == 1), skip_group_check=True)
                if t == 1 and k == 1:
                    ins.then_inc(y_ps.sem, 1)

            def body(c, before, more):
                for n in range(GROUPS):
                    for i in range(4 * n, 4 * n + 4):
                        up(c, i)
                    if n >= 1:
                        down(c, n - 1)
                    elif before:
                        down(c - 1, GROUPS - 1)
                    if not before and n == 0:
                        transpose_gates(0)
                    if more:
                        if n in (2, 3):
                            transpose_xn(c + 1, n - 2)
                        if 4 <= n < 12:
                            project_h(c + 1, n // 4 - 1, n % 4)
                        if n in (13, 14):
                            logits(c + 1, (2 * n - 26, 2 * n - 25))
                        if n == 27:
                            transpose_gates(c + 1)
                    if before and n == 12:
                        combine(c - 1, 1)
                    if before:
                        for piece, out_step in enumerate(OUT_STEPS):
                            if n == out_step:
                                project_out(c - 1, piece // 4, piece // 2 % 2, piece % 2)
                    if n == 26:
                        combine(c, 0)

            pe.wait_ge(loaded.sem, LOADS)
            for k in range(2):
                transpose_xn(0, k)
            for m in range(2):
                for part in range(4):
                    project_h(0, m, part)
            logits(0, range(CT_))
            pe.wait_ge(w_loaded.sem, W_LOADS)
            pe.wait_ge(ones_ready.sem, 1)
            pe.wait_ge(b1_placed.sem, 16)
            pe.wait_ge(w1_high.sem, 2)
            pe.wait_ge(w1_low.sem, 1)
            body(0, False, True)
            with pe.Fori(1, CHUNKS - 1) as c:
                body(c, True, True)
            body(CHUNKS - 1, True, False)
            down(CHUNKS - 1, GROUPS - 1)
            combine(CHUNKS - 1, 1)
            for n in range(2):
                for t in range(2):
                    for k in range(2):
                        project_out(CHUNKS - 1, n, t, k)


def constants():
    p = np.arange(P)
    theta = np.float32(1.0) / np.float32(10000.0) ** (np.arange(0, DH1, 2, dtype=np.float32) / np.float32(DH1))
    angle = np.outer(np.arange(S, dtype=np.float32), theta.astype(np.float32)).astype(np.float32)
    angle = np.concatenate([angle, angle], axis=1)[:, p % DH1].T
    sign = np.where(p % DH1 < DH1 // 2, -1.0, 1.0).astype(np.float32)[:, None]
    table = np.concatenate([np.cos(angle), sign * np.sin(angle)], axis=1).astype(np.float32)
    return {
        "ident_in": np.eye(P, dtype=np.float32),
        "rope": (table * np.float32(Q_SCALE * PROJECTED)).astype(np.float32),
        "rank": np.broadcast_to(np.arange(E, 0, -1, dtype=np.float32), (P, E)).copy(),
        "fold_in": np.tile(np.eye(HD, dtype=np.float32), (P // HD, 1)),
    }


def decoder(nc, x, ctx_1024, w_qkv, w_out, b_out, media_w, media_b, lat_w, lat_b, Wq, Wk, Wv, Wout,
            Wm, bm, expert_emb, W1, b1, W2, b2, Wo, bo, ident_in, rope, rank, fold_in, out):
    qk_parts = nc.dram_tensor("qk_parts", [4, P, 2, S], F16).ap()
    b1_parts = nc.dram_tensor("b1_parts", [3, E, I], F16).ap()
    h_parts = nc.dram_tensor("h_parts", [2, D, B * S], F16).ap()
    gates_t = nc.dram_tensor("gates_t", [HF * E, B * S], F32).ap()
    with ExitStack() as ctx:
        X, ident, x_raw = (ctx.enter_context(nc.sbuf_tensor(name, shape, F32)) for name, shape in
                           (("X", [P, TILES, D]), ("ident", [P, P]), ("x_raw", [P, TILES, 6])))
        with nc.sbuf_tensor("C", [P, TILES, D], F32) as C, nc.sbuf_tensor("c_raw", [P, TILES, 6], F32) as c_raw:
            self_attention(nc, X, C, ident, x_raw, c_raw, qk_parts, x, ctx_1024, ident_in, w_qkv, w_out, b_out, rope)
            cross_attention(nc, X, C, ident, x_raw, c_raw, media_w, media_b, lat_w, lat_b, Wq, Wk, Wv, Wout)
        ffn(nc, X, ident, x_raw, b1_parts, h_parts, gates_t, Wm, bm, expert_emb, rank, W1, b1, W2, b2, Wo, bo, fold_in, out)


_INS = ["x", "ctx_1024", "L0_attn_w_qkv", "L0_attn_w_out", "L0_attn_b_out",
        "L0_xattn_ln_media_w", "L0_xattn_ln_media_b", "L0_xattn_ln_lat_w", "L0_xattn_ln_lat_b",
        "L0_xattn_Wq", "L0_xattn_Wk", "L0_xattn_Wv", "L0_xattn_Wout",
        "L0_ffn_Wm", "L0_ffn_bm", "L0_ffn_expert_emb", "L0_ffn_W1", "L0_ffn_b1", "L0_ffn_W2", "L0_ffn_b2",
        "L0_ffn_Wo", "L0_ffn_bo"]


def kernel(**inputs):
    import concourse.bacc as bacc
    from concourse.bass_utils import run_bass_kernel_spmd

    nc = bacc.Bacc("TRN2", target_bir_lowering=False, num_devices=1)
    arrays, args = {}, []
    for name, a in [(n, inputs[n]) for n in _INS] + list(constants().items()):
        a = np.ascontiguousarray(a)
        arrays[f"in_{name}_dram"] = a
        args.append(nc.dram_tensor(f"in_{name}_dram", a.shape, mybir.dt.from_np(a.dtype), kind="ExternalInput").ap())
    args.append(nc.dram_tensor("out_0_dram", (B, S, D), F32, kind="ExternalOutput").ap())
    decoder(nc, *args)
    r = run_bass_kernel_spmd(nc, [arrays], core_ids=[0])
    return r.results[0]["out_0_dram"]
```
